# Optimizing a Trainium2 kernel written in Bass

```python
import numpy as np
import jax
import jax.numpy as jnp

def _softmax(x, axis=-1):
    return jax.nn.softmax(x, axis=axis)

def _gelu(x):
    return jax.nn.gelu(x, approximate=True)

def _silu(x):
    return jax.nn.silu(x)

def _sigmoid(x):
    return jax.nn.sigmoid(x)

def _layernorm(x, axis=-1, eps=1e-05):
    m = jnp.mean(x, axis=axis, keepdims=True)
    v = jnp.var(x, axis=axis, keepdims=True)
    return (x - m) / jnp.sqrt(v + eps)

def _scatter_add(tgt, idx, src, axis=0):
    return tgt.at[idx].add(src)

def _segment_sum(src, seg, n):
    return jax.ops.segment_sum(src, seg, n)
kernel_name = 'mk_audio_tower_d2_tok_audfeat256_r4_90d58b'

def setup_inputs(seed: int=0):
    np.random.seed(seed)
    _w = jnp.asarray

    def _rec_inputs():
        import jax
        import jax.numpy as jnp
        _rk = jax.random.key(seed)
        x = 7.22013e-05 + 1.00017 * jax.random.normal(jax.random.fold_in(_rk, 1), (64, 375, 64), jnp.float32)
        return x
    x = _rec_inputs()

    def _L0_tok_setup():
        import jax, jax.numpy as jnp
        import numpy as np
        B, T, D = (8, 1024, 64)
        N_RECUR = 2
        TW = 15
        STRIDE = 2
        key = jax.random.key(seed)
        ks = jax.random.split(key, 8)
        glorot = (2.0 / (D + D)) ** 0.5
        X = jax.random.normal(ks[0], (B, T, D), dtype=jnp.float32)
        W_in = jax.random.normal(ks[1], (N_RECUR, D, D), dtype=jnp.float32) * glorot
        b_in = jax.random.normal(ks[2], (N_RECUR, D), dtype=jnp.float32) * 0.05
        W_out = jax.random.normal(ks[3], (N_RECUR, D, D), dtype=jnp.float32) * glorot
        b_out = jax.random.normal(ks[4], (N_RECUR, D), dtype=jnp.float32) * 0.05
        core_diag = jnp.ones((D,), dtype=jnp.float32)
        conv_filter = jax.random.normal(ks[5], (TW,), dtype=jnp.float32) * (2.0 / (TW + 1)) ** 0.5
        return {'X': X, 'W_in': W_in, 'b_in': b_in, 'W_out': W_out, 'b_out': b_out, 'core_diag': core_diag, 'conv_filter': conv_filter, 'stride': STRIDE}
    _L0_tok_all = _L0_tok_setup()
    _L0_tok_in = {k: v for k, v in _L0_tok_all.items() if k in ('W_in', 'b_in', 'W_out', 'b_out', 'core_diag', 'conv_filter')}
    del _L0_tok_all

    def _L0_attn_setup():
        import jax, jax.numpy as jnp
        import numpy as np
        EPS = 1e-06

        def _rmsnorm(x, w):
            xf = x.astype(jnp.float32)
            y = xf * jax.lax.rsqrt(jnp.mean(xf * xf, axis=-1, keepdims=True) + EPS)
            return y.astype(x.dtype) * w
        key = jax.random.key(seed)
        k0, k1, k2 = jax.random.split(key, 3)
        B, T, C = (2, 256, 64)
        x = jax.random.normal(k0, (B, T, C), jnp.float32)
        w_qkv = jax.random.normal(k1, (3 * C, C), jnp.float32) / np.float32(np.sqrt(C))
        w_proj = jax.random.normal(k2, (C, C), jnp.float32) / np.float32(np.sqrt(C))
        qn_w = jnp.ones((2,), jnp.float32)
        kn_w = jnp.ones((2,), jnp.float32)
        return {'x': x, 'w_qkv': w_qkv, 'w_proj': w_proj, 'qn_w': qn_w, 'kn_w': kn_w}
    _L0_attn_all = _L0_attn_setup()
    _L0_attn_in = {k: v for k, v in _L0_attn_all.items() if k in ('w_qkv', 'w_proj', 'qn_w', 'kn_w')}
    del _L0_attn_all

    def _L0_ffn_setup():
        import jax, jax.numpy as jnp
        import numpy as np
        B, S, H, F, E, K = (8, 1024, 64, 128, 16, 2)
        EPS = 1e-05
        key = jax.random.key(seed)
        ks = jax.random.split(key, 9)
        sc = 0.02
        return {'x': jax.random.normal(ks[0], (B, S, H), dtype=jnp.float32), 'gate_w': jax.random.normal(ks[1], (H, E), dtype=jnp.float32) * sc, 'gate_b': jnp.zeros((E,), dtype=jnp.float32), 'w1': jax.random.normal(ks[2], (E, H, F), dtype=jnp.float32) * sc, 'b1': jnp.zeros((E, F), dtype=jnp.float32), 'w2': jax.random.normal(ks[3], (E, F, H), dtype=jnp.float32) * sc, 'b2': jnp.zeros((E, H), dtype=jnp.float32), 'gamma': jnp.ones((H,), dtype=jnp.float32), 'beta': jnp.zeros((H,), dtype=jnp.float32)}
    _L0_ffn_all = _L0_ffn_setup()
    _L0_ffn_in = {k: v for k, v in _L0_ffn_all.items() if k in ('gate_w', 'gate_b', 'w1', 'b1', 'w2', 'b2', 'gamma', 'beta')}
    del _L0_ffn_all

    def _L1_attn_setup():
        import jax, jax.numpy as jnp
        import numpy as np
        NUM_HEADS = 8
        K_RATIO = 0.3
        LN_EPS = 1e-05

        def _layernorm(t, gamma, beta):
            mu = t.mean(axis=-1, keepdims=True)
            var = ((t - mu) ** 2).mean(axis=-1, keepdims=True)
            return (t - mu) * jax.lax.rsqrt(var + LN_EPS) * gamma + beta
        key = jax.random.key(seed)
        ks = jax.random.split(key, 5)
        B, N, C = (1024, 64, 64)
        hd = C // NUM_HEADS
        s = 0.02
        return {'x': jax.random.normal(ks[0], (B, N, C), jnp.float32), 'qkv_w': jax.random.normal(ks[1], (3 * C, C), jnp.float32) * s, 'qkv_b': jnp.zeros((3 * C,), jnp.float32), 'q_gamma': jnp.ones((hd,), jnp.float32), 'q_beta': jnp.zeros((hd,), jnp.float32), 'k_gamma': jnp.ones((hd,), jnp.float32), 'k_beta': jnp.zeros((hd,), jnp.float32), 'proj_w': jax.random.normal(ks[2], (C, C), jnp.float32) * s, 'proj_b': jnp.zeros((C,), jnp.float32)}
    _L1_attn_all = _L1_attn_setup()
    _L1_attn_in = {k: v for k, v in _L1_attn_all.items() if k in ('qkv_w', 'qkv_b', 'q_gamma', 'q_beta', 'k_gamma', 'k_beta', 'proj_w', 'proj_b')}
    del _L1_attn_all

    def _L1_ffn_setup():
        import jax, jax.numpy as jnp
        import numpy as np
        B, S, D = (8, 1024, 64)
        H = 4 * D
        CAPACITY = 0.5
        key = jax.random.key(seed)
        ks = jax.random.split(key, 6)
        x = jax.random.normal(ks[0], (B, S, D), dtype=jnp.float32)
        attention_mask = jnp.zeros((B, 1, 1, S), dtype=jnp.float32)
        wr = jax.random.normal(ks[1], (D, 1), dtype=jnp.float32) * 0.02
        br = jnp.zeros((1,), dtype=jnp.float32)
        w1 = jax.random.normal(ks[2], (D, H), dtype=jnp.float32) * 0.02
        b1 = jnp.zeros((H,), dtype=jnp.float32)
        w2 = jax.random.normal(ks[3], (H, D), dtype=jnp.float32) * 0.02
        b2 = jnp.zeros((D,), dtype=jnp.float32)
        return {'x': x, 'attention_mask': attention_mask, 'wr': wr, 'br': br, 'w1': w1, 'b1': b1, 'w2': w2, 'b2': b2}
    _L1_ffn_all = _L1_ffn_setup()
    _L1_ffn_in = {k: v for k, v in _L1_ffn_all.items() if k in ('attention_mask', 'wr', 'br', 'w1', 'b1', 'w2', 'b2')}
    del _L1_ffn_all
    return {'x': x, 'L0_tok_W_in': _L0_tok_in['W_in'], 'L0_tok_b_in': _L0_tok_in['b_in'], 'L0_tok_W_out': _L0_tok_in['W_out'], 'L0_tok_b_out': _L0_tok_in['b_out'], 'L0_tok_core_diag': _L0_tok_in['core_diag'], 'L0_tok_conv_filter': _L0_tok_in['conv_filter'], 'L0_attn_w_qkv': _L0_attn_in['w_qkv'], 'L0_attn_w_proj': _L0_attn_in['w_proj'], 'L0_attn_qn_w': _L0_attn_in['qn_w'], 'L0_attn_kn_w': _L0_attn_in['kn_w'], 'L0_ffn_gate_w': _L0_ffn_in['gate_w'], 'L0_ffn_gate_b': _L0_ffn_in['gate_b'], 'L0_ffn_w1': _L0_ffn_in['w1'], 'L0_ffn_b1': _L0_ffn_in['b1'], 'L0_ffn_w2': _L0_ffn_in['w2'], 'L0_ffn_b2': _L0_ffn_in['b2'], 'L0_ffn_gamma': _L0_ffn_in['gamma'], 'L0_ffn_beta': _L0_ffn_in['beta'], 'L1_attn_qkv_w': _L1_attn_in['qkv_w'], 'L1_attn_qkv_b': _L1_attn_in['qkv_b'], 'L1_attn_q_gamma': _L1_attn_in['q_gamma'], 'L1_attn_q_beta': _L1_attn_in['q_beta'], 'L1_attn_k_gamma': _L1_attn_in['k_gamma'], 'L1_attn_k_beta': _L1_attn_in['k_beta'], 'L1_attn_proj_w': _L1_attn_in['proj_w'], 'L1_attn_proj_b': _L1_attn_in['proj_b'], 'L1_ffn_attention_mask': _L1_ffn_in['attention_mask'], 'L1_ffn_wr': _L1_ffn_in['wr'], 'L1_ffn_br': _L1_ffn_in['br'], 'L1_ffn_w1': _L1_ffn_in['w1'], 'L1_ffn_b1': _L1_ffn_in['b1'], 'L1_ffn_w2': _L1_ffn_in['w2'], 'L1_ffn_b2': _L1_ffn_in['b2']}

def reference(x, L0_tok_W_in, L0_tok_b_in, L0_tok_W_out, L0_tok_b_out, L0_tok_core_diag, L0_tok_conv_filter, L0_attn_w_qkv, L0_attn_w_proj, L0_attn_qn_w, L0_attn_kn_w, L0_ffn_gate_w, L0_ffn_gate_b, L0_ffn_w1, L0_ffn_b1, L0_ffn_w2, L0_ffn_b2, L0_ffn_gamma, L0_ffn_beta, L1_attn_qkv_w, L1_attn_qkv_b, L1_attn_q_gamma, L1_attn_q_beta, L1_attn_k_gamma, L1_attn_k_beta, L1_attn_proj_w, L1_attn_proj_b, L1_ffn_attention_mask, L1_ffn_wr, L1_ffn_br, L1_ffn_w1, L1_ffn_b1, L1_ffn_w2, L1_ffn_b2):
    import jax
    import jax.numpy as jnp

    def _L0_tok_ref(X, W_in, b_in, W_out, b_out, core_diag, conv_filter, stride):
        import jax, jax.numpy as jnp
        import numpy as np
        B, T, D = (8, 1024, 64)
        N_RECUR = 2
        TW = 15
        STRIDE = 2
        out = X
        for i in range(W_in.shape[0]):
            out = jnp.tanh(out @ W_in[i] + b_in[i])
        out = jnp.abs(core_diag)[None, None, :] * out * out
        n = W_out.shape[0]
        for i in range(n):
            out = jnp.tanh(out @ W_out[n - 1 - i] + b_out[n - 1 - i])
        tw = conv_filter.shape[0]
        pad = tw // 2
        out = jnp.pad(out, ((0, 0), (pad, pad), (0, 0)))
        d = out.shape[-1]
        kernel = jnp.broadcast_to(conv_filter[:, None, None], (tw, 1, d))
        out_pool = jax.lax.conv_general_dilated(out, kernel, window_strides=(stride,), padding='VALID', dimension_numbers=('NWC', 'WIO', 'NWC'), feature_group_count=d)
        return out_pool

    def _L0_attn_ref(x, w_qkv, w_proj, qn_w, kn_w):
        import jax, jax.numpy as jnp
        import numpy as np
        EPS = 1e-06

        def _rmsnorm(x, w):
            xf = x.astype(jnp.float32)
            y = xf * jax.lax.rsqrt(jnp.mean(xf * xf, axis=-1, keepdims=True) + EPS)
            return y.astype(x.dtype) * w
        B, T, C = x.shape
        HD = 2
        H = C // HD
        qkv = x @ w_qkv.T
        q, k, v = jnp.split(qkv, 3, axis=-1)
        heads = lambda t: t.reshape(B, T, H, HD).transpose(0, 2, 1, 3)
        q = _rmsnorm(heads(q), qn_w)
        k = _rmsnorm(heads(k), kn_w)
        v = heads(v)
        scale = np.float32(1.0 / np.sqrt(HD))
        att = jnp.einsum('bhtd,bhsd->bhts', q, k) * scale
        causal = jnp.tril(jnp.ones((T, T), bool))
        att = jnp.where(causal, att, jnp.float32(-1e+30))
        att = jax.nn.softmax(att, axis=-1)
        y = jnp.einsum('bhts,bhsd->bhtd', att, v)
        y = y.transpose(0, 2, 1, 3).reshape(B, T, C)
        return y @ w_proj.T

    def _L0_ffn_ref(x, gate_w, gate_b, w1, b1, w2, b2, gamma, beta):
        import jax, jax.numpy as jnp
        import numpy as np
        B, S, H, F, E, K = (8, 1024, 64, 128, 16, 2)
        EPS = 1e-05
        gate_logits = x @ gate_w + gate_b
        topk_vals, topk_idx = jax.lax.top_k(gate_logits, K)
        topk_w = jax.nn.softmax(topk_vals, axis=-1)
        h = jax.nn.relu(jnp.einsum('bsh,ehf->bsef', x, w1) + b1)
        expert_out = jnp.einsum('bsef,efh->bseh', h, w2) + b2
        sel = jnp.take_along_axis(expert_out, topk_idx[:, :, :, None], axis=2)
        moe = jnp.sum(topk_w[..., None] * sel, axis=2)
        y = x + moe
        mu = jnp.mean(y, axis=-1, keepdims=True)
        var = jnp.var(y, axis=-1, keepdims=True)
        return (y - mu) / jnp.sqrt(var + EPS) * gamma + beta

    def _L1_attn_ref(x, qkv_w, qkv_b, q_gamma, q_beta, k_gamma, k_beta, proj_w, proj_b):
        import jax, jax.numpy as jnp
        import numpy as np
        NUM_HEADS = 8
        K_RATIO = 0.3
        LN_EPS = 1e-05

        def _layernorm(t, gamma, beta):
            mu = t.mean(axis=-1, keepdims=True)
            var = ((t - mu) ** 2).mean(axis=-1, keepdims=True)
            return (t - mu) * jax.lax.rsqrt(var + LN_EPS) * gamma + beta
        B, N, C = x.shape
        H = NUM_HEADS
        hd = C // H
        scale = hd ** (-0.5)
        k_val = int(N * K_RATIO)
        qkv = (x @ qkv_w.T + qkv_b).reshape(B, N, 3, H, hd)
        qkv = jnp.transpose(qkv, (2, 0, 3, 1, 4))
        q, k, v = (qkv[0], qkv[1], qkv[2])
        q = _layernorm(q, q_gamma, q_beta)
        k = _layernorm(k, k_gamma, k_beta)
        attn = jnp.einsum('bhnd,bhmd->bhnm', q, k) * scale
        _, top_idx = jax.lax.top_k(attn, k_val)
        mask = jnp.full(attn.shape, -jnp.inf, attn.dtype)
        bi = jnp.arange(B)[:, None, None, None]
        hi = jnp.arange(H)[None, :, None, None]
        ni = jnp.arange(N)[None, None, :, None]
        mask = mask.at[bi, hi, ni, top_idx].set(0.0)
        attn = jax.nn.softmax(attn + mask, axis=-1)
        out = jnp.einsum('bhnm,bhmd->bhnd', attn, v)
        out = jnp.transpose(out, (0, 2, 1, 3)).reshape(B, N, C)
        return out @ proj_w.T + proj_b

    def _L1_ffn_ref(x, attention_mask, wr, br, w1, b1, w2, b2):
        import jax, jax.numpy as jnp
        import numpy as np
        B, S, D = (8, 1024, 64)
        H = 4 * D
        CAPACITY = 0.5
        b, s, d = x.shape
        weights = (jnp.einsum('bsd,do->bso', x, wr) + br)[..., 0]
        k = max(1, int(CAPACITY * s))
        kk = k - 1 if k > 1 else 1
        _, idx = jax.lax.top_k(weights, k)
        sel_idx = idx[:, :kk]
        sel = jnp.take_along_axis(x, sel_idx[:, :, None], axis=1)
        h = jax.nn.gelu(jnp.einsum('bkd,dh->bkh', sel, w1) + b1)
        y = jnp.einsum('bkh,hd->bkd', h, w2) + b2
        w_sel = jnp.take_along_axis(weights, sel_idx, axis=1)
        y = y * w_sel[..., None]
        batch_idx = jnp.arange(b)[:, None]
        processed = jnp.zeros_like(x).at[batch_idx, sel_idx].set(y)
        return processed + x
    h = _L0_tok_ref(x, L0_tok_W_in, L0_tok_b_in, L0_tok_W_out, L0_tok_b_out, L0_tok_core_diag, L0_tok_conv_filter, 2)
    h = h + _L0_attn_ref(_layernorm(h, axis=-1), L0_attn_w_qkv, L0_attn_w_proj, L0_attn_qn_w, L0_attn_kn_w)
    h = h + _L0_ffn_ref(_layernorm(h, axis=-1), L0_ffn_gate_w, L0_ffn_gate_b, L0_ffn_w1, L0_ffn_b1, L0_ffn_w2, L0_ffn_b2, L0_ffn_gamma, L0_ffn_beta)
    h = h + _L1_attn_ref(_layernorm(h, axis=-1), L1_attn_qkv_w, L1_attn_qkv_b, L1_attn_q_gamma, L1_attn_q_beta, L1_attn_k_gamma, L1_attn_k_beta, L1_attn_proj_w, L1_attn_proj_b)
    h = h + _L1_ffn_ref(_layernorm(h, axis=-1), L1_ffn_attention_mask, L1_ffn_wr, L1_ffn_br, L1_ffn_w1, L1_ffn_b1, L1_ffn_w2, L1_ffn_b2)
    return h

_drawn_inputs = setup_inputs


def setup_inputs(seed=0):
    import zlib

    import numpy as np

    out = dict(_drawn_inputs(seed))
    spreads = {'L0_tok_core_diag': (1.0, 0.2),
     'L0_attn_qn_w': (1.0, 0.6),
     'L0_attn_kn_w': (1.0, 0.6),
     'L0_ffn_gate_b': (0.0, 0.1),
     'L0_ffn_b1': (0.0, 0.8),
     'L0_ffn_b2': (0.0, 0.1),
     'L0_ffn_gamma': (1.0, 0.2),
     'L0_ffn_beta': (0.0, 0.1),
     'L1_attn_qkv_b': (0.0, 0.8),
     'L1_attn_q_gamma': (1.0, 0.6),
     'L1_attn_q_beta': (0.0, 0.8),
     'L1_attn_k_gamma': (1.0, 0.6),
     'L1_attn_k_beta': (0.0, 0.8),
     'L1_attn_proj_b': (0.0, 0.1),
     'L1_ffn_b1': (0.0, 0.8),
     'L1_ffn_b2': (0.0, 0.8)}
    factors = {'L0_ffn_w1': 6.251,
     'L0_ffn_w2': 4.295,
     'L1_attn_qkv_w': 5.536,
     'L1_attn_proj_w': 3.522,
     'L1_ffn_wr': 7.721,
     'L1_ffn_w1': 8.0,
     'L1_ffn_w2': 8.0}
    for name, (base, spread) in spreads.items():
        noise = np.random.default_rng([zlib.crc32(name.encode()), seed]).standard_normal(out[name].shape)
        drawn = base * np.exp(spread * noise) if base else spread * noise
        out[name] = jnp.asarray(drawn.astype(out[name].dtype))
    for name, factor in factors.items():
        out[name] = (out[name] * factor).astype(out[name].dtype)
    return out
```

```python
from contextlib import ExitStack

import concourse.bass as bass
from concourse import mybir

F32 = mybir.dt.float32
BF16 = mybir.dt.bfloat16
I32 = mybir.dt.int32
U32 = mybir.dt.uint32
ALU = mybir.AluOpType
ACT = mybir.ActivationFunctionType
AX_X = mybir.AxisListType.X

P = 128
PAIRS = 32
T_IN, D = 375, 64
XT = T_IN // 3
TAPS, PAD = 15, 7
T = 188
TP = T // 2
S1 = T - P
UNIT = T + S1
H0, HD0 = 32, 2
H1, HD1 = 8, 8
TERMS = 6
ROWS0 = TERMS * HD0 + 3
E, TOPK_E, F_E = 16, 2, 128
KEEP = int(T * 0.3)
ROUNDS = KEEP // 8
CAP = T // 2 - 1
NEG = -3.0e38
NEG_TEST = -1.0e38
MASKED = -1.0e30
RSQRT_MAGIC = 1597463007.0
SHIFT_ROOM = 80.0
CHUNKS = 8


class Steps:

    def __init__(self, sem, names):
        self.sem, self.names, self.next = sem, names, 0
        self.index = {n: k for k, n in enumerate(names)}
        assert len(self.index) == len(names)

    def step(self, name):
        assert self.names[self.next % len(self.names)] == name, (name, self.names[self.next % len(self.names)])
        self.next += 1
        return self.sem, 1

    def of(self, name, i):
        return self.sem, i * len(self.names) + (self.index[name] + 1)


def newton(x):
    return [f"{x}_guess"] + [f"{x}_n{r}{c}" for r in range(3) for c in "abc"]


def ln_steps(x):
    return [f"{x}_sum", f"{x}_mean", f"{x}_cen", f"{x}_sq", f"{x}_ssq", f"{x}_var"] + newton(x)


PE_FRONT = (["xT", "tok0", "tok1", "tok2", "tok3", "conv", "hn0T", "qk0", "v0"]
            + [f"zT{f}" for f in range(8)]
            + [x for n in range(17) for x in ([f"sc{n}"] if n < 16 else []) + ([f"pv{n - 1}"] if n else [])]
            + ["y0T", "yn0T", "proj0"]
            + ["hn1T", "gate", "gT"]
            + [x for e in range(E + 1) for x in ([f"z{e}"] if e < E else []) + ([f"o{e - 1}"] if e else [])]
            + ["moeT", "hn2T", "qk1"] + [f"kqT{f}" for f in range(5)])
ACT_FRONT = (["x0", "x1", "x2", "x2s", "x3", "x4", "h0", "hn0Tc", "qk0c", "qk0s", "v0c"]
             + [f"zTc{f}" for f in range(8)] + [f"ex{n}" for n in range(16)] + ["y0c", "yn0Tc"]
             + ["hn1Tc", "gexp", "gTc"] + [x for e in range(E) for x in (f"relu{e}", f"gc{e}")]
             + ["moec", "hn2Tc", "qk1c"] + [f"kqTc{f}" for f in range(5)])
DVE_FRONT = (ln_steps("a") + ["hn0", "b_guess", "q1", "k1", "c1", "q2", "k2", "c2", "q3", "k3", "c3"]
             + ["rec0", "yn0", "h1"] + ln_steps("c") + ["hn1"]
             + ["lg"] + [f"gm{t}" for t in range(4)] + [f"gi{t}" for t in range(4)]
             + ["gif", "gd", "g1p", "p1", "p2", "e1", "e2", "e1p", "e2p", "G", "G1", "Gr", "G2", "Gr2", "G3"]
             + ["ma", "mb"] + ln_steps("d") + ["dn", "dg", "db", "h2"] + ln_steps("f") + ["hn2"]
             + ["g_sum", "g_mean", "g_cen", "g_ssq", "g_var"] + newton("g"))
POOL_FRONT = (["ss", "sx"] + [f"rn{r}{c}" for r in range(3) for c in "abcd"]
              + ["qr", "qw", "qkp", "self", "negc", "rq1", "rk1", "rc1", "rq2", "rk2", "rc2"]
              + [f"hp{e}" for e in range(E)] + ["g_sq", "g_norm", "g_gam", "gq0", "gq1", "gk0", "gk1"])
PE_SCORE = [f"s{k}" for k in range(CHUNKS)] + ["v1"]
ACT_SCORE = [f"sc{k}{x}" for k in range(CHUNKS) for x in "ab"] + [f"e{k}" for k in range(CHUNKS)] + ["v1c"]
DVE_SCORE = [f"m{k}{x}" for k in range(CHUNKS) for x in ("t0", "t1", "t2", "n")]
DVE_TOPK = [f"k{k}r{r}{c}{t}" for k in range(CHUNKS)
            for r, c in [(0, "r")] + [(r, c) for r in range(1, ROUNDS) for c in "mr"] + [(ROUNDS, "p")]
            for t in range(3)]
PE_BACK = ([f"{x}{k}" for k in range(CHUNKS) for x in ("pt0_", "pt1_", "pv")]
           + ["y1T", "yn1T", "proj1", "h3T", "route", "ffz0", "ffz1", "ffo", "ffT"])
ACT_BACK = ([f"{x}{k}" for k in range(CHUNKS) for x in ("pc0_", "pc1_")]
            + ["y1c", "yn1Tc", "h3Tc", "routec", "gelu0", "gelu1", "ffoc", "ffTc"])
DVE_BACK = ["rec1", "yn1", "h3"] + ln_steps("r") + ["hn3", "hsum"]
POOL_KEEP = ["h2k"]


def audio_tower(nc, dram, out, route_dram, h_dram, y_dram):
    with ExitStack() as ctx:
        def sb(name, shape, dt=F32):
            return ctx.enter_context(nc.sbuf_tensor(name, shape, dt))

        def ps(name, shape, dt=F32):
            return ctx.enter_context(nc.psum_tensor(name, shape, dt))

        def sem(name):
            return ctx.enter_context(nc.semaphore(name))

        ident = sb("ident", [P, P])
        ident_b = sb("ident_b", [P, P], BF16)
        ones = sb("ones", [1, P])
        tok_w = sb("tok_w", [P, 4, P])
        tok_b = sb("tok_b", [P, 3])
        core = sb("core", [P, 1])
        core_abs = sb("core_abs", [P, 1])
        tok_brow = sb("tok_brow", [1, 2, D])
        taps = sb("taps", [XT, TAPS])
        toeplitz = sb("toeplitz", [XT, 3, T])
        w_qkv0 = sb("w_qkv0", [P, 3, 2, D])
        w_qkv1 = sb("w_qkv1", [P, 3, 2, D])
        w_proj = sb("w_proj", [P, 2, 2, D])
        rms_raw = sb("rms_raw", [TP, 2, 2])
        rms_w = sb("rms_w", [TP, 2, P])
        wprod = sb("wprod", [TP, 2])
        room = sb("room", [TP, 1])
        causal = sb("causal", [P, 2, UNIT], BF16)
        gate_w = sb("gate_w", [D, E])
        gate_b = sb("gate_b", [1, E])
        w1e = sb("w1e", [D, E, F_E])
        w2e = sb("w2e", [F_E, E, D])
        b1e = sb("b1e", [F_E, E])
        b2raw = sb("b2raw", [3 * E, D])
        b2res = sb("b2res", [3 * E, 2, D])
        b2e = sb("b2e", [3 * E, 3, D], BF16)
        pick = sb("pick", [3 * E, E, P], BF16)
        expert_id = sb("expert_id", [TP, 4, E])
        ln_gb = sb("ln_gb", [TP, 2, D])
        brow1 = sb("brow1", [1, 3, 2, D])
        gb_raw = sb("gb_raw", [TP, 4, HD1])
        gam1 = sb("gam1", [TP, 2, P])
        bet1 = sb("bet1", [TP, 2, P])
        projb1 = sb("projb1", [1, 2, D])
        wr = sb("wr", [D, 1])
        br = sb("br", [1, 1])
        fw1 = sb("fw1", [D, 2, P])
        fb1 = sb("fb1", [P, 2])
        fw2 = sb("fw2", [P, 2, D])
        fb2 = sb("fb2", [P, 1])

        x_in = sb("x_in", [XT, 3, 2, D])
        gh = sb("gh", [P, 2, 2 * T])
        x0, x1 = gh[:, 0, 0:T_IN], gh[:, 1, 0:T_IN]
        x2 = sb("x2", [P, T_IN])
        x2s, x3 = x0, x1
        x4 = sb("x4", [XT, 3, P])
        h0 = sb("h0", [TP, 4, D])
        h1 = sb("h1", [TP, 4, D])
        h2 = sb("h2", [TP, 4, D])
        h2k = sb("h2k", [TP, 4, D])
        h3 = sb("h3", [TP, 4, D])
        hn3 = sb("hn3", [TP, 4, D])
        hsum = sb("hsum", [TP, 4, D])
        cen = sb("cen", [TP, 4, D])
        sq = sb("sq", [TP, 4, D])
        lnt = sb("lnt", [TP, 6, 4])
        hn0 = sb("hn0", [TP, 4, D])
        hn1 = sb("hn1", [TP, 4, D])
        hn2 = sb("hn2", [TP, 4, D])
        hn0T = sb("hn0T", [P, T])
        hn1T = sb("hn1T", [D, 2 * T])
        hn2T = sb("hn2T", [P, T])
        qk0 = sb("qk0", [TP, 2, 2, P])
        qk0s = sb("qk0s", [TP, 2, 2, P])
        rx = sb("rx", [TP, 256])
        rr = sb("rr", [TP, 256])
        rt = sb("rt", [TP, 256])
        selfp = rt
        selfs = sb("selfs", [TP, P])
        negc = sb("negc", [TP, P])
        hrg = sb("hrg", [P, 2, 2, 2 * T])
        hr, hg = hrg[:, 0], hrg[:, 1]
        res = hrg[0:TP].rearrange("p a b c -> p (a b c)")[:, 0:1024].rearrange("p (r s c) -> p r s c", r=2, s=2)
        resc = sb("resc", [TP, 2, P])
        zq = sb("zq", [TP, P, 32], BF16)
        zk = sb("zk", [TP, P, 32], BF16)
        qT0 = sb("qT0", [P, 2, 8, T], BF16)
        kT0 = sb("kT0", [P, 2, 8, T], BF16)
        e0 = sb("e0", [P, 2, 4, UNIT])
        vp0 = [sb(f"vp0{m}", [P, 2, 1048]) for m in range(2)]
        y0 = sb("y0", [P, 2 * T])
        rec = sb("rec", [TP, 16, 8])
        yn = sb("yn", [TP, 4, D])
        ynT = sb("ynT", [P, T])
        lg = sb("lg", [TP, 4, E])
        gm = sb("gm", [TP, 4, 8])
        gi = sb("gi", [TP, 4, 8], U32)
        gif = sb("gif", [TP, 4, 2])
        gs = sb("gs", [TP, 5, 4])
        ge = sb("ge", [TP, 4, 4, E])
        gg = sb("gg", [TP, 3, 4, E])
        g3 = sb("g3", [TP, 4, 3, E], BF16)
        gT = sb("gT", [3 * E, 2 * T], BF16)
        hp = sb("hp", [P, 2, 2 * T])
        moe = y0
        my = mn = hn0

        qk1 = sb("qk1", [TP, 2, 4, D])
        c1, sq1 = (t[:].rearrange("p k t (u c) -> p k (t u) c", u=2) for t in (qk0, qk0s))
        n1 = sb("n1", [TP, 6, 64])
        zq1 = sb("zq1", [TP, 4, 2, D])
        zk1 = sb("zk1", [TP, 4, 8 * D + 64])
        qT1 = sb("qT1", [P, 2, T])
        kT1 = sb("kT1", [P, 2, 4, T])
        w_s = sb("w_s", [P, CHUNKS, 3, T])
        e_s = sb("e_s", [P, CHUNKS, 3, T])
        m8 = sb("m8", [P, CHUNKS, 3, 8])
        nmax = sb("nmax", [P, CHUNKS, 3])
        vp1 = [sb(f"vp1{m}", [P, 2, 274]) for m in range(2)]
        pt = [sb("pt0", [P, T + D + P]), sb("pt1", [S1, T + D + P])]
        y1 = y0
        rec1 = sb("rec1", [TP, 16, 2])
        yn1 = yn
        yn1T = sb("yn1T", [P, T])
        h3T = sb("h3T", [D, 2 * T])
        rw = sb("rw", [1, 2 * T])
        ffo = sb("ffo", [P, T])
        ffy = sb("ffy", [TP, 4, D])

        def part(tile, at, rows, shape):
            n = 1
            for k in shape:
                n *= k
            flat = tile[0:rows].rearrange("p k a t -> p (k a t)")[:, at:at + n]
            if len(shape) == 1:
                return flat
            names = "abcd"[:len(shape)]
            return flat.rearrange(f"p ({' '.join(names)}) -> p {' '.join(names)}", **dict(zip(names[1:], shape[1:])))

        tap_mask = part(w_s, 0, XT, [2, 3, T])
        nat0 = part(w_s, 6 * T, 96, [2, 2, D])
        nat1 = part(w_s, 6 * T + 256, 96, [2, 2, D])
        natp = part(w_s, 6 * T + 512, D, [2, 2, D])

        B = 2 * PAIRS
        tail_w, tail_x, tail_gt, tail_eq, tail_s = (part(w_s, n * T, B, [T]) for n in range(5))
        tail_c = part(w_s, 5 * T, B, [2, T])
        tail_8 = part(w_s, 7 * T, B, [8])
        tail_n = part(w_s, 7 * T + 8, B, [2])
        wt = part(w_s, 8 * T, TP, [2, B])
        TAIL = min(PAIRS, 8)
        PIECES = PAIRS // TAIL
        fin_y = [part(e_s, 2048 * n, TP, [TAIL, 4, D]) for n in range(2)]
        fin_h = [part(w_s, 12 * T, TP, [TAIL, 4, D]),
                 zq[:].rearrange("p h r -> p (h r)").bitcast(F32)[:, 0:TAIL * 256].rearrange("p (i n c) -> p i n c", i=TAIL, n=4)]

        ps_s = [ps(f"ps_s{n}", [P, 2, 512]) for n in range(2)]
        ps_x = ps("ps_x", [P, 512])
        ps_y = ps("ps_y", [P, 512])
        ps_u = ps("ps_u", [P, 512])
        ps_v = ps("ps_v", [P, 512])

        def bank(n):
            return ps_s[n // 2][:, n % 2, :]

        loaded = sem("weights_loaded")
        zeroed = sem("weight_tiles_zeroed")
        const_pool = sem("pool_constants")
        const_dve = sem("vector_constants")
        const_pe = sem("weights_transposed")
        const_act = sem("weights_copied")
        tap_done = sem("tap_added")
        tap_made = sem("tap_mask_made")
        x_loaded = sem("x_loaded")
        routed = sem("router_rows_stored")
        h_stored = sem("h_stored")
        y_stored = sem("y_stored")
        piece_loaded = [sem("even_last_pieces_loaded"), sem("odd_last_pieces_loaded")]
        sel_loaded = sem("router_rows_loaded")
        tail_dve = sem("tail_vector")
        tail_pe = sem("tail_transposed")
        stored = sem("output_stored")
        pe_f = Steps(sem("pe_front"), PE_FRONT)
        act_f = Steps(sem("act_front"), ACT_FRONT)
        dve_f = Steps(sem("vector_front"), DVE_FRONT)
        pool_f = Steps(sem("pool_front"), POOL_FRONT)
        pe_s = Steps(sem("pe_scores"), PE_SCORE)
        act_s = Steps(sem("act_scores"), ACT_SCORE)
        dve_s = Steps(sem("vector_first_max"), DVE_SCORE)
        dve_t = Steps(sem("vector_topk"), DVE_TOPK)
        pe_b = Steps(sem("pe_back"), PE_BACK)
        act_b = Steps(sem("act_back"), ACT_BACK)
        dve_b = Steps(sem("vector_back"), DVE_BACK)
        pool_k = Steps(sem("pool_kept_h2"), POOL_KEEP)

        def before(eng, steps, name, i):
            if isinstance(i, int) and i == 0:
                return
            eng.wait_ge(*steps.of(name, i - 1))

        turns_pe, turns_dve, turns_pool = sem("pe_turns"), sem("vector_turns"), sem("pool_turns")

        def apart(eng, turns):
            eng.sem_inc(turns, 1)

        def v_view(t, u, step, parts, d0, d1):
            nj = {131: 8, 137: 2}[step]
            return (t[0:parts, u, 0:nj * step].rearrange("p (j x) -> p j x", x=step)[:, :, 0:P]
                    .rearrange("p j (g y) -> p j g y", y=32)[:, :, :, d0:d1])

        block = ctx.enter_context(nc.Block())

        weight_loads = []

        @block.sync
        def _(sp):
            sp.wait_ge(zeroed, 1)

            def load(dst, src):
                sp.dma_start(dst, src).then_inc(loaded, 16)
                weight_loads.append(1)

            with nc.allow_non_contiguous_dma("weights, once"):
                for u in range(2):
                    half = slice(D * u, D * u + D)
                    load(tok_w[half, 0:2, half], dram["L0_tok_W_in"].rearrange("n c m -> c n m"))
                    load(tok_w[half, 2, half], dram["L0_tok_W_out"][1])
                    load(tok_w[half, 3, half], dram["L0_tok_W_out"][0])
                    load(tok_b[half, 0:2], dram["L0_tok_b_in"].rearrange("n c -> c n"))
                    load(tok_b[half, 2:3], dram["L0_tok_b_out"][1:2].rearrange("n c -> c n"))
                    load(core[half, :], dram["L0_tok_core_diag"].rearrange("(c a) -> c a", a=1))
                    load(tok_brow[:, u, :], dram["L0_tok_b_out"][0:1])
                    load(nat0[:, :, u, :], dram["L0_attn_w_qkv"].rearrange("(t r) c -> r t c", r=96))
                    load(nat1[:, :, u, :], dram["L1_attn_qkv_w"].rearrange("(t r) c -> r t c", r=96))
                    for a in range(2):
                        for b in range(2):
                            for gq in range(2):
                                load(natp[:, 0, u, :].rearrange("r (c jp gh d) -> r c gh jp d", c=4, gh=2, d=2)[:, 2 * b + a, gq],
                                     dram["L0_attn_w_proj"].rearrange("r (jp a gh b d) -> r a gh b jp d", a=2, gh=2, b=2, d=2)[:, a, gq, b])
                    for g in range(4):
                        load(natp[:, 1, u, :].rearrange("r (g j d) -> r g j d", g=4, j=2)[:, g],
                             dram["L1_attn_proj_w"].rearrange("r (j g d) -> r g j d", g=4, j=2)[:, g])
                    load(brow1[:, :, u, :], dram["L1_attn_qkv_b"].rearrange("(a k c) -> a k c", a=1, k=3))
                    load(projb1[:, u, :], dram["L1_attn_proj_b"].rearrange("(a c) -> a c", a=1))
                    load(fb2[half, :], dram["L1_ffn_b2"].rearrange("(c a) -> c a", a=1))
                load(gate_w[:], dram["L0_ffn_gate_w"])
                load(gate_b[:], dram["L0_ffn_gate_b"].rearrange("(a e) -> a e", a=1))
                load(w1e[:], dram["L0_ffn_w1"].rearrange("e c f -> c e f"))
                load(wr[:], dram["L1_ffn_wr"])
                load(br[:], dram["L1_ffn_br"].rearrange("(a c) -> a c", a=1))
                load(fw1[:], dram["L1_ffn_w1"].rearrange("c (h f) -> c h f", h=2))
                for s in range(3):
                    load(b2raw[E * s:E * s + E, :], dram["L0_ffn_b2"])
                load(w2e[:], dram["L0_ffn_w2"].rearrange("e f c -> f e c"))
                load(b1e[:], dram["L0_ffn_b1"].rearrange("e f -> f e"))
                load(fw2[:], dram["L1_ffn_w2"].rearrange("(h f) c -> f h c", h=2))
                load(fb1[:], dram["L1_ffn_b1"].rearrange("(h f) -> f h", h=2))
                load(taps[:], dram["L0_tok_conv_filter"].partition_broadcast(XT))
                load(rms_raw[:, 0, :], dram["L0_attn_qn_w"].partition_broadcast(TP))
                load(rms_raw[:, 1, :], dram["L0_attn_kn_w"].partition_broadcast(TP))
                load(ln_gb[:, 0, :], dram["L0_ffn_gamma"].partition_broadcast(TP))
                load(ln_gb[:, 1, :], dram["L0_ffn_beta"].partition_broadcast(TP))
                for n, name in enumerate(("q_gamma", "k_gamma", "q_beta", "k_beta")):
                    load(gb_raw[:, n, :], dram["L1_attn_" + name].partition_broadcast(TP))

            x_pairs = dram["x"].rearrange("(i u) (j p) c -> i u p j c", u=2, p=XT)

            def load_x(i):
                before(sp, pe_f, "xT", i)
                for u in range(2):
                    sp.dma_start(x_in[:, :, u, :], x_pairs[bass.ds(i, 1), u].rearrange("a p j c -> p (a j) c"))\
                      .then_inc(x_loaded, 16)

            def store_route(i):
                sp.wait_ge(*act_b.of("routec", i))
                sp.dma_start(route_dram[bass.ds(i, 1)], rw[:]).then_inc(routed, 16)
                sp.wait_ge(*dve_b.of("hsum", i))
                sp.dma_start(h_dram[bass.ds(i, 1)].rearrange("a p c -> p (a c)"), hsum[:].rearrange("p n c -> p (n c)"))\
                  .then_inc(h_stored, 16)
                sp.wait_ge(*act_b.of("ffTc", i))
                sp.dma_start(y_dram[bass.ds(i, 1)].rearrange("a p c -> p (a c)"), ffy[:].rearrange("p n c -> p (n c)"))\
                  .then_inc(y_stored, 16)

            load_x(0)
            if PAIRS > 1:
                load_x(1)
            if PAIRS > 2:
                with sp.Fori(2, PAIRS) as i:
                    load_x(i)
                    store_route(i - 2)
            for i in range(max(0, PAIRS - 2), PAIRS):
                store_route(i)
            sp.wait_ge(routed, 16 * PAIRS)
            sp.wait_ge(h_stored, 16 * PAIRS)
            sp.wait_ge(y_stored, 16 * PAIRS)
            sp.wait_ge(*dve_t.of(f"k{CHUNKS - 1}r{ROUNDS}p2", PAIRS - 1))
            sp.wait_ge(*pe_b.of(f"pt1_{CHUNKS - 1}", PAIRS - 1))
            sp.dma_start(tail_w, route_dram.rearrange("i (u t) -> (i u) t", u=2)).then_inc(sel_loaded, 16)

            def load_piece(n):
                if n >= 2:
                    sp.wait_ge(stored, 64 * (n - 1))
                    sp.wait_ge(tail_dve, TAIL_FIRST + 8 * (n - 1))
                rows = slice(TAIL * n, TAIL * n + TAIL)
                sp.dma_start(fin_y[n % 2], y_dram[rows].rearrange("i p (n c) -> p i n c", n=4)).then_inc(piece_loaded[n % 2], 16)
                sp.dma_start(fin_h[n % 2], h_dram[rows].rearrange("i p (n c) -> p i n c", n=4)).then_inc(piece_loaded[n % 2], 16)

            out_v = out.rearrange("(i u) (t p) c -> t u p i c", u=2, p=TP)
            load_piece(0)
            if PIECES > 1:
                load_piece(1)
            for n in range(PIECES):
                sp.wait_ge(tail_dve, TAIL_FIRST + 8 * n + 8)
                for m in range(4):
                    sp.dma_start(out_v[m // 2, m % 2, :, TAIL * n:TAIL * n + TAIL, :], fin_y[n % 2][:, :, m, :]).then_inc(stored, 16)
                if n + 2 < PIECES:
                    load_piece(n + 2)
            sp.wait_ge(stored, 64 * PIECES)

        n_loads = 16 * len(weight_loads)

        @block.tensor
        def _(pe):
            pe.wait_ge(loaded, n_loads)
            pe.wait_ge(const_pool, 1)
            for n, nat in enumerate((nat0, nat1)):
                for t in range(2):
                    pe.transpose(ps_x[:, 192 * n + 96 * t:192 * n + 96 * t + 96],
                                 nat[:, t].rearrange("r u c -> r (u c)"), ident[0:96, 0:96])
            for n in range(2):
                last = pe.transpose(ps_x[:, 384 + D * n:384 + D * n + D],
                                    natp[:, n].rearrange("r u c -> r (u c)"), ident[0:D, 0:D])
            last.then_inc(const_pe, 1)
            pe.wait_ge(const_pool, POOL_CONSTANTS)
            pe.wait_ge(const_dve, DVE_CONSTANTS)
            pe.wait_ge(const_act, 1)

            def front(i):
                pe.wait_ge(x_loaded, 32 * i + 32)
                before(pe, act_s, "v1c", i)
                for j in range(3):
                    last = pe.transpose(ps_x[:, XT * j:XT * j + XT], x_in[:, j].rearrange("p u c -> p (u c)"),
                                        ident[0:XT, 0:XT])
                last.then_inc(*pe_f.step("xT"))
                for n, (name, src, rhs) in enumerate((("x0", 0, x0), ("x1", 1, x1), ("x2s", 2, x2s))):
                    pe.wait_ge(*act_f.of(name, i))
                    pe.matmul(ps_x[:, 0:T_IN], tok_w[:, n, :], rhs, start=True, stop=True)\
                      .then_inc(*pe_f.step(f"tok{n}"))
                pe.wait_ge(*act_f.of("x3", i))
                for j in range(3):
                    o = ps_x[0:XT, P * j:P * j + P]
                    pe.matmul(o, x3[:, XT * j:XT * j + XT], tok_w[:, 3, :], start=True, stop=False)
                    last = pe.matmul(o, ones[:, 0:XT], tok_brow[:].rearrange("a u c -> a (u c)"), start=False, stop=True)
                last.then_inc(*pe_f.step("tok3"))
                pe.wait_ge(*act_f.of("x4", i))
                for t in range(2):
                    for j in range(2):
                        last = pe.matmul(ps_x[0:TP, P * t:P * t + P], toeplitz[:, t + j, TP * t:TP * t + TP],
                                         x4[:, t + j, :], start=(j == 0), stop=(j == 1))
                last.then_inc(*pe_f.step("conv"))
                pe.wait_ge(*dve_f.of("hn0", i))
                to_features(hn0, ps_x).then_inc(*pe_f.step("hn0T"))
                pe.wait_ge(*act_f.of("hn0Tc", i))
                for t in range(2):
                    last = pe.matmul(ps_x[0:TP, 256 * t:256 * t + 256], hn0T[:, TP * t:TP * t + TP],
                                     w_qkv0[:, 0:2].rearrange("p k u c -> p (k u c)"), start=True, stop=True)
                last.then_inc(*pe_f.step("qk0"))
                pe.wait_ge(*act_f.of("qk0s", i))
                w_v = w_qkv0[:, 2].rearrange("p u c -> p (u c)")
                pe.matmul(ps_x[:, 0:P], hn0T[:, 0:P], w_v, start=True, stop=True)
                pe.matmul(ps_x[0:S1, P:2 * P], hn0T[:, P:T], w_v, start=True, stop=True)\
                  .then_inc(*pe_f.step("v0"))
                before(pe, act_s, f"sc{CHUNKS - 1}b", i)
                pe.wait_ge(*dve_f.of("c3", i))
                for f in range(8):
                    side, u, half = f // 4, f // 2 % 2, f % 2
                    if f >= 4:
                        pe.wait_ge(*act_f.of(f"zTc{f - 4}", i))
                    o = bank(f % 4).bitcast(BF16)
                    z = (zq, zk)[side][:].rearrange("p (n j y) r -> p n j (y r)", n=4, y=4)
                    for j in range(4):
                        for t in range(2):
                            c = T * j + TP * t
                            last = pe.transpose(o[:, c:c + TP], z[:, 2 * t + u, 4 * half + j, :], ident_b[0:TP, 0:TP])
                    last.then_inc(*pe_f.step(f"zT{f}"))
                pe.wait_ge(*act_f.of("zTc7", i))
                pe.wait_ge(*act_f.of("v0c", i))
                before(pe, act_f, "moec", i)

                def scores(n):
                    u, m = n // 8, n % 8
                    if n >= 2:
                        pe.wait_ge(*act_f.of(f"ex{n - 2}", i))
                    for b in range(2):
                        o = ps_s[n % 2][:, b, :]
                        pe.matmul(o[:, 0:2 * UNIT], ident_b[:], causal[:].rearrange("p a c -> p (a c)"),
                                  start=True, stop=False, skip_group_check=True)
                        g = 2 * (m % 2) + b
                        rows = slice(32 * g, 32 * g + ROWS0)
                        for a in range(2):
                            j = 2 * (m // 2) + a
                            pe.matmul(o[:, UNIT * a:UNIT * a + T], kT0[rows, u, j, 0:P], qT0[rows, u, j, :],
                                      start=False, stop=False, skip_group_check=True)
                            last = pe.matmul(o[0:S1, UNIT * a + T:UNIT * a + UNIT], kT0[rows, u, j, P:T],
                                             qT0[rows, u, j, P:T], start=False, stop=(a == 1), skip_group_check=True)
                    last.then_inc(*pe_f.step(f"sc{n}"))

                def values(n):
                    u, m = n // 8, n % 8
                    pe.wait_ge(*act_f.of(f"ex{n}", i))
                    for c in range(4):
                        w = slice(32 * (4 * m + c), 32 * (4 * m + c) + 32)
                        pe.matmul(ps_y[32 * c:32 * c + 32, T * u:T * u + T], vp0[0][:, u, w], e0[:, n % 2, c, 0:T],
                                  start=(m == 0), stop=False, skip_group_check=True)
                    for c in range(4):
                        w = slice(32 * (4 * m + c), 32 * (4 * m + c) + 32)
                        last = pe.matmul(ps_y[32 * c:32 * c + 32, T * u + P:T * u + T], vp0[1][0:S1, u, w],
                                         e0[0:S1, n % 2, c, T:UNIT], start=False, stop=(m == 7), skip_group_check=True)
                    last.then_inc(*pe_f.step(f"pv{n}"))

                for n in range(17):
                    if n < 16:
                        scores(n)
                    if n:
                        values(n - 1)
                pe.wait_ge(*act_f.of("y0c", i))
                to_tokens(y0, ps_x).then_inc(*pe_f.step("y0T"))
                pe.wait_ge(*dve_f.of("yn0", i))
                to_features(yn, ps_x).then_inc(*pe_f.step("yn0T"))
                pe.wait_ge(*act_f.of("yn0Tc", i))
                for t in range(2):
                    last = pe.matmul(ps_x[0:TP, P * t:P * t + P], ynT[:, TP * t:TP * t + TP],
                                     w_proj[:, 0].rearrange("p u c -> p (u c)"), start=True, stop=True)
                last.then_inc(*pe_f.step("proj0"))
                pe.wait_ge(*dve_f.of("hn1", i))
                apart(pe, turns_pe)
                to_features64(hn1, ps_x).then_inc(*pe_f.step("hn1T"))
                pe.wait_ge(*act_f.of("hn1Tc", i))
                for n in range(4):
                    t, u = n // 2, n % 2
                    o = ps_x[0:TP, E * n:E * n + E]
                    pe.matmul(o, hn1T[:, T * u + TP * t:T * u + TP * t + TP], gate_w[:], start=True, stop=False)
                    last = pe.matmul(o, ones[:, 0:TP], gate_b[:], start=False, stop=True)
                last.then_inc(*pe_f.step("gate"))
                pe.wait_ge(*dve_f.of("G3", i))
                apart(pe, turns_pe)
                o = ps_x[:].bitcast(BF16)
                for n in range(4):
                    t, u = n // 2, n % 2
                    last = pe.transpose(o[0:3 * E, T * u + TP * t:T * u + TP * t + TP],
                                        g3[:, n].rearrange("p s e -> p (s e)"), ident_b[0:TP, 0:TP])
                last.then_inc(*pe_f.step("gT"))
                pe.wait_ge(*act_f.of("gTc", i))

                def up(e):
                    if e >= 2:
                        pe.wait_ge(*act_f.of(f"gc{e - 2}", i))
                    pe.matmul(bank(e % 2)[:, 0:2 * T], w1e[:, e, :], hn1T[:], start=True, stop=True)
                    pe.matmul(bank(2 + e % 2)[:, 0:2 * T], pick[:, e, :], gT[:], start=True, stop=True)\
                      .then_inc(*pe_f.step(f"z{e}"))

                def down(e):
                    if e == 0:
                        for s in range(3):
                            pe.matmul(ps_y[0:D, 0:2 * T], b2e[:, s, :], gT[:], start=(s == 0), stop=False,
                                      skip_group_check=True)
                    pe.wait_ge(*pool_f.of(f"hp{e}", i))
                    r = D * (e % 2)
                    pe.matmul(ps_y[r:r + D, 0:2 * T], w2e[:, e, :], hp[:, e % 2, :], start=(e == 1), stop=(e >= E - 2),
                              skip_group_check=True).then_inc(*pe_f.step(f"o{e}"))

                for e in range(E + 1):
                    if e < E:
                        up(e)
                    if e:
                        down(e - 1)
                pe.wait_ge(*act_f.of("moec", i))
                to_tokens(moe, ps_x).then_inc(*pe_f.step("moeT"))
                pe.wait_ge(*dve_f.of("hn2", i))
                to_features(hn2, ps_x).then_inc(*pe_f.step("hn2T"))
                pe.wait_ge(*act_f.of("hn2Tc", i))
                for t in range(2):
                    o = ps_x[0:TP, 256 * t:256 * t + 256]
                    pe.matmul(o, hn2T[:, TP * t:TP * t + TP], w_qkv1[:, 0:2].rearrange("p k u c -> p (k u c)"),
                              start=True, stop=False)
                    last = pe.matmul(o, ones[:, 0:TP], brow1[:, 0:2].rearrange("a k u c -> a (k u c)"), start=False, stop=True)
                last.then_inc(*pe_f.step("qk1"))
                pe.wait_ge(*act_f.of(f"gc{E - 1}", i))
                pe.wait_ge(*pool_f.of("gk1", i))
                for f in range(5):
                    if f == 4:
                        pe.wait_ge(*act_f.of("kqTc0", i))
                    for a in range(2):
                        for t in range(2):
                            if f < 4:
                                u, p = f // 2, 2 * (f % 2) + a
                                src = zk1[:, 2 * t + u, P * p:P * p + P]
                            else:
                                u = a
                                src = zq1[:, 2 * t + u].rearrange("p n c -> p (n c)")
                            c = T * a + TP * t
                            last = pe.transpose(bank(f % 4)[:, c:c + TP], src, ident[0:TP, 0:TP])
                    last.then_inc(*pe_f.step(f"kqT{f}"))
                pe.wait_ge(*act_f.of("kqTc4", i))

            def to_features(src, dst):
                for t in range(2):
                    last = pe.transpose(dst[:, TP * t:TP * t + TP], src[:, 2 * t:2 * t + 2].rearrange("p u c -> p (u c)"),
                                        ident[0:TP, 0:TP])
                return last

            def to_features64(src, dst):
                for n in range(4):
                    t, u = n // 2, n % 2
                    last = pe.transpose(dst[0:D, T * u + TP * t:T * u + TP * t + TP], src[:, n, :], ident[0:TP, 0:TP])
                return last

            def to_tokens(src, dst):
                for n in range(4):
                    t, u = n // 2, n % 2
                    last = pe.transpose(dst[0:TP, P * n:P * n + P], src[:, T * u + TP * t:T * u + TP * t + TP], ident[:])
                return last

            def scores1(i, k):
                u, p = k // 4, k % 4
                if k >= 2:
                    pe.wait_ge(*act_s.of(f"sc{k - 2}b", i))
                o = ps_s[k % 2]
                for a in range(2):
                    half = slice(D * a, D * a + D)
                    pe.matmul(o[:, a, 0:T], qT1[half, u, 0:P], kT1[half, u, p, :], start=True, stop=True)
                    last = pe.matmul(o[half, a, T:2 * T], qT1[half, u, T - D:T], kT1[half, u, p, :], start=True, stop=True)
                last.then_inc(*pe_s.step(f"s{k}"))

            def values1(i, k):
                u, p = k // 4, k % 4
                pe.wait_ge(*dve_t.of(f"k{k}r{ROUNDS}p2", i))
                if k:
                    pe.wait_ge(*act_b.of(f"pc1_{k - 1}", i))
                else:
                    before(pe, act_b, "ffTc", i)
                for m, (m0, m1) in enumerate(((0, P), (P, T))):
                    if m:
                        pe.wait_ge(*act_b.of(f"pc0_{k}", i))
                        apart(pe, turns_pe)
                    pe.transpose(ps_u[0:m1 - m0, T - D:T + D], e_s[:, k, 2, m0:m1], ident[:])
                    pe.transpose(ps_u[0:m1 - m0, 0:P], e_s[:, k, 0, m0:m1], ident[:])
                    last = pe.transpose(ps_u[0:m1 - m0, T + D:T + D + P], e_s[:, k, 1, m0:m1], ident[:])
                    last.then_inc(*pe_b.step(f"pt{m}_{k}"))
                pe.wait_ge(*act_b.of(f"pc1_{k}", i))
                for a in range(2):
                    h = 2 * p + a
                    g, j = h % 4, h // 4
                    pieces = ((T + D, 0, P), (T + D - S1, P, T)) if a else ((0, 0, T),)
                    for m, rows in enumerate((P, S1)):
                        for at, n0, n1 in pieces:
                            last = pe.matmul(ps_v[32 * g:32 * g + 32, T * u + n0:T * u + n1], vp1[m][0:rows, u, 32 * h:32 * h + 32],
                                             pt[m][0:rows, at:at + n1 - n0], start=(j == 0 and m == 0 and n0 == 0),
                                             stop=(j == 1 and m == 1), skip_group_check=True)
                last.then_inc(*pe_b.step(f"pv{k}"))

            def v1(i):
                pe.wait_ge(*act_f.of("qk1c", i))
                w_v, b_v = (w[:, 2].rearrange("p u c -> p (u c)") for w in (w_qkv1, brow1))
                for o, c, n in ((ps_x[:, 0:P], slice(0, P), P), (ps_x[0:S1, P:2 * P], slice(P, T), S1)):
                    pe.matmul(o, hn2T[:, c], w_v, start=True, stop=False)
                    last = pe.matmul(o, ones[:, 0:n], b_v, start=False, stop=True)
                last.then_inc(*pe_s.step("v1"))

            def back(i):
                pe.wait_ge(*act_b.of("y1c", i))
                to_tokens(y1, ps_u).then_inc(*pe_b.step("y1T"))
                pe.wait_ge(*dve_b.of("yn1", i))
                to_features(yn1, ps_u).then_inc(*pe_b.step("yn1T"))
                pe.wait_ge(*act_b.of("yn1Tc", i))
                for t in range(2):
                    o = ps_u[0:TP, P * t:P * t + P]
                    pe.matmul(o, yn1T[:, TP * t:TP * t + TP], w_proj[:, 1].rearrange("p u c -> p (u c)"), start=True, stop=False)
                    last = pe.matmul(o, ones[:, 0:TP], projb1[:].rearrange("a u c -> a (u c)"), start=False, stop=True)
                last.then_inc(*pe_b.step("proj1"))
                pe.wait_ge(*dve_b.of("hn3", i))
                apart(pe, turns_pe)
                to_features64(hn3, ps_u).then_inc(*pe_b.step("h3T"))
                pe.wait_ge(*act_b.of("h3Tc", i))
                apart(pe, turns_pe)
                pe.matmul(ps_u[0:1, 0:2 * T], wr[:], h3T[:], start=True, stop=True).then_inc(*pe_b.step("route"))
                for h in range(2):
                    if h:
                        pe.wait_ge(*act_b.of("routec", i))
                    pe.matmul((ps_v, ps_u)[h][:, 0:2 * T], fw1[:, h, :], h3T[:], start=True, stop=True)\
                      .then_inc(*pe_b.step(f"ffz{h}"))
                pe.wait_ge(*act_b.of("gelu1", i))
                for u in range(2):
                    for h in range(2):
                        last = pe.matmul(ps_v[D * u:D * u + D, 0:T], fw2[:, h, :], gh[:, h, T * u:T * u + T],
                                         start=(h == 0), stop=(h == 1))
                last.then_inc(*pe_b.step("ffo"))
                pe.wait_ge(*act_b.of("ffoc", i))
                for t in range(2):
                    last = pe.transpose(ps_u[0:TP, P * t:P * t + P], ffo[:, TP * t:TP * t + TP], ident[:])
                last.then_inc(*pe_b.step("ffT"))

            def body(i, prev):
                front(i)
                for k in range(CHUNKS):
                    if prev is not None:
                        values1(prev, k)
                    scores1(i, k)
                v1(i)
                if prev is not None:
                    back(prev)

            body(0, None)
            if PAIRS > 1:
                body(1, 0)
            if PAIRS > 2:
                with pe.Fori(2, PAIRS) as i:
                    body(i, i - 1)
            for k in range(CHUNKS):
                values1(PAIRS - 1, k)
            back(PAIRS - 1)
            pe.wait_ge(tail_dve, TAIL_SELECTED)
            for t in range(2):
                last = pe.transpose(ps_x[0:TP, B * t:B * t + B], tail_s[:, TP * t:TP * t + TP], ident[0:B, 0:B])
            last.then_inc(tail_pe, 1)

        @block.scalar
        def _(act):
            act.wait_ge(const_pe, 1)
            for n, w in enumerate((w_qkv0, w_qkv1)):
                for u in range(2):
                    half = slice(D * u, D * u + D)
                    kinds = 2 + n
                    act.copy(w[half, 0:kinds, u, :], ps_x[half, 192 * n:192 * n + D * kinds].rearrange("p (k c) -> p k c", k=kinds))
            for u in range(2):
                half = slice(D * u, D * u + D)
                for a in range(2):
                    for gq in range(2):
                        act.copy(w_qkv0[half, 2, u, :].rearrange("p (jp gh b a d) -> p a gh jp b d", gh=2, b=2, a=2, d=2)[:, a, gq],
                                 ps_x[half, 128:192].rearrange("p (jp a gh b d) -> p a gh jp b d", a=2, gh=2, b=2, d=2)[:, a, gq])
            for u in range(2):
                half = slice(D * u, D * u + D)
                last = act.copy(w_proj[half, :, u, :], ps_x[half, 384:512].rearrange("p (k c) -> p k c", k=2))
            last.then_inc(const_act, 1)
            act.wait_ge(const_pool, POOL_CONSTANTS)
            act.wait_ge(const_dve, DVE_CONSTANTS)
            act.wait_ge(loaded, n_loads)

            def v_copy(tiles, psum, u, step, j, d):
                for m, rows in enumerate((P, S1)):
                    src = psum[0:rows, P * m + D * u:P * m + D * u + D].rearrange("p (j g d) -> p j g d", j=j, g=4)
                    last = act.copy(v_view(tiles[m], u, step, rows, 0, d), src)
                return last

            def front(i):
                act.wait_ge(*pe_f.of("xT", i))
                act.copy(x0, ps_x[:, 0:T_IN]).then_inc(*act_f.step("x0"))
                act.wait_ge(*pe_f.of("tok0", i))
                act.activation(x1, ps_x[:, 0:T_IN], ACT.Tanh, bias=tok_b[:, 0:1]).then_inc(*act_f.step("x1"))
                act.wait_ge(*pe_f.of("tok1", i))
                act.activation(x2[:], ps_x[:, 0:T_IN], ACT.Tanh, bias=tok_b[:, 1:2]).then_inc(*act_f.step("x2"))
                act.wait_ge(*act_f.of("x2", i))
                act.activation(x2s, x2[:], ACT.Square).then_inc(*act_f.step("x2s"))
                act.wait_ge(*pe_f.of("tok2", i))
                act.activation(x3, ps_x[:, 0:T_IN], ACT.Tanh, bias=tok_b[:, 2:3]).then_inc(*act_f.step("x3"))
                act.wait_ge(*pe_f.of("tok3", i))
                act.activation(x4[:].rearrange("p j c -> p (j c)"), ps_x[0:XT, 0:3 * P], ACT.Tanh).then_inc(*act_f.step("x4"))
                act.wait_ge(*pe_f.of("conv", i))
                before(act, dve_f, "h1", i)
                act.copy(h0[:].rearrange("p n c -> p (n c)"), ps_x[0:TP, 0:256]).then_inc(*act_f.step("h0"))
                act.wait_ge(*pe_f.of("hn0T", i))
                act.copy(hn0T[:], ps_x[:, 0:T]).then_inc(*act_f.step("hn0Tc"))
                act.wait_ge(*pe_f.of("qk0", i))
                src = ps_x[0:TP, :].rearrange("p (t k c) -> p k t c", t=2, k=2)
                act.copy(qk0[:], src).then_inc(*act_f.step("qk0c"))
                act.activation(qk0s[:], src, ACT.Square).then_inc(*act_f.step("qk0s"))
                act.wait_ge(*pe_f.of("v0", i))
                for u in range(2):
                    last = v_copy(vp0, ps_x, u, 131, 8, HD0)
                last.then_inc(*act_f.step("v0c"))
                for f in range(8):
                    side, u, half = f // 4, f // 2 % 2, f % 2
                    act.wait_ge(*pe_f.of(f"zT{f}", i))
                    dst = (qT0, kT0)[side][:, u, 4 * half:4 * half + 4, :].rearrange("p j t -> p (j t)")
                    act.copy(dst, bank(f % 4).bitcast(BF16)[:, 0:4 * T]).then_inc(*act_f.step(f"zTc{f}"))
                for n in range(16):
                    act.wait_ge(*pe_f.of(f"sc{n}", i))
                    if n >= 2:
                        act.wait_ge(*pe_f.of(f"pv{n - 2}", i))
                    act.activation(e0[:, n % 2].rearrange("p (b a) c -> p b (a c)", b=2), ps_s[n % 2][:, :, 0:2 * UNIT], ACT.Exp)\
                       .then_inc(*act_f.step(f"ex{n}"))
                act.wait_ge(*pe_f.of("pv15", i))
                act.copy(y0[:], ps_y[:, 0:2 * T]).then_inc(*act_f.step("y0c"))
                act.wait_ge(*pe_f.of("yn0T", i))
                act.copy(ynT[:], ps_x[:, 0:T]).then_inc(*act_f.step("yn0Tc"))
                act.wait_ge(*pe_f.of("hn1T", i))
                act.copy(hn1T[:], ps_x[0:D, 0:2 * T]).then_inc(*act_f.step("hn1Tc"))
                act.wait_ge(*dve_f.of("gd", i))
                act.activation(gs[:, 1, :], gs[:, 0, :], ACT.Exp).then_inc(*act_f.step("gexp"))
                act.wait_ge(*pe_f.of("gT", i))
                act.copy(gT[:], ps_x[:].bitcast(BF16)[0:3 * E, 0:2 * T]).then_inc(*act_f.step("gTc"))
                for e in range(E):
                    act.wait_ge(*pe_f.of(f"z{e}", i))
                    if e >= 2:
                        act.wait_ge(*pool_f.of(f"hp{e - 2}", i))
                    act.activation(hr[:, e % 2, :], bank(e % 2)[:, 0:2 * T], ACT.Relu, bias=b1e[:, e:e + 1])\
                       .then_inc(*act_f.step(f"relu{e}"))
                    act.copy(hg[:, e % 2, :], bank(2 + e % 2)[:, 0:2 * T]).then_inc(*act_f.step(f"gc{e}"))
                act.wait_ge(*pe_f.of(f"o{E - 1}", i))
                act.copy(moe[:], ps_y[:, 0:2 * T]).then_inc(*act_f.step("moec"))
                act.wait_ge(*pe_f.of("hn2T", i))
                act.copy(hn2T[:], ps_x[:, 0:T]).then_inc(*act_f.step("hn2Tc"))
                act.wait_ge(*pe_f.of("qk1", i))
                for t in range(2):
                    last = act.copy(qk1[:, :, 2 * t:2 * t + 2, :],
                                    ps_x[0:TP, 256 * t:256 * t + 256].rearrange("p (k u c) -> p k u c", k=2, u=2))
                last.then_inc(*act_f.step("qk1c"))
                for f in range(5):
                    act.wait_ge(*pe_f.of(f"kqT{f}", i))
                    dst = kT1[:, f // 2, 2 * (f % 2):2 * (f % 2) + 2, :] if f < 4 else qT1[:]
                    act.copy(dst.rearrange("p a t -> p (a t)"), bank(f % 4)[:, 0:2 * T]).then_inc(*act_f.step(f"kqTc{f}"))

            def scores1(i, k):
                before(act, dve_t, f"k{k}r{ROUNDS}p2", i)
                act.wait_ge(*pe_s.of(f"s{k}", i))
                act.copy(w_s[:, k, 0:2, :], ps_s[k % 2][:, :, 0:T]).then_inc(*act_s.step(f"sc{k}a"))
                for a in range(2):
                    half = slice(D * a, D * a + D)
                    last = act.copy(w_s[half, k, 2, :], ps_s[k % 2][half, a, T:2 * T])
                last.then_inc(*act_s.step(f"sc{k}b"))

            def exps1(i, k):
                act.wait_ge(*dve_s.of(f"m{k}n", i))
                before(act, pe_b, f"pt1_{k}", i)
                for t in range(3):
                    last = act.activation(e_s[:, k, t, :], w_s[:, k, t, :], ACT.Exp, bias=nmax[:, k, t:t + 1])
                last.then_inc(*act_s.step(f"e{k}"))

            def values1(i, k):
                for m, rows in enumerate((P, S1)):
                    act.wait_ge(*pe_b.of(f"pt{m}_{k}", i))
                    act.copy(pt[m][:], ps_u[0:rows, 0:T + D + P]).then_inc(*act_b.step(f"pc{m}_{k}"))

            def v1(i):
                act.wait_ge(*pe_s.of("v1", i))
                before(act, pe_b, f"pv{CHUNKS - 1}", i)
                for u in range(2):
                    last = v_copy(vp1, ps_x, u, 137, 2, HD1)
                last.then_inc(*act_s.step("v1c"))

            def back(i):
                act.wait_ge(*pe_b.of(f"pv{CHUNKS - 1}", i))
                act.copy(y1[:], ps_v[:, 0:2 * T]).then_inc(*act_b.step("y1c"))
                act.wait_ge(*pe_b.of("yn1T", i))
                act.copy(yn1T[:], ps_u[:, 0:T]).then_inc(*act_b.step("yn1Tc"))
                act.wait_ge(*pe_b.of("h3T", i))
                act.copy(h3T[:], ps_u[0:D, 0:2 * T]).then_inc(*act_b.step("h3Tc"))
                act.wait_ge(*pe_b.of("route", i))
                if not (isinstance(i, int) and i == 0):
                    act.wait_ge(routed, 16 * i)
                act.activation(rw[:], ps_u[0:1, 0:2 * T], ACT.Identity, bias=br[:, 0:1]).then_inc(*act_b.step("routec"))
                for h in range(2):
                    act.wait_ge(*pe_b.of(f"ffz{h}", i))
                    act.activation(gh[:, h, :], (ps_v, ps_u)[h][:, 0:2 * T], ACT.Gelu_apprx_tanh, bias=fb1[:, h:h + 1])\
                       .then_inc(*act_b.step(f"gelu{h}"))
                act.wait_ge(*pe_b.of("ffo", i))
                act.activation(ffo[:], ps_v[:, 0:T], ACT.Identity, bias=fb2[:, 0:1]).then_inc(*act_b.step("ffoc"))
                act.wait_ge(*pe_b.of("ffT", i))
                if not (isinstance(i, int) and i == 0):
                    act.wait_ge(y_stored, 16 * i)
                act.copy(ffy[:].rearrange("p n c -> p (n c)"), ps_u[0:TP, 0:256]).then_inc(*act_b.step("ffTc"))

            def body(i, prev):
                front(i)
                for k in range(CHUNKS):
                    if prev is not None:
                        values1(prev, k)
                    scores1(i, k)
                for k in range(CHUNKS):
                    exps1(i, k)
                v1(i)
                if prev is not None:
                    back(prev)

            body(0, None)
            if PAIRS > 1:
                body(1, 0)
            if PAIRS > 2:
                with act.Fori(2, PAIRS) as i:
                    body(i, i - 1)
            for k in range(CHUNKS):
                values1(PAIRS - 1, k)
            back(PAIRS - 1)

        @block.gpsimd
        def _(pool):
            for w in (tok_w, w_qkv0, w_qkv1):
                pool.memset(w[:], 0.0)
            pool.memset(w_proj[:], 0.0).then_inc(zeroed, 1)
            pool.memset(ident[:], 0.0)
            pool.memset(ident_b[:], 0.0)
            pool.memset(pick[:], 0.0)
            pool.memset(causal[:], 0.0).then_inc(zeroed, 1)
            pool.wait_ge(zeroed, 2)
            pool.affine_select(ident[:], ident[:], [[-1, P]], ALU.not_equal, 1.0, base=0, channel_multiplier=1)
            pool.affine_select(ident_b[:], ident_b[:], [[-1, P]], ALU.not_equal, 1.0, base=0, channel_multiplier=1)\
                .then_inc(const_pool, 1)
            pool.affine_select(causal[:, :, 0:T], causal[:, :, 0:T], [[0, 2], [1, T]], ALU.is_ge, MASKED,
                               base=0, channel_multiplier=-1)
            pool.affine_select(causal[:, :, T:UNIT], causal[:, :, T:UNIT], [[0, 2], [1, S1]], ALU.is_ge, MASKED,
                               base=0, channel_multiplier=-1).then_inc(const_pool, 1)
            for s in range(3):
                pool.wait_ge(const_pool, 2 + s)
                pool.affine_select(pick[:], pick[:], [[-1, E], [0, P]], ALU.not_equal, 1.0,
                                   base=-E * s, channel_multiplier=1).then_inc(const_pool, 1)
            pool.iota(expert_id[:], [[0, 4], [1, E]], base=0, channel_multiplier=0,
                      allow_small_or_imprecise_dtypes=True).then_inc(const_pool, 1)
            for k in range(TAPS):
                if k >= 2:
                    pool.wait_ge(tap_done, k)
                pool.memset(tap_mask[:, k % 2], 0.0).then_inc(tap_made, 1)
                pool.wait_ge(tap_made, 2 * k + 1)
                pool.affine_select(tap_mask[:, k % 2], tap_mask[:, k % 2], [[XT, 3], [-2, T]], ALU.not_equal, 1.0,
                                   base=PAD - k, channel_multiplier=1).then_inc(tap_made, 1)
            pool.wait_ge(const_dve, DVE_CONSTANTS)

            def front(i):
                pool.wait_ge(*act_f.of("qk0s", i))
                sq2 = qk0s[:].rearrange("p k t (h d) -> p (k t h) d", d=2)
                pool.tensor_tensor(rx[:], sq2[:, :, 0], sq2[:, :, 1], ALU.add).then_inc(*pool_f.step("ss"))
                pool.wait_ge(*pool_f.of("ss", i))
                apart(pool, turns_pool)
                pool.tensor_scalar(rx[:], rx[:], 1.0 / HD0, 1e-6, ALU.mult, ALU.add).then_inc(*pool_f.step("sx"))
                y = rr[:]
                pool.wait_ge(*dve_f.of("b_guess", i))
                for r in range(3):
                    pool.tensor_tensor(rt[:], y, y, ALU.mult).then_inc(*pool_f.step(f"rn{r}a"))
                    pool.wait_ge(*pool_f.of(f"rn{r}a", i))
                    pool.tensor_tensor(rt[:], rt[:], rx[:], ALU.mult).then_inc(*pool_f.step(f"rn{r}b"))
                    pool.wait_ge(*pool_f.of(f"rn{r}b", i))
                    apart(pool, turns_pool)
                    pool.tensor_scalar(rt[:], rt[:], -0.5, 1.5, ALU.mult, ALU.add).then_inc(*pool_f.step(f"rn{r}c"))
                    pool.wait_ge(*pool_f.of(f"rn{r}c", i))
                    pool.tensor_tensor(y, y, rt[:], ALU.mult).then_inc(*pool_f.step(f"rn{r}d"))
                    pool.wait_ge(*pool_f.of(f"rn{r}d", i))
                q2 = qk0[:].rearrange("p k t (h d) -> p (k t h) d", d=2)
                pool.tensor_tensor(q2, q2, y.unsqueeze(2).broadcast_to([TP, 256, 2]), ALU.mult).then_inc(*pool_f.step("qr"))
                pool.wait_ge(*pool_f.of("qr", i))
                pool.tensor_tensor(qk0[:], qk0[:], rms_w[:].unsqueeze(2).broadcast_to([TP, 2, 2, P]), ALU.mult)\
                    .then_inc(*pool_f.step("qw"))
                pool.wait_ge(*pool_f.of("qw", i))
                qn, kn = (qk0[:, s].rearrange("p t c -> p (t c)") for s in range(2))
                pool.tensor_tensor(selfp[:], qn, kn, ALU.mult).then_inc(*pool_f.step("qkp"))
                pool.wait_ge(*pool_f.of("qkp", i))
                sp2 = selfp[:].rearrange("p (h d) -> p h d", d=2)
                pool.tensor_tensor(selfs[:], sp2[:, :, 0], sp2[:, :, 1], ALU.add).then_inc(*pool_f.step("self"))
                pool.wait_ge(*pool_f.of("self", i))
                apart(pool, turns_pool)
                pool.tensor_scalar(negc[:], selfs[:], room[:, 0:1], -1.0, ALU.max, ALU.mult).then_inc(*pool_f.step("negc"))
                pool.wait_ge(*dve_f.of("c1", i))
                q4 = [qk0[:, s].rearrange("p t (h d) -> p (t h) d", d=2) for s in range(2)]
                r4 = [[res[:, r, s].rearrange("p (h d) -> p h d", d=2) for s in range(2)] for r in range(2)]
                slot = lambda z, n: z[:, :, 2 * n:2 * n + 2]
                pool.tensor_tensor(r4[0][0], q4[0], slot(zq, 0), ALU.subtract).then_inc(*pool_f.step("rq1"))
                pool.tensor_tensor(r4[0][1], q4[1], slot(zk, 2), ALU.subtract).then_inc(*pool_f.step("rk1"))
                pool.tensor_tensor(resc[:, 0], negc[:], zq[:, :, 12], ALU.subtract).then_inc(*pool_f.step("rc1"))
                pool.wait_ge(*dve_f.of("c2", i))
                pool.tensor_tensor(r4[1][0], r4[0][0], slot(zq, 3), ALU.subtract).then_inc(*pool_f.step("rq2"))
                pool.tensor_tensor(r4[1][1], r4[0][1], slot(zk, 1), ALU.subtract).then_inc(*pool_f.step("rk2"))
                pool.tensor_tensor(resc[:, 1], resc[:, 0], zq[:, :, 13], ALU.subtract).then_inc(*pool_f.step("rc2"))
                for e in range(E):
                    pool.wait_ge(*act_f.of(f"gc{e}", i))
                    if e >= 2:
                        pool.wait_ge(*pe_f.of(f"o{e - 2}", i))
                    pool.tensor_tensor(hp[:, e % 2, :], hr[:, e % 2, :], hg[:, e % 2, :], ALU.mult).then_inc(*pool_f.step(f"hp{e}"))
                flat = lambda t: t.rearrange("p k n c -> p (k n c)")
                pool.wait_ge(*dve_f.of("g_cen", i))
                pool.tensor_tensor(flat(sq1), flat(c1), flat(c1), ALU.mult).then_inc(*pool_f.step("g_sq"))
                pool.wait_ge(*dve_f.of("g_n2c", i))
                c8 = c1.rearrange("p k n (h d) -> p (k n h) d", d=HD1)
                pool.tensor_tensor(c8, c8, n1[:, 4, :].unsqueeze(2).broadcast_to([TP, 64, HD1]), ALU.mult)\
                    .then_inc(*pool_f.step("g_norm"))
                pool.wait_ge(*pool_f.of("g_norm", i))
                c4 = c1.rearrange("p k (t u) c -> p k t (u c)", t=2)
                pool.tensor_tensor(c4, c4, gam1[:].unsqueeze(2).broadcast_to([TP, 2, 2, P]), ALU.mult).then_inc(*pool_f.step("g_gam"))
                pool.wait_ge(*pool_f.of("g_gam", i))
                for n in range(2):
                    dst = zq1[:, :, n, :].rearrange("p (t u) c -> p t u c", t=2)
                    pool.tensor_tensor(dst, c1[:, 0].rearrange("p (t u) c -> p t u c", t=2),
                                       bet1[:, 0].rearrange("p (u c) -> p u c", u=2).unsqueeze(1).broadcast_to([TP, 2, 2, D]),
                                       ALU.add).then_inc(*pool_f.step(f"gq{n}"))
                for t in range(2):
                    dst = zk1[:, 2 * t:2 * t + 2, :].rearrange("p u (h x) -> p u h x", x=72)[:, :, :, 0:HD1]
                    pool.tensor_tensor(dst, c1[:, 1, 2 * t:2 * t + 2].rearrange("p u (h d) -> p u h d", d=HD1),
                                       bet1[:, 1].rearrange("p (u h d) -> p u h d", u=2, d=HD1), ALU.add)\
                        .then_inc(*pool_f.step(f"gk{t}"))

            def keep(i):
                if not (isinstance(i, int) and i == 0):
                    pool.wait_ge(*dve_b.of("h3", i - 1))
                pool.wait_ge(*dve_f.of("h2", i))
                apart(pool, turns_pool)
                pool.tensor_copy(h2k[:], h2[:]).then_inc(*pool_k.step("h2k"))

            def body(i, prev):
                front(i)
                keep(i)

            body(0, None)
            if PAIRS > 1:
                body(1, 0)
            if PAIRS > 2:
                with pool.Fori(2, PAIRS) as i:
                    body(i, i - 1)

        @block.vector
        def _(dve):
            chain = [0]

            def const(ins):
                chain[0] += 1
                ins.then_inc(const_dve, 1)

            const(dve.memset(ones[:], 1.0))
            for m in range(2):
                const(dve.memset(vp0[m][:], 0.0))
                const(dve.memset(vp1[m][:], 0.0))
            for z in (zq, zk, zk1):
                const(dve.memset(z[:], 0.0))
            const(dve.memset(toeplitz[:], 0.0))
            dve.wait_ge(const_dve, chain[0])
            for m in range(2):
                for u in range(2):
                    const(dve.memset(v_view(vp0[m], u, 131, P, HD0, HD0 + 1), 1.0))
                    const(dve.memset(v_view(vp1[m], u, 137, P, HD1, HD1 + 1), 1.0))
            const(dve.memset(zk[:, :, 12:15], 1.0))
            dve.wait_ge(loaded, n_loads)
            const(dve.tensor_scalar(core_abs[:], core[:], -1.0, None, ALU.mult))
            dve.wait_ge(const_dve, chain[0])
            const(dve.tensor_tensor(core_abs[:], core_abs[:], core[:], ALU.max))
            dve.wait_ge(const_dve, chain[0])
            const(dve.tensor_scalar(tok_w[:, 2, :], tok_w[:, 2, :], core_abs[:, 0:1], None, ALU.mult))
            for s in range(2):
                const(dve.tensor_scalar(rms_w[:, s, :].rearrange("p (h d) -> p h d", d=2),
                                        rms_raw[:, s, :].unsqueeze(1).broadcast_to([TP, D, 2]),
                                        HD0 ** -0.5 if s == 0 else 1.0, None, ALU.mult))
            dve.wait_ge(const_dve, chain[0])
            const(dve.tensor_tensor(wprod[:], rms_w[:, 0, 0:2], rms_w[:, 1, 0:2], ALU.mult))
            dve.wait_ge(const_dve, chain[0])
            const(dve.tensor_reduce(room[:], wprod[:], AX_X, ALU.max, apply_absolute_value=True))
            dve.wait_ge(const_dve, chain[0])
            const(dve.tensor_scalar(room[:], room[:], float(HD0), -SHIFT_ROOM, ALU.mult, ALU.add))
            for s in range(2):
                for dst, n in ((gam1, s), (bet1, 2 + s)):
                    const(dve.tensor_scalar(dst[:, s, :].rearrange("p (h d) -> p h d", d=HD1),
                                            gb_raw[:, n, :].unsqueeze(1).broadcast_to([TP, 16, HD1]),
                                            HD1 ** -0.5 if s == 0 else 1.0, None, ALU.mult))
            const(dve.tensor_copy(b2e[:, 0, :], b2raw[:]))
            dve.wait_ge(const_dve, chain[0])
            const(dve.tensor_tensor(b2res[:, 0, :], b2raw[:], b2e[:, 0, :], ALU.subtract))
            dve.wait_ge(const_dve, chain[0])
            const(dve.tensor_copy(b2e[:, 1, :], b2res[:, 0, :]))
            dve.wait_ge(const_dve, chain[0])
            const(dve.tensor_tensor(b2res[:, 1, :], b2res[:, 0, :], b2e[:, 1, :], ALU.subtract))
            dve.wait_ge(const_dve, chain[0])
            const(dve.tensor_copy(b2e[:, 2, :], b2res[:, 1, :]))
            for k in range(TAPS):
                dve.wait_ge(tap_made, 2 * k + 2)
                if k:
                    dve.wait_ge(tap_done, k)
                dve.scalar_tensor_tensor(toeplitz[:], tap_mask[:, k % 2], taps[:, k:k + 1], toeplitz[:], ALU.mult, ALU.add)\
                   .then_inc(tap_done, 1)
            dve.wait_ge(tap_done, TAPS)
            const(dve.memset(gs[:, 4, :], 0.0))
            assert chain[0] == DVE_CONSTANTS, chain[0]
            dve.wait_ge(const_pool, POOL_CONSTANTS)

            def rsqrt(x, y, t, tag, i, steps):
                dve.tensor_scalar(y.bitcast(I32), x.bitcast(I32), -0.5, RSQRT_MAGIC, ALU.mult, ALU.add)\
                   .then_inc(*steps.step(f"{tag}_guess"))
                dve.wait_ge(*steps.of(f"{tag}_guess", i))
                for r in range(3):
                    dve.scalar_tensor_tensor(t, y, -0.5, y, ALU.mult, ALU.mult).then_inc(*steps.step(f"{tag}_n{r}a"))
                    dve.wait_ge(*steps.of(f"{tag}_n{r}a", i))
                    dve.tensor_tensor(t, t, x, ALU.mult).then_inc(*steps.step(f"{tag}_n{r}b"))
                    dve.wait_ge(*steps.of(f"{tag}_n{r}b", i))
                    dve.scalar_tensor_tensor(y, t, 1.5, y, ALU.add, ALU.mult).then_inc(*steps.step(f"{tag}_n{r}c"))
                    dve.wait_ge(*steps.of(f"{tag}_n{r}c", i))

            def centre(src, tag, i, steps):
                dve.tensor_reduce(lnt[:, 0, :], src[:], AX_X, ALU.add).then_inc(*steps.step(f"{tag}_sum"))
                dve.wait_ge(*steps.of(f"{tag}_sum", i))
                dve.tensor_scalar(lnt[:, 1, :], lnt[:, 0, :], 1.0 / D, None, ALU.mult).then_inc(*steps.step(f"{tag}_mean"))
                dve.wait_ge(*steps.of(f"{tag}_mean", i))
                dve.tensor_tensor(cen[:], src[:], over(lnt[:, 1, :]), ALU.subtract).then_inc(*steps.step(f"{tag}_cen"))
                dve.wait_ge(*steps.of(f"{tag}_cen", i))
                dve.tensor_tensor(sq[:], cen[:], cen[:], ALU.mult).then_inc(*steps.step(f"{tag}_sq"))
                dve.wait_ge(*steps.of(f"{tag}_sq", i))
                dve.tensor_reduce(lnt[:, 2, :], sq[:], AX_X, ALU.add).then_inc(*steps.step(f"{tag}_ssq"))
                dve.wait_ge(*steps.of(f"{tag}_ssq", i))
                dve.tensor_scalar(lnt[:, 3, :], lnt[:, 2, :], 1.0 / D, 1e-5, ALU.mult, ALU.add).then_inc(*steps.step(f"{tag}_var"))
                dve.wait_ge(*steps.of(f"{tag}_var", i))
                rsqrt(lnt[:, 3, :], lnt[:, 4, :], lnt[:, 5, :], tag, i, steps)

            def over(x, n=D):
                return x.unsqueeze(2).broadcast_to([TP, x.shape[1], n])

            def norm_tok(i):
                dve.wait_ge(*act_f.of("h0", i))
                centre(h0, "a", i, dve_f)
                dve.tensor_tensor(hn0[:], cen[:], over(lnt[:, 4, :]), ALU.mult).then_inc(*dve_f.step("hn0"))

            def parts0(i):
                dve.wait_ge(*pool_f.of("sx", i))
                dve.tensor_scalar(rr[:].bitcast(I32), rx[:].bitcast(I32), -0.5, RSQRT_MAGIC, ALU.mult, ALU.add)\
                   .then_inc(*dve_f.step("b_guess"))
                slots = lambda z, a, b, s: z[:, :, 0:12].rearrange("p h (s d) -> p h s d", d=2)[:, :, a:b:s, :]
                wide = lambda x, n: x.rearrange("p (h d) -> p h d", d=2).unsqueeze(2).broadcast_to([TP, P, n, 2])
                qn, kn = (qk0[:, s].rearrange("p t c -> p (t c)") for s in range(2))
                dve.wait_ge(*pool_f.of("negc", i))
                before(dve, pe_f, "zT7", i)
                dve.tensor_copy(slots(zq, 0, 3, 1), wide(qn, 3)).then_inc(*dve_f.step("q1"))
                dve.tensor_copy(slots(zk, 2, 5, 1), wide(kn, 3)).then_inc(*dve_f.step("k1"))
                dve.tensor_copy(zq[:, :, 12], negc[:]).then_inc(*dve_f.step("c1"))
                dve.wait_ge(*pool_f.of("rc1", i))
                dve.tensor_copy(slots(zq, 3, 6, 2), wide(res[:, 0, 0], 2)).then_inc(*dve_f.step("q2"))
                dve.tensor_copy(slots(zk, 1, 6, 4), wide(res[:, 0, 1], 2)).then_inc(*dve_f.step("k2"))
                dve.tensor_copy(zq[:, :, 13], resc[:, 0]).then_inc(*dve_f.step("c2"))
                dve.wait_ge(*pool_f.of("rc2", i))
                dve.tensor_copy(slots(zq, 4, 5, 1), wide(res[:, 1, 0], 1)).then_inc(*dve_f.step("q3"))
                dve.tensor_copy(slots(zk, 0, 1, 1), wide(res[:, 1, 1], 1)).then_inc(*dve_f.step("k3"))
                dve.tensor_copy(zq[:, :, 14], resc[:, 1]).then_inc(*dve_f.step("c3"))

            def heads_out(psum, r, y, nj, d, steps, names, i):
                v = psum[0:TP, :].rearrange("p (n y) -> p n y", y=32)
                dve.reciprocal(r[:, :, 0:nj], v[:, :, d:d + (d + 1) * (nj - 1) + 1:d + 1]).then_inc(*steps.step(names[0]))
                dve.wait_ge(*steps.of(names[0], i))
                dve.tensor_tensor(y[:].rearrange("p n (g j d) -> p (n g) j d", g=4, d=d),
                                  v[:, :, 0:nj * (d + 1)].rearrange("p n (j d) -> p n j d", d=d + 1)[:, :, :, 0:d],
                                  r[:, :, 0:nj].unsqueeze(3).broadcast_to([TP, 16, nj, d]), ALU.mult)\
                   .then_inc(*steps.step(names[1]))

            def attended(i):
                dve.wait_ge(*pe_f.of("y0T", i))
                heads_out(ps_x, rec, yn, 8, HD0, dve_f, ("rec0", "yn0"), i)
                dve.wait_ge(*pe_f.of("proj0", i))
                dve.tensor_tensor(h1[:].rearrange("p n c -> p (n c)"), ps_x[0:TP, 0:256], h0[:].rearrange("p n c -> p (n c)"),
                                  ALU.add).then_inc(*dve_f.step("h1"))
                dve.wait_ge(*dve_f.of("h1", i))
                centre(h1, "c", i, dve_f)
                dve.tensor_tensor(hn1[:], cen[:], over(lnt[:, 4, :]), ALU.mult).then_inc(*dve_f.step("hn1"))

            def gates(i):
                dve.wait_ge(*pe_f.of("gate", i))
                dve.tensor_copy(lg[:].rearrange("p n e -> p (n e)"), ps_x[0:TP, 0:4 * E]).then_inc(*dve_f.step("lg"))
                dve.wait_ge(*dve_f.of("lg", i))
                for n in range(4):
                    apart(dve, turns_dve)
                    dve.max(gm[:, n, :], lg[:, n, :]).then_inc(*dve_f.step(f"gm{n}"))
                for n in range(4):
                    dve.wait_ge(*dve_f.of(f"gm{n}", i))
                    apart(dve, turns_dve)
                    dve.max_index(gi[:, n, :], gm[:, n, :], lg[:, n, :]).then_inc(*dve_f.step(f"gi{n}"))
                dve.wait_ge(*dve_f.of("gi3", i))
                dve.tensor_copy(gif[:], gi[:, :, 0:TOPK_E]).then_inc(*dve_f.step("gif"))
                dve.tensor_tensor(gs[:, 0, :], gm[:, :, 1], gm[:, :, 0], ALU.subtract).then_inc(*dve_f.step("gd"))
                dve.wait_ge(*act_f.of("gexp", i))
                dve.tensor_scalar(gs[:, 2, :], gs[:, 1, :], 1.0, None, ALU.add).then_inc(*dve_f.step("g1p"))
                dve.wait_ge(*dve_f.of("g1p", i))
                dve.reciprocal(gs[:, 3, :], gs[:, 2, :]).then_inc(*dve_f.step("p1"))
                dve.wait_ge(*dve_f.of("p1", i))
                dve.tensor_tensor(gs[:, 4, :], gs[:, 1, :], gs[:, 3, :], ALU.mult).then_inc(*dve_f.step("p2"))
                for n in range(2):
                    dve.tensor_tensor(ge[:, n], expert_id[:], over(gif[:, :, n], E), ALU.is_equal).then_inc(*dve_f.step(f"e{n + 1}"))
                for n in range(2):
                    dve.wait_ge(*dve_f.of(f"e{n + 1}", i))
                    dve.tensor_tensor(ge[:, 2 + n], ge[:, n], over(gs[:, 3 + n, :], E), ALU.mult).then_inc(*dve_f.step(f"e{n + 1}p"))
                dve.wait_ge(*dve_f.of("e2p", i))
                dve.tensor_tensor(gg[:, 0], ge[:, 2], ge[:, 3], ALU.add).then_inc(*dve_f.step("G"))
                dve.wait_ge(*dve_f.of("G", i))
                dve.tensor_copy(g3[:, :, 0, :], gg[:, 0]).then_inc(*dve_f.step("G1"))
                dve.wait_ge(*dve_f.of("G1", i))
                dve.tensor_tensor(gg[:, 1], gg[:, 0], g3[:, :, 0, :], ALU.subtract).then_inc(*dve_f.step("Gr"))
                dve.wait_ge(*dve_f.of("Gr", i))
                dve.tensor_copy(g3[:, :, 1, :], gg[:, 1]).then_inc(*dve_f.step("G2"))
                dve.wait_ge(*dve_f.of("G2", i))
                dve.tensor_tensor(gg[:, 2], gg[:, 1], g3[:, :, 1, :], ALU.subtract).then_inc(*dve_f.step("Gr2"))
                dve.wait_ge(*dve_f.of("Gr2", i))
                dve.tensor_copy(g3[:, :, 2, :], gg[:, 2]).then_inc(*dve_f.step("G3"))

            def mixed(i):
                dve.wait_ge(*pe_f.of("moeT", i))
                v = ps_x[0:TP, :].rearrange("p (n a c) -> p n a c", n=4, a=2)
                dve.tensor_tensor(my[:], hn1[:], v[:, :, 0, :], ALU.add).then_inc(*dve_f.step("ma"))
                dve.wait_ge(*dve_f.of("ma", i))
                dve.tensor_tensor(my[:], my[:], v[:, :, 1, :], ALU.add).then_inc(*dve_f.step("mb"))
                dve.wait_ge(*dve_f.of("mb", i))
                centre(my[:], "d", i, dve_f)
                dve.tensor_tensor(mn[:], cen[:], over(lnt[:, 4, :]), ALU.mult).then_inc(*dve_f.step("dn"))
                dve.wait_ge(*dve_f.of("dn", i))
                gb = [ln_gb[:, n, :].unsqueeze(1).broadcast_to([TP, 4, D]) for n in range(2)]
                dve.tensor_tensor(mn[:], mn[:], gb[0], ALU.mult).then_inc(*dve_f.step("dg"))
                dve.wait_ge(*dve_f.of("dg", i))
                dve.tensor_tensor(mn[:], mn[:], gb[1], ALU.add).then_inc(*dve_f.step("db"))
                dve.wait_ge(*dve_f.of("db", i))
                before(dve, pool_k, "h2k", i)
                dve.tensor_tensor(h2[:], mn[:], h1[:], ALU.add).then_inc(*dve_f.step("h2"))
                dve.wait_ge(*dve_f.of("h2", i))
                centre(h2, "f", i, dve_f)
                dve.tensor_tensor(hn2[:], cen[:], over(lnt[:, 4, :]), ALU.mult).then_inc(*dve_f.step("hn2"))

            def norm_heads(i):
                dve.wait_ge(*act_f.of("qk1c", i))
                groups = lambda t: t.rearrange("p k n (h d) -> p (k n h) d", d=HD1)
                dve.tensor_reduce(n1[:, 0, :], groups(qk1[:]), AX_X, ALU.add).then_inc(*dve_f.step("g_sum"))
                dve.wait_ge(*dve_f.of("g_sum", i))
                dve.tensor_scalar(n1[:, 1, :], n1[:, 0, :], 1.0 / HD1, None, ALU.mult).then_inc(*dve_f.step("g_mean"))
                dve.wait_ge(*dve_f.of("g_mean", i))
                dve.tensor_tensor(groups(c1), groups(qk1[:]), over(n1[:, 1, :], HD1), ALU.subtract).then_inc(*dve_f.step("g_cen"))
                dve.wait_ge(*pool_f.of("g_sq", i))
                dve.tensor_reduce(n1[:, 2, :], groups(sq1), AX_X, ALU.add).then_inc(*dve_f.step("g_ssq"))
                dve.wait_ge(*dve_f.of("g_ssq", i))
                dve.tensor_scalar(n1[:, 3, :], n1[:, 2, :], 1.0 / HD1, 1e-5, ALU.mult, ALU.add).then_inc(*dve_f.step("g_var"))
                dve.wait_ge(*dve_f.of("g_var", i))
                rsqrt(n1[:, 3, :], n1[:, 4, :], n1[:, 5, :], "g", i, dve_f)

            def first_max(i, k):
                dve.wait_ge(*act_s.of(f"sc{k}b", i))
                for t in range(3):
                    apart(dve, turns_dve)
                    dve.max(m8[:, k, t, :], w_s[:, k, t, :]).then_inc(*dve_s.step(f"m{k}t{t}"))
                dve.wait_ge(*dve_s.of(f"m{k}t2", i))
                dve.tensor_scalar(nmax[:, k, :], m8[:, k, :, 0], -1.0, None, ALU.mult).then_inc(*dve_s.step(f"m{k}n"))

            def topk(i, k):
                if i is None:
                    return
                dve.wait_ge(*act_s.of(f"e{k}", i))
                for r in range(ROUNDS):
                    if r:
                        for t in range(3):
                            dve.wait_ge(*dve_t.of(f"k{k}r{r - 1}r{t}", i))
                            apart(dve, turns_dve)
                            dve.max(m8[:, k, t, :], w_s[:, k, t, :]).then_inc(*dve_t.step(f"k{k}r{r}m{t}"))
                    for t in range(3):
                        if r:
                            dve.wait_ge(*dve_t.of(f"k{k}r{r}m{t}", i))
                        apart(dve, turns_dve)
                        dve.match_replace(w_s[:, k, t, :], m8[:, k, t, :], w_s[:, k, t, :], NEG)\
                           .then_inc(*dve_t.step(f"k{k}r{r}r{t}"))
                for t in range(3):
                    dve.wait_ge(*dve_t.of(f"k{k}r{ROUNDS - 1}r{t}", i))
                    dve.scalar_tensor_tensor(e_s[:, k, t, :], w_s[:, k, t, :], NEG_TEST, e_s[:, k, t, :], ALU.is_lt, ALU.mult)\
                       .then_inc(*dve_t.step(f"k{k}r{ROUNDS}p{t}"))

            def back(i):
                dve.wait_ge(*pe_b.of("y1T", i))
                heads_out(ps_u, rec1, yn1, 2, HD1, dve_b, ("rec1", "yn1"), i)
                dve.wait_ge(*pe_b.of("proj1", i))
                dve.wait_ge(*pool_k.of("h2k", i))
                dve.tensor_tensor(h3[:].rearrange("p n c -> p (n c)"), ps_u[0:TP, 0:256], h2k[:].rearrange("p n c -> p (n c)"),
                                  ALU.add).then_inc(*dve_b.step("h3"))
                dve.wait_ge(*dve_b.of("h3", i))
                centre(h3, "r", i, dve_b)
                dve.tensor_tensor(hn3[:], cen[:], over(lnt[:, 4, :]), ALU.mult).then_inc(*dve_b.step("hn3"))
                dve.wait_ge(*dve_b.of("hn3", i))
                if not (isinstance(i, int) and i == 0):
                    dve.wait_ge(h_stored, 16 * i)
                dve.tensor_tensor(hsum[:], h3[:], hn3[:], ALU.add).then_inc(*dve_b.step("hsum"))

            def body(i, prev):
                topk(prev, 0)
                norm_tok(i)
                topk(prev, 1)
                parts0(i)
                topk(prev, 2)
                topk(prev, 3)
                attended(i)
                gates(i)
                topk(prev, 4)
                topk(prev, 5)
                mixed(i)
                norm_heads(i)
                topk(prev, 6)
                topk(prev, 7)
                for k in range(CHUNKS):
                    first_max(i, k)
                if prev is not None:
                    back(prev)

            body(0, None)
            if PAIRS > 1:
                body(1, 0)
            if PAIRS > 2:
                with dve.Fori(2, PAIRS) as i:
                    body(i, i - 1)
            for k in range(CHUNKS):
                topk(PAIRS - 1, k)
            back(PAIRS - 1)

            count = [0]

            def tail(ins):
                count[0] += 1
                ins.then_inc(tail_dve, 1)
                dve.wait_ge(tail_dve, count[0])

            dve.wait_ge(sel_loaded, 16)
            tail(dve.tensor_copy(tail_x, tail_w))
            for _ in range(CAP // 8):
                tail(dve.max(tail_8, tail_x))
                tail(dve.match_replace(tail_x, tail_8, tail_x, NEG))
            tail(dve.max(tail_8, tail_x))
            edge = tail_8[:, CAP % 8 - 1:CAP % 8]
            tail(dve.tensor_scalar(tail_gt, tail_x, edge, None, ALU.is_gt))
            tail(dve.tensor_scalar(tail_eq, tail_x, edge, None, ALU.is_equal))
            tail(dve.tensor_reduce(tail_n[:, 0:1], tail_gt, AX_X, ALU.add))
            tail(dve.tensor_scalar(tail_n[:, 1:2], tail_n[:, 0:1], -1.0, float(CAP % 8), ALU.mult, ALU.add))
            tail(dve.tensor_copy(tail_c[:, 0, :], tail_eq))
            shift, a = 1, 0
            while shift < T:
                tail(dve.tensor_copy(tail_c[:, 1 - a, 0:shift], tail_c[:, a, 0:shift]))
                tail(dve.tensor_tensor(tail_c[:, 1 - a, shift:T], tail_c[:, a, shift:T], tail_c[:, a, 0:T - shift], ALU.add))
                shift, a = 2 * shift, 1 - a
            tail(dve.scalar_tensor_tensor(tail_eq, tail_c[:, a, :], tail_n[:, 1:2], tail_eq, ALU.is_le, ALU.mult))
            tail(dve.tensor_tensor(tail_gt, tail_gt, tail_eq, ALU.add))
            tail(dve.scalar_tensor_tensor(tail_gt, tail_x, NEG_TEST, tail_gt, ALU.is_lt, ALU.add))
            tail(dve.tensor_tensor(tail_s, tail_gt, tail_w, ALU.mult))
            assert count[0] == TAIL_SELECTED, count[0]
            dve.wait_ge(tail_pe, 1)
            tail(dve.tensor_copy(wt.rearrange("p t b -> p (t b)"), ps_x[0:TP, 0:2 * B]))
            assert count[0] == TAIL_FIRST
            for n in range(PIECES):
                dve.wait_ge(piece_loaded[n % 2], 32 * (n // 2) + 32)
                for m in range(4):
                    w = wt[:, m // 2, :].rearrange("p (i u) -> p i u", u=2)[:, TAIL * n:TAIL * n + TAIL, m % 2]
                    y = fin_y[n % 2][:, :, m, :]
                    tail(dve.tensor_tensor(y, y, over(w), ALU.mult))
                    tail(dve.tensor_tensor(y, y, fin_h[n % 2][:, :, m, :], ALU.add))


POOL_CONSTANTS = 6
DVE_CONSTANTS = 36
TAIL_SELECTED = 1 + 2 * (CAP // 8) + 1 + 5 + 2 * 8 + 4
TAIL_FIRST = TAIL_SELECTED + 1

NAMES = ["x", "L0_tok_W_in", "L0_tok_b_in", "L0_tok_W_out", "L0_tok_b_out", "L0_tok_core_diag", "L0_tok_conv_filter",
         "L0_attn_w_qkv", "L0_attn_w_proj", "L0_attn_qn_w", "L0_attn_kn_w", "L0_ffn_gate_w", "L0_ffn_gate_b", "L0_ffn_w1",
         "L0_ffn_b1", "L0_ffn_w2", "L0_ffn_b2", "L0_ffn_gamma", "L0_ffn_beta", "L1_attn_qkv_w", "L1_attn_qkv_b",
         "L1_attn_q_gamma", "L1_attn_q_beta", "L1_attn_k_gamma", "L1_attn_k_beta", "L1_attn_proj_w", "L1_attn_proj_b",
         "L1_ffn_wr", "L1_ffn_br", "L1_ffn_w1", "L1_ffn_b1", "L1_ffn_w2", "L1_ffn_b2"]


def kernel(**inputs):
    import numpy as np
    import concourse.bacc as bacc
    from concourse.bass_utils import run_bass_kernel_spmd

    nc = bacc.Bacc("TRN2", target_bir_lowering=False, num_devices=1)
    arrays, dram = {}, {}
    for name in NAMES:
        a = np.ascontiguousarray(inputs[name])
        arrays["in_" + name] = a
        dram[name] = nc.dram_tensor("in_" + name, a.shape, mybir.dt.from_np(a.dtype), kind="ExternalInput").ap()
    out = nc.dram_tensor("out", (2 * PAIRS, T, D), F32, kind="ExternalOutput").ap()
    route = nc.dram_tensor("route", (PAIRS, 2 * T), F32, kind="Internal").ap()
    h3, ffy = (nc.dram_tensor(n, (PAIRS, TP, 4 * D), F32, kind="Internal").ap() for n in ("h3_rows", "ff_rows"))
    audio_tower(nc, dram, out, route, h3, ffy)
    return run_bass_kernel_spmd(nc, [arrays], core_ids=[0]).results[0]["out"]
```

```python
from contextlib import ExitStack

import concourse.bass as bass
from concourse import mybir

F32 = mybir.dt.float32
BF16 = mybir.dt.bfloat16
I32 = mybir.dt.int32
U32 = mybir.dt.uint32
ALU = mybir.AluOpType
ACT = mybir.ActivationFunctionType
AX_X = mybir.AxisListType.X

P = 128
PAIRS = 32
T_IN, D = 375, 64
XT = T_IN // 3
TAPS, PAD = 15, 7
T = 188
TP = T // 2
S1 = T - P
UNIT = T + S1
H0, HD0 = 32, 2
H1, HD1 = 8, 8
TERMS = 6
ROWS0 = TERMS * HD0 + 3
E, TOPK_E, F_E = 16, 2, 128
KEEP = int(T * 0.3)
ROUNDS = KEEP // 8
CAP = T // 2 - 1
NEG = -3.0e38
NEG_TEST = -1.0e38
MASKED = -1.0e30
RSQRT_MAGIC = 1597463007.0
SHIFT_ROOM = 80.0
CHUNKS = 8


class Steps:

    def __init__(self, sem, names):
        self.sem, self.names, self.next = sem, names, 0
        self.index = {n: k for k, n in enumerate(names)}
        assert len(self.index) == len(names)

    def step(self, name):
        assert self.names[self.next % len(self.names)] == name, (name, self.names[self.next % len(self.names)])
        self.next += 1
        return self.sem, 1

    def of(self, name, i):
        return self.sem, i * len(self.names) + (self.index[name] + 1)


def newton(x):
    return [f"{x}_guess"] + [f"{x}_n{r}{c}" for r in range(3) for c in "abc"]


def ln_steps(x):
    return [f"{x}_sum", f"{x}_mean", f"{x}_cen", f"{x}_sq", f"{x}_ssq", f"{x}_var"] + newton(x)


PE_FIRST = ["xT", "tok0", "tok1", "tok2", "tok3", "conv", "hn0T", "qk0", "v0"]
ACT_FIRST = ["x0", "x1", "x2", "x2s", "x3", "x4", "h0", "hn0Tc", "qk0c", "qk0s", "v0c"]
DVE_FIRST = ln_steps("a") + ["hn0"] + newton("b") + ["q1", "k1", "c1", "q2", "k2", "c2", "q3", "k3", "c3"]
POOL_FIRST = ["ss", "sx", "qr", "qw", "qkp", "self", "negc", "rq1", "rk1", "rc1", "rq2", "rk2", "rc2"]
PE_FRONT = ([f"zT{f}" for f in range(8)]
            + [x for n in range(17) for x in ([f"sc{n}"] if n < 16 else []) + ([f"pv{n - 1}"] if n else [])]
            + ["y0T", "yn0T", "proj0"]
            + ["hn1T", "gate", "gT"]
            + [x for e in range(E + 1) for x in ([f"z{e}"] if e < E else []) + ([f"o{e - 1}"] if e else [])]
            + ["moeT", "hn2T", "qk1"] + [f"kqT{f}" for f in range(5)])
ACT_FRONT = ([f"zTc{f}" for f in range(8)] + [f"ex{n}" for n in range(16)] + ["y0c", "yn0Tc"]
             + ["hn1Tc", "gexp", "gTc"] + [x for e in range(E) for x in (f"relu{e}", f"gc{e}")]
             + ["moec", "hn2Tc", "qk1c"] + [f"kqTc{f}" for f in range(5)])
DVE_FRONT = (["rec0", "yn0", "h1"] + ln_steps("c") + ["hn1"]
             + ["lg"] + [f"gm{t}" for t in range(4)] + [f"gi{t}" for t in range(4)]
             + ["gif", "gd", "g1p", "p1", "p2", "e1", "e2", "e1p", "e2p", "G", "G1", "Gr", "G2", "Gr2", "G3"]
             + ["ma", "mb"] + ln_steps("d") + ["dn", "dg", "db", "h2"] + ln_steps("f") + ["hn2"]
             + ["g_sum", "g_mean", "g_cen", "g_ssq", "g_var"] + newton("g"))
POOL_FRONT = [f"hp{e}" for e in range(E)] + ["g_sq", "g_norm", "g_gam", "gq0", "gq1", "gk0", "gk1"]
PE_SCORE = [f"s{k}" for k in range(CHUNKS)] + ["v1"]
ACT_SCORE = [f"sc{k}{x}" for k in range(CHUNKS) for x in "ab"] + [f"e{k}" for k in range(CHUNKS)] + ["v1c"]
DVE_SCORE = [f"m{k}{x}" for k in range(CHUNKS) for x in ("t0", "t1", "t2", "n")]
DVE_TOPK = [f"k{k}r{r}{c}{t}" for k in range(CHUNKS)
            for r, c in [(0, "r")] + [(r, c) for r in range(1, ROUNDS) for c in "mr"] + [(ROUNDS, "p")]
            for t in range(3)]
PE_BACK = ([f"{x}{k}" for k in range(CHUNKS) for x in ("pt0_", "pt1_", "pv")]
           + ["y1T", "yn1T", "proj1", "h3T", "route", "ffz0", "ffz1", "ffo", "ffT"])
ACT_BACK = ([f"{x}{k}" for k in range(CHUNKS) for x in ("pc0_", "pc1_")]
            + ["y1c", "yn1Tc", "h3Tc", "routec", "gelu0", "gelu1", "ffoc", "ffTc"])
DVE_BACK = ["rec1", "yn1", "h3"] + ln_steps("r") + ["hn3", "hsum"]
POOL_KEEP = ["h2k"]

FIRST_XT, FIRST_DENSE, FIRST_TOK3, FIRST_CONV, FIRST_HN0T, FIRST_QK0, FIRST_V0 = 0, (1, 2, 3), 4, 5, 12, 13, 14
BACK_Y1T, BACK_YN1T, BACK_PROJ1, BACK_H3T, BACK_ROUTE, BACK_FFZ1, BACK_FFO, BACK_FFT = 0, 2, 3, 10, 11, 12, 13, 15


def audio_tower(nc, dram, out, route_dram, h_dram, y_dram):
    with ExitStack() as ctx:
        def sb(name, shape, dt=F32):
            return ctx.enter_context(nc.sbuf_tensor(name, shape, dt))

        def ps(name, shape, dt=F32):
            return ctx.enter_context(nc.psum_tensor(name, shape, dt))

        def sem(name):
            return ctx.enter_context(nc.semaphore(name))

        ident = sb("ident", [P, P])
        ident_b = sb("ident_b", [P, P], BF16)
        ones = sb("ones", [1, P])
        tok_w = sb("tok_w", [P, 4, P])
        tok_b = sb("tok_b", [P, 3])
        core = sb("core", [P, 1])
        core_abs = sb("core_abs", [P, 1])
        tok_brow = sb("tok_brow", [1, 2, D])
        taps = sb("taps", [XT, TAPS])
        toeplitz = sb("toeplitz", [XT, 3, T])
        w_qkv0 = sb("w_qkv0", [P, 3, 2, D])
        w_qkv1 = sb("w_qkv1", [P, 3, 2, D])
        w_proj = sb("w_proj", [P, 2, 2, D])
        rms_raw = sb("rms_raw", [TP, 2, 2])
        rms_w = sb("rms_w", [TP, 2, P])
        wprod = sb("wprod", [TP, 2])
        room = sb("room", [TP, 1])
        causal = sb("causal", [P, 2, UNIT], BF16)
        gate_w = sb("gate_w", [D, E])
        gate_b = sb("gate_b", [1, E])
        w1e = sb("w1e", [D, E, F_E])
        w2e = sb("w2e", [F_E, E, D])
        b1e = sb("b1e", [F_E, E])
        b2raw = sb("b2raw", [3 * E, D])
        b2res = sb("b2res", [3 * E, 2, D])
        b2e = sb("b2e", [3 * E, 3, D], BF16)
        pick = sb("pick", [3 * E, E, P], BF16)
        expert_id = sb("expert_id", [TP, 4, E])
        ln_gb = sb("ln_gb", [TP, 2, D])
        brow1 = sb("brow1", [1, 3, 2, D])
        gb_raw = sb("gb_raw", [TP, 4, HD1])
        gam1 = sb("gam1", [TP, 2, P])
        bet1 = sb("bet1", [TP, 2, P])
        projb1 = sb("projb1", [1, 2, D])
        wr = sb("wr", [D, 1])
        br = sb("br", [1, 1])
        fw1 = sb("fw1", [D, 2, P])
        fb1 = sb("fb1", [P, 2])
        fw2 = sb("fw2", [P, 2, D])
        fb2 = sb("fb2", [P, 1])

        x_in = sb("x_in", [XT, 3, 2, D])
        gh = sb("gh", [P, 2, 2 * T])
        x0, x1 = gh[:, 0, 0:T_IN], gh[:, 1, 0:T_IN]
        x2 = sb("x2", [P, T_IN])
        x2s, x3 = x0, x1
        x4 = sb("x4", [XT, 3, P])
        h0 = sb("h0", [TP, 4, D])
        h1 = sb("h1", [TP, 4, D])
        h2 = sb("h2", [TP, 4, D])
        h2k = sb("h2k", [TP, 4, D])
        h3 = sb("h3", [TP, 4, D])
        hn3 = sb("hn3", [TP, 4, D])
        hsum = sb("hsum", [TP, 4, D])
        cen = sb("cen", [TP, 4, D])
        sq = sb("sq", [TP, 4, D])
        lnt = sb("lnt", [TP, 6, 4])
        hn0 = sb("hn0", [TP, 4, D])
        hn1 = sb("hn1", [TP, 4, D])
        hn2 = sb("hn2", [TP, 4, D])
        hn0T = sb("hn0T", [P, T])
        hn1T = sb("hn1T", [D, 2 * T])
        hn2T = sb("hn2T", [P, T])
        qk0 = sb("qk0", [TP, 2, 2, P])
        qk0s = sb("qk0s", [TP, 2, 2, P])
        rx = sb("rx", [TP, 256])
        rr = sb("rr", [TP, 256])
        rt = sb("rt", [TP, 256])
        selfp = rt
        selfs = sb("selfs", [TP, P])
        negc = sb("negc", [TP, P])
        hrg = sb("hrg", [P, 2, 2, 2 * T])
        hr, hg = hrg[:, 0], hrg[:, 1]
        resc = sb("resc", [TP, 2, P])
        zq = sb("zq", [TP, P, 32], BF16)
        zk = sb("zk", [TP, P, 32], BF16)
        qT0 = sb("qT0", [P, 2, 8, T], BF16)
        kT0 = sb("kT0", [P, 2, 8, T], BF16)
        e0 = sb("e0", [P, 2, 4, UNIT])
        res = e0[0:TP].rearrange("p a b c -> p (a b c)")[:, 0:1024].rearrange("p (r s c) -> p r s c", r=2, s=2)
        vp0 = [sb(f"vp0{m}", [P, 2, 1048]) for m in range(2)]
        y0 = sb("y0", [P, 2 * T])
        rec = sb("rec", [TP, 16, 8])
        yn = sb("yn", [TP, 4, D])
        ynT = sb("ynT", [P, T])
        lg = sb("lg", [TP, 4, E])
        gm = sb("gm", [TP, 4, 8])
        gi = sb("gi", [TP, 4, 8], U32)
        gif = sb("gif", [TP, 4, 2])
        gs = sb("gs", [TP, 5, 4])
        ge = sb("ge", [TP, 4, 4, E])
        gg = sb("gg", [TP, 3, 4, E])
        g3 = sb("g3", [TP, 4, 3, E], BF16)
        gT = sb("gT", [3 * E, 2 * T], BF16)
        hp = sb("hp", [P, 2, 2 * T])
        moe = y0
        my = mn = yn

        qk1 = sb("qk1", [TP, 2, 4, D])
        c1, sq1 = (hrg[0:TP].rearrange("p a b c -> p (a b c)")[:, 512 * n:512 * n + 512]
                   .rearrange("p (k n c) -> p k n c", k=2, n=4) for n in range(2))
        n1 = sb("n1", [TP, 6, 64])
        zq1 = sb("zq1", [TP, 4, 2, D])
        zk1 = sb("zk1", [TP, 4, 8 * D + 64])
        qT1 = sb("qT1", [P, 2, T])
        kT1 = sb("kT1", [P, 2, 4, T])
        w_s = sb("w_s", [P, CHUNKS, 3, T])
        e_s = sb("e_s", [P, CHUNKS, 3, T])
        m8 = sb("m8", [P, CHUNKS, 3, 8])
        nmax = sb("nmax", [P, CHUNKS, 3])
        vp1 = [sb(f"vp1{m}", [P, 2, 274]) for m in range(2)]
        pt = [sb("pt0", [P, T + D + P]), sb("pt1", [S1, T + D + P])]
        y1 = y0
        rec1 = sb("rec1", [TP, 16, 2])
        yn1 = yn
        yn1T = sb("yn1T", [P, T])
        h3T = sb("h3T", [D, 2 * T])
        rw = sb("rw", [1, 2 * T])
        ffo = sb("ffo", [P, T])
        ffy = sb("ffy", [TP, 4, D])

        def part(tile, at, rows, shape):
            n = 1
            for k in shape:
                n *= k
            flat = tile[0:rows].rearrange("p k a t -> p (k a t)")[:, at:at + n]
            if len(shape) == 1:
                return flat
            names = "abcd"[:len(shape)]
            return flat.rearrange(f"p ({' '.join(names)}) -> p {' '.join(names)}", **dict(zip(names[1:], shape[1:])))

        tap_mask = part(w_s, 0, XT, [2, 3, T])
        nat0 = part(w_s, 6 * T, 96, [2, 2, D])
        nat1 = part(w_s, 6 * T + 256, 96, [2, 2, D])
        natp = part(w_s, 6 * T + 512, D, [2, 2, D])

        B = 2 * PAIRS
        tail_w, tail_x, tail_gt, tail_eq, tail_s = (part(w_s, n * T, B, [T]) for n in range(5))
        tail_c = part(w_s, 5 * T, B, [2, T])
        tail_8 = part(w_s, 7 * T, B, [8])
        tail_n = part(w_s, 7 * T + 8, B, [2])
        wt = part(w_s, 8 * T, TP, [2, B])
        TAIL = min(PAIRS, 8)
        PIECES = PAIRS // TAIL
        fin_y = [part(e_s, 2048 * n, TP, [TAIL, 4, D]) for n in range(2)]
        fin_h = [part(w_s, 12 * T, TP, [TAIL, 4, D]),
                 zq[:].rearrange("p h r -> p (h r)").bitcast(F32)[:, 0:TAIL * 256].rearrange("p (i n c) -> p i n c", i=TAIL, n=4)]

        ps_s = [ps(f"ps_s{n}", [P, 2, 512]) for n in range(2)]
        ps_x = ps("ps_x", [P, 512])
        ps_y = ps("ps_y", [P, 512])
        ps_u = ps("ps_u", [P, 512])
        ps_v = ps("ps_v", [P, 512])

        def bank(n):
            return ps_s[n // 2][:, n % 2, :]

        loaded = sem("weights_loaded")
        zeroed = sem("weight_tiles_zeroed")
        const_pool = sem("pool_constants")
        const_dve = sem("vector_constants")
        const_pe = sem("weights_transposed")
        const_act = sem("weights_copied")
        tap_done = sem("tap_added")
        tap_made = sem("tap_mask_made")
        x_loaded = sem("x_loaded")
        routed = sem("router_rows_stored")
        h_stored = sem("h_stored")
        y_stored = sem("y_stored")
        piece_loaded = [sem("even_last_pieces_loaded"), sem("odd_last_pieces_loaded")]
        sel_loaded = sem("router_rows_loaded")
        tail_dve = sem("tail_vector")
        tail_pe = sem("tail_transposed")
        stored = sem("output_stored")
        pe_a = Steps(sem("pe_first"), PE_FIRST)
        act_a = Steps(sem("act_first"), ACT_FIRST)
        dve_a = Steps(sem("vector_first"), DVE_FIRST)
        pool_a = Steps(sem("pool_first"), POOL_FIRST)
        pe_f = Steps(sem("pe_front"), PE_FRONT)
        act_f = Steps(sem("act_front"), ACT_FRONT)
        dve_f = Steps(sem("vector_front"), DVE_FRONT)
        pool_f = Steps(sem("pool_front"), POOL_FRONT)
        pe_s = Steps(sem("pe_scores"), PE_SCORE)
        act_s = Steps(sem("act_scores"), ACT_SCORE)
        dve_s = Steps(sem("vector_first_max"), DVE_SCORE)
        dve_t = Steps(sem("vector_topk"), DVE_TOPK)
        pe_b = Steps(sem("pe_back"), PE_BACK)
        act_b = Steps(sem("act_back"), ACT_BACK)
        dve_b = Steps(sem("vector_back"), DVE_BACK)
        pool_k = Steps(sem("pool_kept_h2"), POOL_KEEP)

        def before(eng, steps, name, i):
            if isinstance(i, int) and i == 0:
                return
            eng.wait_ge(*steps.of(name, i - 1))

        turns_pe, turns_dve, turns_pool = sem("pe_turns"), sem("vector_turns"), sem("pool_turns")

        def apart(eng, turns):
            eng.sem_inc(turns, 1)

        def v_view(t, u, step, parts, d0, d1):
            nj = {131: 8, 137: 2}[step]
            return (t[0:parts, u, 0:nj * step].rearrange("p (j x) -> p j x", x=step)[:, :, 0:P]
                    .rearrange("p j (g y) -> p j g y", y=32)[:, :, :, d0:d1])

        block = ctx.enter_context(nc.Block())

        weight_loads = []

        @block.sync
        def _(sp):
            sp.wait_ge(zeroed, 1)

            def load(dst, src):
                sp.dma_start(dst, src).then_inc(loaded, 16)
                weight_loads.append(1)

            with nc.allow_non_contiguous_dma("weights, once"):
                for u in range(2):
                    half = slice(D * u, D * u + D)
                    load(tok_w[half, 0:2, half], dram["L0_tok_W_in"].rearrange("n c m -> c n m"))
                    load(tok_w[half, 2, half], dram["L0_tok_W_out"][1])
                    load(tok_w[half, 3, half], dram["L0_tok_W_out"][0])
                    load(tok_b[half, 0:2], dram["L0_tok_b_in"].rearrange("n c -> c n"))
                    load(tok_b[half, 2:3], dram["L0_tok_b_out"][1:2].rearrange("n c -> c n"))
                    load(core[half, :], dram["L0_tok_core_diag"].rearrange("(c a) -> c a", a=1))
                    load(tok_brow[:, u, :], dram["L0_tok_b_out"][0:1])
                    load(nat0[:, :, u, :], dram["L0_attn_w_qkv"].rearrange("(t r) c -> r t c", r=96))
                    load(nat1[:, :, u, :], dram["L1_attn_qkv_w"].rearrange("(t r) c -> r t c", r=96))
                    for a in range(2):
                        for b in range(2):
                            for gq in range(2):
                                load(natp[:, 0, u, :].rearrange("r (c jp gh d) -> r c gh jp d", c=4, gh=2, d=2)[:, 2 * b + a, gq],
                                     dram["L0_attn_w_proj"].rearrange("r (jp a gh b d) -> r a gh b jp d", a=2, gh=2, b=2, d=2)[:, a, gq, b])
                    for g in range(4):
                        load(natp[:, 1, u, :].rearrange("r (g j d) -> r g j d", g=4, j=2)[:, g],
                             dram["L1_attn_proj_w"].rearrange("r (j g d) -> r g j d", g=4, j=2)[:, g])
                    load(brow1[:, :, u, :], dram["L1_attn_qkv_b"].rearrange("(a k c) -> a k c", a=1, k=3))
                    load(projb1[:, u, :], dram["L1_attn_proj_b"].rearrange("(a c) -> a c", a=1))
                    load(fb2[half, :], dram["L1_ffn_b2"].rearrange("(c a) -> c a", a=1))
                load(gate_w[:], dram["L0_ffn_gate_w"])
                load(gate_b[:], dram["L0_ffn_gate_b"].rearrange("(a e) -> a e", a=1))
                load(w1e[:], dram["L0_ffn_w1"].rearrange("e c f -> c e f"))
                load(wr[:], dram["L1_ffn_wr"])
                load(br[:], dram["L1_ffn_br"].rearrange("(a c) -> a c", a=1))
                load(fw1[:], dram["L1_ffn_w1"].rearrange("c (h f) -> c h f", h=2))
                for s in range(3):
                    load(b2raw[E * s:E * s + E, :], dram["L0_ffn_b2"])
                load(w2e[:], dram["L0_ffn_w2"].rearrange("e f c -> f e c"))
                load(b1e[:], dram["L0_ffn_b1"].rearrange("e f -> f e"))
                load(fw2[:], dram["L1_ffn_w2"].rearrange("(h f) c -> f h c", h=2))
                load(fb1[:], dram["L1_ffn_b1"].rearrange("(h f) -> f h", h=2))
                load(taps[:], dram["L0_tok_conv_filter"].partition_broadcast(XT))
                load(rms_raw[:, 0, :], dram["L0_attn_qn_w"].partition_broadcast(TP))
                load(rms_raw[:, 1, :], dram["L0_attn_kn_w"].partition_broadcast(TP))
                load(ln_gb[:, 0, :], dram["L0_ffn_gamma"].partition_broadcast(TP))
                load(ln_gb[:, 1, :], dram["L0_ffn_beta"].partition_broadcast(TP))
                for n, name in enumerate(("q_gamma", "k_gamma", "q_beta", "k_beta")):
                    load(gb_raw[:, n, :], dram["L1_attn_" + name].partition_broadcast(TP))

            x_pairs = dram["x"].rearrange("(i u) (j p) c -> i u p j c", u=2, p=XT)

            def load_x(i):
                before(sp, pe_a, "xT", i)
                for u in range(2):
                    sp.dma_start(x_in[:, :, u, :], x_pairs[bass.ds(i, 1), u].rearrange("a p j c -> p (a j) c"))\
                      .then_inc(x_loaded, 16)

            def store_route(i):
                sp.wait_ge(*act_b.of("routec", i))
                sp.dma_start(route_dram[bass.ds(i, 1)], rw[:]).then_inc(routed, 16)
                sp.wait_ge(*dve_b.of("hsum", i))
                sp.dma_start(h_dram[bass.ds(i, 1)].rearrange("a p c -> p (a c)"), hsum[:].rearrange("p n c -> p (n c)"))\
                  .then_inc(h_stored, 16)
                sp.wait_ge(*act_b.of("ffTc", i))
                sp.dma_start(y_dram[bass.ds(i, 1)].rearrange("a p c -> p (a c)"), ffy[:].rearrange("p n c -> p (n c)"))\
                  .then_inc(y_stored, 16)

            for i in range(3):
                load_x(i)
            with sp.Fori(3, PAIRS) as i:
                load_x(i)
                store_route(i - 3)
            for i in range(PAIRS - 3, PAIRS):
                store_route(i)
            sp.wait_ge(routed, 16 * PAIRS)
            sp.wait_ge(h_stored, 16 * PAIRS)
            sp.wait_ge(y_stored, 16 * PAIRS)
            sp.wait_ge(*dve_t.of(f"k{CHUNKS - 1}r{ROUNDS}p2", PAIRS - 1))
            sp.wait_ge(*pe_b.of(f"pt1_{CHUNKS - 1}", PAIRS - 1))
            sp.dma_start(tail_w, route_dram.rearrange("i (u t) -> (i u) t", u=2)).then_inc(sel_loaded, 16)

            def load_piece(n):
                if n >= 2:
                    sp.wait_ge(stored, 64 * (n - 1))
                    sp.wait_ge(tail_dve, TAIL_FIRST + 8 * (n - 1))
                rows = slice(TAIL * n, TAIL * n + TAIL)
                sp.dma_start(fin_y[n % 2], y_dram[rows].rearrange("i p (n c) -> p i n c", n=4)).then_inc(piece_loaded[n % 2], 16)
                sp.dma_start(fin_h[n % 2], h_dram[rows].rearrange("i p (n c) -> p i n c", n=4)).then_inc(piece_loaded[n % 2], 16)

            out_v = out.rearrange("(i u) (t p) c -> t u p i c", u=2, p=TP)
            load_piece(0)
            if PIECES > 1:
                load_piece(1)
            for n in range(PIECES):
                sp.wait_ge(tail_dve, TAIL_FIRST + 8 * n + 8)
                for m in range(4):
                    sp.dma_start(out_v[m // 2, m % 2, :, TAIL * n:TAIL * n + TAIL, :], fin_y[n % 2][:, :, m, :]).then_inc(stored, 16)
                if n + 2 < PIECES:
                    load_piece(n + 2)
            sp.wait_ge(stored, 64 * PIECES)

        n_loads = 16 * len(weight_loads)

        @block.tensor
        def _(pe):
            pe.wait_ge(loaded, n_loads)
            pe.wait_ge(const_pool, 1)
            for n, nat in enumerate((nat0, nat1)):
                for t in range(2):
                    pe.transpose(ps_x[:, 192 * n + 96 * t:192 * n + 96 * t + 96],
                                 nat[:, t].rearrange("r u c -> r (u c)"), ident[0:96, 0:96])
            for n in range(2):
                last = pe.transpose(ps_x[:, 384 + D * n:384 + D * n + D],
                                    natp[:, n].rearrange("r u c -> r (u c)"), ident[0:D, 0:D])
            last.then_inc(const_pe, 1)
            pe.wait_ge(const_pool, POOL_CONSTANTS)
            pe.wait_ge(const_dve, DVE_CONSTANTS)
            pe.wait_ge(const_act, 1)

            def first_xT(i):
                pe.wait_ge(x_loaded, 32 * i + 32)
                for j in range(3):
                    last = pe.transpose(ps_x[:, XT * j:XT * j + XT], x_in[:, j].rearrange("p u c -> p (u c)"),
                                        ident[0:XT, 0:XT])
                last.then_inc(*pe_a.step("xT"))

            def first_dense(i, n):
                name, rhs = (("x0", x0), ("x1", x1), ("x2s", x2s))[n]
                pe.wait_ge(*act_a.of(name, i))
                pe.matmul(ps_x[:, 0:T_IN], tok_w[:, n, :], rhs, start=True, stop=True).then_inc(*pe_a.step(f"tok{n}"))

            def first_tok3(i):
                pe.wait_ge(*act_a.of("x3", i))
                for j in range(3):
                    o = ps_x[0:XT, P * j:P * j + P]
                    pe.matmul(o, x3[:, XT * j:XT * j + XT], tok_w[:, 3, :], start=True, stop=False)
                    last = pe.matmul(o, ones[:, 0:XT], tok_brow[:].rearrange("a u c -> a (u c)"), start=False, stop=True)
                last.then_inc(*pe_a.step("tok3"))

            def first_conv(i):
                pe.wait_ge(*act_a.of("x4", i))
                for t in range(2):
                    for j in range(2):
                        last = pe.matmul(ps_x[0:TP, P * t:P * t + P], toeplitz[:, t + j, TP * t:TP * t + TP],
                                         x4[:, t + j, :], start=(j == 0), stop=(j == 1))
                last.then_inc(*pe_a.step("conv"))

            def first_hn0T(i):
                pe.wait_ge(*dve_a.of("hn0", i))
                to_features(hn0, ps_x).then_inc(*pe_a.step("hn0T"))

            def first_qk0(i):
                pe.wait_ge(*act_a.of("hn0Tc", i))
                for t in range(2):
                    last = pe.matmul(ps_x[0:TP, 256 * t:256 * t + 256], hn0T[:, TP * t:TP * t + TP],
                                     w_qkv0[:, 0:2].rearrange("p k u c -> p (k u c)"), start=True, stop=True)
                last.then_inc(*pe_a.step("qk0"))

            def first_v0(i):
                pe.wait_ge(*act_a.of("qk0s", i))
                w_v = w_qkv0[:, 2].rearrange("p u c -> p (u c)")
                pe.matmul(ps_x[:, 0:P], hn0T[:, 0:P], w_v, start=True, stop=True)
                pe.matmul(ps_x[0:S1, P:2 * P], hn0T[:, P:T], w_v, start=True, stop=True)\
                  .then_inc(*pe_a.step("v0"))

            def first(i, e):
                if i is None:
                    return
                if e == FIRST_XT:
                    first_xT(i)
                elif e in FIRST_DENSE:
                    first_dense(i, FIRST_DENSE.index(e))
                elif e == FIRST_TOK3:
                    first_tok3(i)
                elif e == FIRST_CONV:
                    first_conv(i)
                elif e == FIRST_HN0T:
                    first_hn0T(i)
                elif e == FIRST_QK0:
                    first_qk0(i)
                elif e == FIRST_V0:
                    first_v0(i)

            def attention0(i, done):
                before(pe, act_s, f"sc{CHUNKS - 1}b", i)
                pe.wait_ge(*dve_a.of("c3", i))
                for f in range(8):
                    side, u, half = f // 4, f // 2 % 2, f % 2
                    if f >= 4:
                        pe.wait_ge(*act_f.of(f"zTc{f - 4}", i))
                    o = bank(f % 4).bitcast(BF16)
                    z = (zq, zk)[side][:].rearrange("p (n j y) r -> p n j (y r)", n=4, y=4)
                    for j in range(4):
                        for t in range(2):
                            c = T * j + TP * t
                            last = pe.transpose(o[:, c:c + TP], z[:, 2 * t + u, 4 * half + j, :], ident_b[0:TP, 0:TP])
                    last.then_inc(*pe_f.step(f"zT{f}"))
                pe.wait_ge(*act_f.of("zTc7", i))
                pe.wait_ge(*act_a.of("v0c", i))
                before(pe, act_f, "moec", i)

                def scores(n):
                    u, m = n // 8, n % 8
                    if n >= 2:
                        pe.wait_ge(*act_f.of(f"ex{n - 2}", i))
                    for b in range(2):
                        o = ps_s[n % 2][:, b, :]
                        pe.matmul(o[:, 0:2 * UNIT], ident_b[:], causal[:].rearrange("p a c -> p (a c)"),
                                  start=True, stop=False, skip_group_check=True)
                        g = 2 * (m % 2) + b
                        rows = slice(32 * g, 32 * g + ROWS0)
                        for a in range(2):
                            j = 2 * (m // 2) + a
                            pe.matmul(o[:, UNIT * a:UNIT * a + T], kT0[rows, u, j, 0:P], qT0[rows, u, j, :],
                                      start=False, stop=False, skip_group_check=True)
                            last = pe.matmul(o[0:S1, UNIT * a + T:UNIT * a + UNIT], kT0[rows, u, j, P:T],
                                             qT0[rows, u, j, P:T], start=False, stop=(a == 1), skip_group_check=True)
                    last.then_inc(*pe_f.step(f"sc{n}"))

                def values(n):
                    u, m = n // 8, n % 8
                    pe.wait_ge(*act_f.of(f"ex{n}", i))
                    for c in range(4):
                        w = slice(32 * (4 * m + c), 32 * (4 * m + c) + 32)
                        pe.matmul(ps_y[32 * c:32 * c + 32, T * u:T * u + T], vp0[0][:, u, w], e0[:, n % 2, c, 0:T],
                                  start=(m == 0), stop=False, skip_group_check=True)
                    for c in range(4):
                        w = slice(32 * (4 * m + c), 32 * (4 * m + c) + 32)
                        last = pe.matmul(ps_y[32 * c:32 * c + 32, T * u + P:T * u + T], vp0[1][0:S1, u, w],
                                         e0[0:S1, n % 2, c, T:UNIT], start=False, stop=(m == 7), skip_group_check=True)
                    last.then_inc(*pe_f.step(f"pv{n}"))

                for n in range(17):
                    if n < 16:
                        scores(n)
                    if n:
                        values(n - 1)
                    if done is not None:
                        back(done, n)

            def middle(i, prev):
                before(pe, act_s, "v1c", i)
                pe.wait_ge(*act_f.of("y0c", i))
                to_tokens(y0, ps_x).then_inc(*pe_f.step("y0T"))
                pe.wait_ge(*dve_f.of("yn0", i))
                to_features(yn, ps_x).then_inc(*pe_f.step("yn0T"))
                pe.wait_ge(*act_f.of("yn0Tc", i))
                for t in range(2):
                    last = pe.matmul(ps_x[0:TP, P * t:P * t + P], ynT[:, TP * t:TP * t + TP],
                                     w_proj[:, 0].rearrange("p u c -> p (u c)"), start=True, stop=True)
                last.then_inc(*pe_f.step("proj0"))
                values1(prev, 0)
                values1(prev, 1)
                pe.wait_ge(*dve_f.of("hn1", i))
                apart(pe, turns_pe)
                to_features64(hn1, ps_x).then_inc(*pe_f.step("hn1T"))
                pe.wait_ge(*act_f.of("hn1Tc", i))
                for n in range(4):
                    t, u = n // 2, n % 2
                    o = ps_x[0:TP, E * n:E * n + E]
                    pe.matmul(o, hn1T[:, T * u + TP * t:T * u + TP * t + TP], gate_w[:], start=True, stop=False)
                    last = pe.matmul(o, ones[:, 0:TP], gate_b[:], start=False, stop=True)
                last.then_inc(*pe_f.step("gate"))
                values1(prev, 2)
                pe.wait_ge(*dve_f.of("G3", i))
                apart(pe, turns_pe)
                o = ps_x[:].bitcast(BF16)
                for n in range(4):
                    t, u = n // 2, n % 2
                    last = pe.transpose(o[0:3 * E, T * u + TP * t:T * u + TP * t + TP],
                                        g3[:, n].rearrange("p s e -> p (s e)"), ident_b[0:TP, 0:TP])
                last.then_inc(*pe_f.step("gT"))
                pe.wait_ge(*act_f.of("gTc", i))

            def experts(i, after):
                def up(e):
                    if e >= 2:
                        pe.wait_ge(*act_f.of(f"gc{e - 2}", i))
                    pe.matmul(bank(e % 2)[:, 0:2 * T], w1e[:, e, :], hn1T[:], start=True, stop=True)
                    pe.matmul(bank(2 + e % 2)[:, 0:2 * T], pick[:, e, :], gT[:], start=True, stop=True)\
                      .then_inc(*pe_f.step(f"z{e}"))

                def down(e):
                    if e == 0:
                        for s in range(3):
                            pe.matmul(ps_y[0:D, 0:2 * T], b2e[:, s, :], gT[:], start=(s == 0), stop=False,
                                      skip_group_check=True)
                    pe.wait_ge(*pool_f.of(f"hp{e}", i))
                    r = D * (e % 2)
                    pe.matmul(ps_y[r:r + D, 0:2 * T], w2e[:, e, :], hp[:, e % 2, :], start=(e == 1), stop=(e >= E - 2),
                              skip_group_check=True).then_inc(*pe_f.step(f"o{e}"))

                for e in range(E + 1):
                    if e < E:
                        up(e)
                    if e:
                        down(e - 1)
                    first(after, e)

            def rest(i, prev, after):
                if after is not None:
                    pe.wait_ge(*act_a.of("v0c", after))
                pe.wait_ge(*act_f.of("moec", i))
                to_tokens(moe, ps_x).then_inc(*pe_f.step("moeT"))
                values1(prev, 3)
                values1(prev, 4)
                pe.wait_ge(*dve_f.of("hn2", i))
                to_features(hn2, ps_x).then_inc(*pe_f.step("hn2T"))
                pe.wait_ge(*act_f.of("hn2Tc", i))
                for t in range(2):
                    o = ps_x[0:TP, 256 * t:256 * t + 256]
                    pe.matmul(o, hn2T[:, TP * t:TP * t + TP], w_qkv1[:, 0:2].rearrange("p k u c -> p (k u c)"),
                              start=True, stop=False)
                    last = pe.matmul(o, ones[:, 0:TP], brow1[:, 0:2].rearrange("a k u c -> a (k u c)"), start=False, stop=True)
                last.then_inc(*pe_f.step("qk1"))
                values1(prev, 5)
                pe.wait_ge(*act_f.of(f"gc{E - 1}", i))
                pe.wait_ge(*pool_f.of("gk1", i))
                for f in range(5):
                    if f == 4:
                        pe.wait_ge(*act_f.of("kqTc0", i))
                    for a in range(2):
                        for t in range(2):
                            if f < 4:
                                u, p = f // 2, 2 * (f % 2) + a
                                src = zk1[:, 2 * t + u, P * p:P * p + P]
                            else:
                                u = a
                                src = zq1[:, 2 * t + u].rearrange("p n c -> p (n c)")
                            c = T * a + TP * t
                            last = pe.transpose(bank(f % 4)[:, c:c + TP], src, ident[0:TP, 0:TP])
                    last.then_inc(*pe_f.step(f"kqT{f}"))
                pe.wait_ge(*act_f.of("kqTc4", i))

            def to_features(src, dst):
                for t in range(2):
                    last = pe.transpose(dst[:, TP * t:TP * t + TP], src[:, 2 * t:2 * t + 2].rearrange("p u c -> p (u c)"),
                                        ident[0:TP, 0:TP])
                return last

            def to_features64(src, dst):
                for n in range(4):
                    t, u = n // 2, n % 2
                    last = pe.transpose(dst[0:D, T * u + TP * t:T * u + TP * t + TP], src[:, n, :], ident[0:TP, 0:TP])
                return last

            def to_tokens(src, dst):
                for n in range(4):
                    t, u = n // 2, n % 2
                    last = pe.transpose(dst[0:TP, P * n:P * n + P], src[:, T * u + TP * t:T * u + TP * t + TP], ident[:])
                return last

            def scores1(i, k):
                u, p = k // 4, k % 4
                if k >= 2:
                    pe.wait_ge(*act_s.of(f"sc{k - 2}b", i))
                o = ps_s[k % 2]
                for a in range(2):
                    half = slice(D * a, D * a + D)
                    pe.matmul(o[:, a, 0:T], qT1[half, u, 0:P], kT1[half, u, p, :], start=True, stop=True)
                    last = pe.matmul(o[half, a, T:2 * T], qT1[half, u, T - D:T], kT1[half, u, p, :], start=True, stop=True)
                last.then_inc(*pe_s.step(f"s{k}"))

            def values1(i, k):
                if i is None:
                    return
                u, p = k // 4, k % 4
                pe.wait_ge(*dve_t.of(f"k{k}r{ROUNDS}p2", i))
                if k:
                    pe.wait_ge(*act_b.of(f"pc1_{k - 1}", i))
                else:
                    before(pe, act_b, "ffTc", i)
                for m, (m0, m1) in enumerate(((0, P), (P, T))):
                    if m:
                        pe.wait_ge(*act_b.of(f"pc0_{k}", i))
                        apart(pe, turns_pe)
                    pe.transpose(ps_u[0:m1 - m0, T - D:T + D], e_s[:, k, 2, m0:m1], ident[:])
                    pe.transpose(ps_u[0:m1 - m0, 0:P], e_s[:, k, 0, m0:m1], ident[:])
                    last = pe.transpose(ps_u[0:m1 - m0, T + D:T + D + P], e_s[:, k, 1, m0:m1], ident[:])
                    last.then_inc(*pe_b.step(f"pt{m}_{k}"))
                pe.wait_ge(*act_b.of(f"pc1_{k}", i))
                for a in range(2):
                    h = 2 * p + a
                    g, j = h % 4, h // 4
                    pieces = ((T + D, 0, P), (T + D - S1, P, T)) if a else ((0, 0, T),)
                    for m, rows in enumerate((P, S1)):
                        for at, n0, n1 in pieces:
                            last = pe.matmul(ps_v[32 * g:32 * g + 32, T * u + n0:T * u + n1], vp1[m][0:rows, u, 32 * h:32 * h + 32],
                                             pt[m][0:rows, at:at + n1 - n0], start=(j == 0 and m == 0 and n0 == 0),
                                             stop=(j == 1 and m == 1), skip_group_check=True)
                last.then_inc(*pe_b.step(f"pv{k}"))

            def v1(i):
                pe.wait_ge(*act_f.of("qk1c", i))
                w_v, b_v = (w[:, 2].rearrange("p u c -> p (u c)") for w in (w_qkv1, brow1))
                for o, c, n in ((ps_x[:, 0:P], slice(0, P), P), (ps_x[0:S1, P:2 * P], slice(P, T), S1)):
                    pe.matmul(o, hn2T[:, c], w_v, start=True, stop=False)
                    last = pe.matmul(o, ones[:, 0:n], b_v, start=False, stop=True)
                last.then_inc(*pe_s.step("v1"))

            def back_y1T(i):
                pe.wait_ge(*act_b.of("y1c", i))
                to_tokens(y1, ps_u).then_inc(*pe_b.step("y1T"))

            def back_yn1T(i):
                pe.wait_ge(*dve_b.of("yn1", i))
                to_features(yn1, ps_u).then_inc(*pe_b.step("yn1T"))

            def back_proj1(i):
                pe.wait_ge(*act_b.of("yn1Tc", i))
                for t in range(2):
                    o = ps_u[0:TP, P * t:P * t + P]
                    pe.matmul(o, yn1T[:, TP * t:TP * t + TP], w_proj[:, 1].rearrange("p u c -> p (u c)"), start=True, stop=False)
                    last = pe.matmul(o, ones[:, 0:TP], projb1[:].rearrange("a u c -> a (u c)"), start=False, stop=True)
                last.then_inc(*pe_b.step("proj1"))

            def back_h3T(i):
                pe.wait_ge(*dve_b.of("hn3", i))
                apart(pe, turns_pe)
                to_features64(hn3, ps_u).then_inc(*pe_b.step("h3T"))

            def back_route(i):
                pe.wait_ge(*act_b.of("h3Tc", i))
                apart(pe, turns_pe)
                pe.matmul(ps_u[0:1, 0:2 * T], wr[:], h3T[:], start=True, stop=True).then_inc(*pe_b.step("route"))

            def back_ffz(i, h):
                if h:
                    pe.wait_ge(*act_b.of("routec", i))
                pe.matmul((ps_v, ps_u)[h][:, 0:2 * T], fw1[:, h, :], h3T[:], start=True, stop=True)\
                  .then_inc(*pe_b.step(f"ffz{h}"))

            def back_ffo(i):
                pe.wait_ge(*act_b.of("gelu1", i))
                for u in range(2):
                    for h in range(2):
                        last = pe.matmul(ps_v[D * u:D * u + D, 0:T], fw2[:, h, :], gh[:, h, T * u:T * u + T],
                                         start=(h == 0), stop=(h == 1))
                last.then_inc(*pe_b.step("ffo"))

            def back_ffT(i):
                pe.wait_ge(*act_b.of("ffoc", i))
                for t in range(2):
                    last = pe.transpose(ps_u[0:TP, P * t:P * t + P], ffo[:, TP * t:TP * t + TP], ident[:])
                last.then_inc(*pe_b.step("ffT"))

            def back(i, n):
                if n == BACK_Y1T:
                    back_y1T(i)
                elif n == BACK_YN1T:
                    back_yn1T(i)
                elif n == BACK_PROJ1:
                    back_proj1(i)
                elif n == BACK_H3T:
                    back_h3T(i)
                elif n == BACK_ROUTE:
                    back_route(i)
                    back_ffz(i, 0)
                elif n == BACK_FFZ1:
                    back_ffz(i, 1)
                elif n == BACK_FFO:
                    back_ffo(i)
                elif n == BACK_FFT:
                    back_ffT(i)

            def body(i, prev, done, after):
                attention0(i, done)
                middle(i, prev)
                experts(i, after)
                rest(i, prev, after)
                for k in range(CHUNKS):
                    if k == 2:
                        values1(prev, 6)
                    if k == 6:
                        values1(prev, 7)
                    scores1(i, k)
                v1(i)

            for e in range(E):
                first(0, e)
            body(0, None, None, 1)
            body(1, 0, None, 2)
            with pe.Fori(2, PAIRS - 1) as i:
                body(i, i - 1, i - 2, i + 1)
            body(PAIRS - 1, PAIRS - 2, PAIRS - 3, None)
            for n in range(17):
                back(PAIRS - 2, n)
            for k in range(CHUNKS):
                values1(PAIRS - 1, k)
            for n in range(17):
                back(PAIRS - 1, n)
            pe.wait_ge(tail_dve, TAIL_SELECTED)
            for t in range(2):
                last = pe.transpose(ps_x[0:TP, B * t:B * t + B], tail_s[:, TP * t:TP * t + TP], ident[0:B, 0:B])
            last.then_inc(tail_pe, 1)

        @block.scalar
        def _(act):
            act.wait_ge(const_pe, 1)
            for n, w in enumerate((w_qkv0, w_qkv1)):
                for u in range(2):
                    half = slice(D * u, D * u + D)
                    kinds = 2 + n
                    act.copy(w[half, 0:kinds, u, :], ps_x[half, 192 * n:192 * n + D * kinds].rearrange("p (k c) -> p k c", k=kinds))
            for u in range(2):
                half = slice(D * u, D * u + D)
                for a in range(2):
                    for gq in range(2):
                        act.copy(w_qkv0[half, 2, u, :].rearrange("p (jp gh b a d) -> p a gh jp b d", gh=2, b=2, a=2, d=2)[:, a, gq],
                                 ps_x[half, 128:192].rearrange("p (jp a gh b d) -> p a gh jp b d", a=2, gh=2, b=2, d=2)[:, a, gq])
            for u in range(2):
                half = slice(D * u, D * u + D)
                last = act.copy(w_proj[half, :, u, :], ps_x[half, 384:512].rearrange("p (k c) -> p k c", k=2))
            last.then_inc(const_act, 1)
            act.wait_ge(const_pool, POOL_CONSTANTS)
            act.wait_ge(const_dve, DVE_CONSTANTS)
            act.wait_ge(loaded, n_loads)

            def v_copy(tiles, psum, u, step, j, d):
                for m, rows in enumerate((P, S1)):
                    src = psum[0:rows, P * m + D * u:P * m + D * u + D].rearrange("p (j g d) -> p j g d", j=j, g=4)
                    last = act.copy(v_view(tiles[m], u, step, rows, 0, d), src)
                return last

            def first_dense(i, n):
                if n == 0:
                    act.wait_ge(*pe_a.of("xT", i))
                    act.copy(x0, ps_x[:, 0:T_IN]).then_inc(*act_a.step("x0"))
                elif n == 1:
                    act.wait_ge(*pe_a.of("tok0", i))
                    act.activation(x1, ps_x[:, 0:T_IN], ACT.Tanh, bias=tok_b[:, 0:1]).then_inc(*act_a.step("x1"))
                elif n == 2:
                    act.wait_ge(*pe_a.of("tok1", i))
                    act.activation(x2[:], ps_x[:, 0:T_IN], ACT.Tanh, bias=tok_b[:, 1:2]).then_inc(*act_a.step("x2"))
                    act.wait_ge(*act_a.of("x2", i))
                    act.activation(x2s, x2[:], ACT.Square).then_inc(*act_a.step("x2s"))
                else:
                    act.wait_ge(*pe_a.of("tok2", i))
                    act.activation(x3, ps_x[:, 0:T_IN], ACT.Tanh, bias=tok_b[:, 2:3]).then_inc(*act_a.step("x3"))

            def first_x4(i):
                act.wait_ge(*pe_a.of("tok3", i))
                act.activation(x4[:].rearrange("p j c -> p (j c)"), ps_x[0:XT, 0:3 * P], ACT.Tanh).then_inc(*act_a.step("x4"))

            def first_h0(i):
                act.wait_ge(*pe_a.of("conv", i))
                before(act, dve_f, "h1", i)
                act.copy(h0[:].rearrange("p n c -> p (n c)"), ps_x[0:TP, 0:256]).then_inc(*act_a.step("h0"))

            def first_hn0T(i):
                act.wait_ge(*pe_a.of("hn0T", i))
                act.copy(hn0T[:], ps_x[:, 0:T]).then_inc(*act_a.step("hn0Tc"))

            def first_qk0(i):
                act.wait_ge(*pe_a.of("qk0", i))
                src = ps_x[0:TP, :].rearrange("p (t k c) -> p k t c", t=2, k=2)
                act.copy(qk0[:], src).then_inc(*act_a.step("qk0c"))
                act.activation(qk0s[:], src, ACT.Square).then_inc(*act_a.step("qk0s"))

            def first_v0(i):
                act.wait_ge(*pe_a.of("v0", i))
                for u in range(2):
                    last = v_copy(vp0, ps_x, u, 131, 8, HD0)
                last.then_inc(*act_a.step("v0c"))

            def first(i, e):
                if i is None:
                    return
                if e == FIRST_XT:
                    first_dense(i, 0)
                elif e in FIRST_DENSE:
                    first_dense(i, 1 + FIRST_DENSE.index(e))
                elif e == FIRST_TOK3:
                    first_x4(i)
                elif e == FIRST_CONV:
                    first_h0(i)
                elif e == FIRST_HN0T:
                    first_hn0T(i)
                elif e == FIRST_QK0:
                    first_qk0(i)
                elif e == FIRST_V0:
                    first_v0(i)

            def attention0(i, done):
                for f in range(8):
                    side, u, half = f // 4, f // 2 % 2, f % 2
                    act.wait_ge(*pe_f.of(f"zT{f}", i))
                    dst = (qT0, kT0)[side][:, u, 4 * half:4 * half + 4, :].rearrange("p j t -> p (j t)")
                    act.copy(dst, bank(f % 4).bitcast(BF16)[:, 0:4 * T]).then_inc(*act_f.step(f"zTc{f}"))
                for n in range(16):
                    act.wait_ge(*pe_f.of(f"sc{n}", i))
                    if n >= 2:
                        act.wait_ge(*pe_f.of(f"pv{n - 2}", i))
                    act.activation(e0[:, n % 2].rearrange("p (b a) c -> p b (a c)", b=2), ps_s[n % 2][:, :, 0:2 * UNIT], ACT.Exp)\
                       .then_inc(*act_f.step(f"ex{n}"))
                    if done is not None:
                        back(done, n)

            def middle(i, prev):
                act.wait_ge(*pe_f.of("pv15", i))
                act.copy(y0[:], ps_y[:, 0:2 * T]).then_inc(*act_f.step("y0c"))
                act.wait_ge(*pe_f.of("yn0T", i))
                act.copy(ynT[:], ps_x[:, 0:T]).then_inc(*act_f.step("yn0Tc"))
                values1(prev, 0)
                values1(prev, 1)
                act.wait_ge(*pe_f.of("hn1T", i))
                act.copy(hn1T[:], ps_x[0:D, 0:2 * T]).then_inc(*act_f.step("hn1Tc"))
                values1(prev, 2)
                act.wait_ge(*dve_f.of("gd", i))
                act.activation(gs[:, 1, :], gs[:, 0, :], ACT.Exp).then_inc(*act_f.step("gexp"))
                act.wait_ge(*pe_f.of("gT", i))
                act.copy(gT[:], ps_x[:].bitcast(BF16)[0:3 * E, 0:2 * T]).then_inc(*act_f.step("gTc"))

            def experts(i, after):
                for e in range(E):
                    act.wait_ge(*pe_f.of(f"z{e}", i))
                    if e >= 2:
                        act.wait_ge(*pool_f.of(f"hp{e - 2}", i))
                    act.activation(hr[:, e % 2, :], bank(e % 2)[:, 0:2 * T], ACT.Relu, bias=b1e[:, e:e + 1])\
                       .then_inc(*act_f.step(f"relu{e}"))
                    act.copy(hg[:, e % 2, :], bank(2 + e % 2)[:, 0:2 * T]).then_inc(*act_f.step(f"gc{e}"))
                    first(after, e)

            def rest(i, prev):
                act.wait_ge(*pe_f.of(f"o{E - 1}", i))
                act.copy(moe[:], ps_y[:, 0:2 * T]).then_inc(*act_f.step("moec"))
                values1(prev, 3)
                values1(prev, 4)
                act.wait_ge(*pe_f.of("hn2T", i))
                act.copy(hn2T[:], ps_x[:, 0:T]).then_inc(*act_f.step("hn2Tc"))
                act.wait_ge(*pe_f.of("qk1", i))
                for t in range(2):
                    last = act.copy(qk1[:, :, 2 * t:2 * t + 2, :],
                                    ps_x[0:TP, 256 * t:256 * t + 256].rearrange("p (k u c) -> p k u c", k=2, u=2))
                last.then_inc(*act_f.step("qk1c"))
                values1(prev, 5)
                for f in range(5):
                    act.wait_ge(*pe_f.of(f"kqT{f}", i))
                    dst = kT1[:, f // 2, 2 * (f % 2):2 * (f % 2) + 2, :] if f < 4 else qT1[:]
                    act.copy(dst.rearrange("p a t -> p (a t)"), bank(f % 4)[:, 0:2 * T]).then_inc(*act_f.step(f"kqTc{f}"))

            def scores1(i, k):
                before(act, dve_t, f"k{k}r{ROUNDS}p2", i)
                act.wait_ge(*pe_s.of(f"s{k}", i))
                act.copy(w_s[:, k, 0:2, :], ps_s[k % 2][:, :, 0:T]).then_inc(*act_s.step(f"sc{k}a"))
                for a in range(2):
                    half = slice(D * a, D * a + D)
                    last = act.copy(w_s[half, k, 2, :], ps_s[k % 2][half, a, T:2 * T])
                last.then_inc(*act_s.step(f"sc{k}b"))

            def exps1(i, k):
                act.wait_ge(*dve_s.of(f"m{k}n", i))
                before(act, pe_b, f"pt1_{k}", i)
                for t in range(3):
                    last = act.activation(e_s[:, k, t, :], w_s[:, k, t, :], ACT.Exp, bias=nmax[:, k, t:t + 1])
                last.then_inc(*act_s.step(f"e{k}"))

            def values1(i, k):
                if i is None:
                    return
                for m, rows in enumerate((P, S1)):
                    act.wait_ge(*pe_b.of(f"pt{m}_{k}", i))
                    act.copy(pt[m][:], ps_u[0:rows, 0:T + D + P]).then_inc(*act_b.step(f"pc{m}_{k}"))

            def v1(i):
                act.wait_ge(*pe_s.of("v1", i))
                before(act, pe_b, f"pv{CHUNKS - 1}", i)
                for u in range(2):
                    last = v_copy(vp1, ps_x, u, 137, 2, HD1)
                last.then_inc(*act_s.step("v1c"))

            def back_y1(i):
                act.wait_ge(*pe_b.of(f"pv{CHUNKS - 1}", i))
                act.copy(y1[:], ps_v[:, 0:2 * T]).then_inc(*act_b.step("y1c"))

            def back_yn1T(i):
                act.wait_ge(*pe_b.of("yn1T", i))
                act.copy(yn1T[:], ps_u[:, 0:T]).then_inc(*act_b.step("yn1Tc"))

            def back_h3T(i):
                act.wait_ge(*pe_b.of("h3T", i))
                act.copy(h3T[:], ps_u[0:D, 0:2 * T]).then_inc(*act_b.step("h3Tc"))

            def back_route(i):
                act.wait_ge(*pe_b.of("route", i))
                if not (isinstance(i, int) and i == 0):
                    act.wait_ge(routed, 16 * i)
                act.activation(rw[:], ps_u[0:1, 0:2 * T], ACT.Identity, bias=br[:, 0:1]).then_inc(*act_b.step("routec"))

            def back_gelu(i):
                for h in range(2):
                    act.wait_ge(*pe_b.of(f"ffz{h}", i))
                    act.activation(gh[:, h, :], (ps_v, ps_u)[h][:, 0:2 * T], ACT.Gelu_apprx_tanh, bias=fb1[:, h:h + 1])\
                       .then_inc(*act_b.step(f"gelu{h}"))

            def back_ffo(i):
                act.wait_ge(*pe_b.of("ffo", i))
                act.activation(ffo[:], ps_v[:, 0:T], ACT.Identity, bias=fb2[:, 0:1]).then_inc(*act_b.step("ffoc"))

            def back_ffT(i):
                act.wait_ge(*pe_b.of("ffT", i))
                if not (isinstance(i, int) and i == 0):
                    act.wait_ge(y_stored, 16 * i)
                act.copy(ffy[:].rearrange("p n c -> p (n c)"), ps_u[0:TP, 0:256]).then_inc(*act_b.step("ffTc"))

            def back(i, n):
                if n == BACK_Y1T:
                    back_y1(i)
                elif n == BACK_YN1T:
                    back_yn1T(i)
                elif n == BACK_H3T:
                    back_h3T(i)
                elif n == BACK_ROUTE:
                    back_route(i)
                elif n == BACK_FFZ1:
                    back_gelu(i)
                elif n == BACK_FFO:
                    back_ffo(i)
                elif n == BACK_FFT:
                    back_ffT(i)

            def body(i, prev, done, after):
                attention0(i, done)
                middle(i, prev)
                experts(i, after)
                rest(i, prev)
                for k in range(CHUNKS):
                    if k == 2:
                        values1(prev, 6)
                    if k == 6:
                        values1(prev, 7)
                    scores1(i, k)
                for k in range(CHUNKS):
                    exps1(i, k)
                v1(i)

            for e in range(E):
                first(0, e)
            body(0, None, None, 1)
            body(1, 0, None, 2)
            with act.Fori(2, PAIRS - 1) as i:
                body(i, i - 1, i - 2, i + 1)
            body(PAIRS - 1, PAIRS - 2, PAIRS - 3, None)
            for n in range(17):
                back(PAIRS - 2, n)
            for k in range(CHUNKS):
                values1(PAIRS - 1, k)
            for n in range(17):
                back(PAIRS - 1, n)

        @block.gpsimd
        def _(pool):
            for w in (tok_w, w_qkv0, w_qkv1):
                pool.memset(w[:], 0.0)
            pool.memset(w_proj[:], 0.0).then_inc(zeroed, 1)
            pool.memset(ident[:], 0.0)
            pool.memset(ident_b[:], 0.0)
            pool.memset(pick[:], 0.0)
            pool.memset(causal[:], 0.0).then_inc(zeroed, 1)
            pool.wait_ge(zeroed, 2)
            pool.affine_select(ident[:], ident[:], [[-1, P]], ALU.not_equal, 1.0, base=0, channel_multiplier=1)
            pool.affine_select(ident_b[:], ident_b[:], [[-1, P]], ALU.not_equal, 1.0, base=0, channel_multiplier=1)\
                .then_inc(const_pool, 1)
            pool.affine_select(causal[:, :, 0:T], causal[:, :, 0:T], [[0, 2], [1, T]], ALU.is_ge, MASKED,
                               base=0, channel_multiplier=-1)
            pool.affine_select(causal[:, :, T:UNIT], causal[:, :, T:UNIT], [[0, 2], [1, S1]], ALU.is_ge, MASKED,
                               base=0, channel_multiplier=-1).then_inc(const_pool, 1)
            for s in range(3):
                pool.wait_ge(const_pool, 2 + s)
                pool.affine_select(pick[:], pick[:], [[-1, E], [0, P]], ALU.not_equal, 1.0,
                                   base=-E * s, channel_multiplier=1).then_inc(const_pool, 1)
            pool.iota(expert_id[:], [[0, 4], [1, E]], base=0, channel_multiplier=0,
                      allow_small_or_imprecise_dtypes=True).then_inc(const_pool, 1)
            for k in range(TAPS):
                if k >= 2:
                    pool.wait_ge(tap_done, k)
                pool.memset(tap_mask[:, k % 2], 0.0).then_inc(tap_made, 1)
                pool.wait_ge(tap_made, 2 * k + 1)
                pool.affine_select(tap_mask[:, k % 2], tap_mask[:, k % 2], [[XT, 3], [-2, T]], ALU.not_equal, 1.0,
                                   base=PAD - k, channel_multiplier=1).then_inc(tap_made, 1)
            pool.wait_ge(const_dve, DVE_CONSTANTS)

            def squares(i):
                pool.wait_ge(*act_a.of("qk0s", i))
                sq2 = qk0s[:].rearrange("p k t (h d) -> p (k t h) d", d=2)
                pool.tensor_tensor(rx[:], sq2[:, :, 0], sq2[:, :, 1], ALU.add).then_inc(*pool_a.step("ss"))
                pool.wait_ge(*pool_a.of("ss", i))
                apart(pool, turns_pool)
                pool.tensor_scalar(rx[:], rx[:], 1.0 / HD0, 1e-6, ALU.mult, ALU.add).then_inc(*pool_a.step("sx"))

            def scaled(i):
                pool.wait_ge(*dve_a.of("b_n2c", i))
                y = rr[:]
                q2 = qk0[:].rearrange("p k t (h d) -> p (k t h) d", d=2)
                pool.tensor_tensor(q2, q2, y.unsqueeze(2).broadcast_to([TP, 256, 2]), ALU.mult).then_inc(*pool_a.step("qr"))
                pool.wait_ge(*pool_a.of("qr", i))
                pool.tensor_tensor(qk0[:], qk0[:], rms_w[:].unsqueeze(2).broadcast_to([TP, 2, 2, P]), ALU.mult)\
                    .then_inc(*pool_a.step("qw"))
                pool.wait_ge(*pool_a.of("qw", i))
                qn, kn = (qk0[:, s].rearrange("p t c -> p (t c)") for s in range(2))
                pool.tensor_tensor(selfp[:], qn, kn, ALU.mult).then_inc(*pool_a.step("qkp"))
                pool.wait_ge(*pool_a.of("qkp", i))
                sp2 = selfp[:].rearrange("p (h d) -> p h d", d=2)
                pool.tensor_tensor(selfs[:], sp2[:, :, 0], sp2[:, :, 1], ALU.add).then_inc(*pool_a.step("self"))
                pool.wait_ge(*pool_a.of("self", i))
                apart(pool, turns_pool)
                pool.tensor_scalar(negc[:], selfs[:], room[:, 0:1], -1.0, ALU.max, ALU.mult).then_inc(*pool_a.step("negc"))

            def parts(i):
                pool.wait_ge(*dve_a.of("c1", i))
                q4 = [qk0[:, s].rearrange("p t (h d) -> p (t h) d", d=2) for s in range(2)]
                r4 = [[res[:, r, s].rearrange("p (h d) -> p h d", d=2) for s in range(2)] for r in range(2)]
                slot = lambda z, n: z[:, :, 2 * n:2 * n + 2]
                pool.tensor_tensor(r4[0][0], q4[0], slot(zq, 0), ALU.subtract).then_inc(*pool_a.step("rq1"))
                pool.tensor_tensor(r4[0][1], q4[1], slot(zk, 2), ALU.subtract).then_inc(*pool_a.step("rk1"))
                pool.tensor_tensor(resc[:, 0], negc[:], zq[:, :, 12], ALU.subtract).then_inc(*pool_a.step("rc1"))
                pool.wait_ge(*dve_a.of("c2", i))
                pool.tensor_tensor(r4[1][0], r4[0][0], slot(zq, 3), ALU.subtract).then_inc(*pool_a.step("rq2"))
                pool.tensor_tensor(r4[1][1], r4[0][1], slot(zk, 1), ALU.subtract).then_inc(*pool_a.step("rk2"))
                pool.tensor_tensor(resc[:, 1], resc[:, 0], zq[:, :, 13], ALU.subtract).then_inc(*pool_a.step("rc2"))

            def experts(i):
                for e in range(E):
                    pool.wait_ge(*act_f.of(f"gc{e}", i))
                    if e >= 2:
                        pool.wait_ge(*pe_f.of(f"o{e - 2}", i))
                    pool.tensor_tensor(hp[:, e % 2, :], hr[:, e % 2, :], hg[:, e % 2, :], ALU.mult).then_inc(*pool_f.step(f"hp{e}"))

            def norm_heads(i):
                flat = lambda t: t.rearrange("p k n c -> p (k n c)")
                pool.wait_ge(*dve_f.of("g_cen", i))
                pool.tensor_tensor(flat(sq1), flat(c1), flat(c1), ALU.mult).then_inc(*pool_f.step("g_sq"))
                pool.wait_ge(*dve_f.of("g_n2c", i))
                c8 = c1.rearrange("p k n (h d) -> p (k n h) d", d=HD1)
                pool.tensor_tensor(c8, c8, n1[:, 4, :].unsqueeze(2).broadcast_to([TP, 64, HD1]), ALU.mult)\
                    .then_inc(*pool_f.step("g_norm"))
                pool.wait_ge(*pool_f.of("g_norm", i))
                c4 = c1.rearrange("p k (t u) c -> p k t (u c)", t=2)
                pool.tensor_tensor(c4, c4, gam1[:].unsqueeze(2).broadcast_to([TP, 2, 2, P]), ALU.mult).then_inc(*pool_f.step("g_gam"))
                pool.wait_ge(*pool_f.of("g_gam", i))
                for n in range(2):
                    dst = zq1[:, :, n, :].rearrange("p (t u) c -> p t u c", t=2)
                    pool.tensor_tensor(dst, c1[:, 0].rearrange("p (t u) c -> p t u c", t=2),
                                       bet1[:, 0].rearrange("p (u c) -> p u c", u=2).unsqueeze(1).broadcast_to([TP, 2, 2, D]),
                                       ALU.add).then_inc(*pool_f.step(f"gq{n}"))
                for t in range(2):
                    dst = zk1[:, 2 * t:2 * t + 2, :].rearrange("p u (h x) -> p u h x", x=72)[:, :, :, 0:HD1]
                    pool.tensor_tensor(dst, c1[:, 1, 2 * t:2 * t + 2].rearrange("p u (h d) -> p u h d", d=HD1),
                                       bet1[:, 1].rearrange("p (u h d) -> p u h d", u=2, d=HD1), ALU.add)\
                        .then_inc(*pool_f.step(f"gk{t}"))

            def keep(i):
                if not (isinstance(i, int) and i == 0):
                    pool.wait_ge(*dve_b.of("h3", i - 1))
                pool.wait_ge(*dve_f.of("h2", i))
                apart(pool, turns_pool)
                pool.tensor_copy(h2k[:], h2[:]).then_inc(*pool_k.step("h2k"))

            def body(i, prev, after):
                if prev is not None:
                    keep(prev)
                experts(i)
                if after is not None:
                    squares(after)
                    scaled(after)
                norm_heads(i)
                if after is not None:
                    parts(after)

            squares(0)
            scaled(0)
            parts(0)
            body(0, None, 1)
            body(1, 0, 2)
            with pool.Fori(2, PAIRS - 1) as i:
                body(i, i - 1, i + 1)
            body(PAIRS - 1, PAIRS - 2, None)
            keep(PAIRS - 1)

        @block.vector
        def _(dve):
            chain = [0]

            def const(ins):
                chain[0] += 1
                ins.then_inc(const_dve, 1)

            const(dve.memset(ones[:], 1.0))
            for m in range(2):
                const(dve.memset(vp0[m][:], 0.0))
                const(dve.memset(vp1[m][:], 0.0))
            for z in (zq, zk, zk1):
                const(dve.memset(z[:], 0.0))
            const(dve.memset(toeplitz[:], 0.0))
            dve.wait_ge(const_dve, chain[0])
            for m in range(2):
                for u in range(2):
                    const(dve.memset(v_view(vp0[m], u, 131, P, HD0, HD0 + 1), 1.0))
                    const(dve.memset(v_view(vp1[m], u, 137, P, HD1, HD1 + 1), 1.0))
            const(dve.memset(zk[:, :, 12:15], 1.0))
            dve.wait_ge(loaded, n_loads)
            const(dve.tensor_scalar(core_abs[:], core[:], -1.0, None, ALU.mult))
            dve.wait_ge(const_dve, chain[0])
            const(dve.tensor_tensor(core_abs[:], core_abs[:], core[:], ALU.max))
            dve.wait_ge(const_dve, chain[0])
            const(dve.tensor_scalar(tok_w[:, 2, :], tok_w[:, 2, :], core_abs[:, 0:1], None, ALU.mult))
            for s in range(2):
                const(dve.tensor_scalar(rms_w[:, s, :].rearrange("p (h d) -> p h d", d=2),
                                        rms_raw[:, s, :].unsqueeze(1).broadcast_to([TP, D, 2]),
                                        HD0 ** -0.5 if s == 0 else 1.0, None, ALU.mult))
            dve.wait_ge(const_dve, chain[0])
            const(dve.tensor_tensor(wprod[:], rms_w[:, 0, 0:2], rms_w[:, 1, 0:2], ALU.mult))
            dve.wait_ge(const_dve, chain[0])
            const(dve.tensor_reduce(room[:], wprod[:], AX_X, ALU.max, apply_absolute_value=True))
            dve.wait_ge(const_dve, chain[0])
            const(dve.tensor_scalar(room[:], room[:], float(HD0), -SHIFT_ROOM, ALU.mult, ALU.add))
            for s in range(2):
                for dst, n in ((gam1, s), (bet1, 2 + s)):
                    const(dve.tensor_scalar(dst[:, s, :].rearrange("p (h d) -> p h d", d=HD1),
                                            gb_raw[:, n, :].unsqueeze(1).broadcast_to([TP, 16, HD1]),
                                            HD1 ** -0.5 if s == 0 else 1.0, None, ALU.mult))
            const(dve.tensor_copy(b2e[:, 0, :], b2raw[:]))
            dve.wait_ge(const_dve, chain[0])
            const(dve.tensor_tensor(b2res[:, 0, :], b2raw[:], b2e[:, 0, :], ALU.subtract))
            dve.wait_ge(const_dve, chain[0])
            const(dve.tensor_copy(b2e[:, 1, :], b2res[:, 0, :]))
            dve.wait_ge(const_dve, chain[0])
            const(dve.tensor_tensor(b2res[:, 1, :], b2res[:, 0, :], b2e[:, 1, :], ALU.subtract))
            dve.wait_ge(const_dve, chain[0])
            const(dve.tensor_copy(b2e[:, 2, :], b2res[:, 1, :]))
            for k in range(TAPS):
                dve.wait_ge(tap_made, 2 * k + 2)
                if k:
                    dve.wait_ge(tap_done, k)
                dve.scalar_tensor_tensor(toeplitz[:], tap_mask[:, k % 2], taps[:, k:k + 1], toeplitz[:], ALU.mult, ALU.add)\
                   .then_inc(tap_done, 1)
            dve.wait_ge(tap_done, TAPS)
            const(dve.memset(gs[:, 4, :], 0.0))
            assert chain[0] == DVE_CONSTANTS, chain[0]
            dve.wait_ge(const_pool, POOL_CONSTANTS)

            def rsqrt(x, y, t, tag, i, steps):
                dve.tensor_scalar(y.bitcast(I32), x.bitcast(I32), -0.5, RSQRT_MAGIC, ALU.mult, ALU.add)\
                   .then_inc(*steps.step(f"{tag}_guess"))
                dve.wait_ge(*steps.of(f"{tag}_guess", i))
                for r in range(3):
                    dve.scalar_tensor_tensor(t, y, -0.5, y, ALU.mult, ALU.mult).then_inc(*steps.step(f"{tag}_n{r}a"))
                    dve.wait_ge(*steps.of(f"{tag}_n{r}a", i))
                    dve.tensor_tensor(t, t, x, ALU.mult).then_inc(*steps.step(f"{tag}_n{r}b"))
                    dve.wait_ge(*steps.of(f"{tag}_n{r}b", i))
                    dve.scalar_tensor_tensor(y, t, 1.5, y, ALU.add, ALU.mult).then_inc(*steps.step(f"{tag}_n{r}c"))
                    dve.wait_ge(*steps.of(f"{tag}_n{r}c", i))

            def centre(src, tag, i, steps):
                dve.tensor_reduce(lnt[:, 0, :], src[:], AX_X, ALU.add).then_inc(*steps.step(f"{tag}_sum"))
                dve.wait_ge(*steps.of(f"{tag}_sum", i))
                dve.tensor_scalar(lnt[:, 1, :], lnt[:, 0, :], 1.0 / D, None, ALU.mult).then_inc(*steps.step(f"{tag}_mean"))
                dve.wait_ge(*steps.of(f"{tag}_mean", i))
                dve.tensor_tensor(cen[:], src[:], over(lnt[:, 1, :]), ALU.subtract).then_inc(*steps.step(f"{tag}_cen"))
                dve.wait_ge(*steps.of(f"{tag}_cen", i))
                dve.tensor_tensor(sq[:], cen[:], cen[:], ALU.mult).then_inc(*steps.step(f"{tag}_sq"))
                dve.wait_ge(*steps.of(f"{tag}_sq", i))
                dve.tensor_reduce(lnt[:, 2, :], sq[:], AX_X, ALU.add).then_inc(*steps.step(f"{tag}_ssq"))
                dve.wait_ge(*steps.of(f"{tag}_ssq", i))
                dve.tensor_scalar(lnt[:, 3, :], lnt[:, 2, :], 1.0 / D, 1e-5, ALU.mult, ALU.add).then_inc(*steps.step(f"{tag}_var"))
                dve.wait_ge(*steps.of(f"{tag}_var", i))
                rsqrt(lnt[:, 3, :], lnt[:, 4, :], lnt[:, 5, :], tag, i, steps)

            def over(x, n=D):
                return x.unsqueeze(2).broadcast_to([TP, x.shape[1], n])

            def norm_tok(i):
                dve.wait_ge(*act_a.of("h0", i))
                centre(h0, "a", i, dve_a)
                dve.tensor_tensor(hn0[:], cen[:], over(lnt[:, 4, :]), ALU.mult).then_inc(*dve_a.step("hn0"))

            def roots0(i):
                dve.wait_ge(*pool_a.of("sx", i))
                rsqrt(rx[:], rr[:], rt[:], "b", i, dve_a)

            def parts0(i):
                slots = lambda z, a, b, s: z[:, :, 0:12].rearrange("p h (s d) -> p h s d", d=2)[:, :, a:b:s, :]
                wide = lambda x, n: x.rearrange("p (h d) -> p h d", d=2).unsqueeze(2).broadcast_to([TP, P, n, 2])
                qn, kn = (qk0[:, s].rearrange("p t c -> p (t c)") for s in range(2))
                dve.wait_ge(*pool_a.of("negc", i))
                before(dve, pe_f, "zT7", i)
                dve.tensor_copy(slots(zq, 0, 3, 1), wide(qn, 3)).then_inc(*dve_a.step("q1"))
                dve.tensor_copy(slots(zk, 2, 5, 1), wide(kn, 3)).then_inc(*dve_a.step("k1"))
                dve.tensor_copy(zq[:, :, 12], negc[:]).then_inc(*dve_a.step("c1"))
                dve.wait_ge(*pool_a.of("rc1", i))
                dve.tensor_copy(slots(zq, 3, 6, 2), wide(res[:, 0, 0], 2)).then_inc(*dve_a.step("q2"))
                dve.tensor_copy(slots(zk, 1, 6, 4), wide(res[:, 0, 1], 2)).then_inc(*dve_a.step("k2"))
                dve.tensor_copy(zq[:, :, 13], resc[:, 0]).then_inc(*dve_a.step("c2"))
                dve.wait_ge(*pool_a.of("rc2", i))
                dve.tensor_copy(slots(zq, 4, 5, 1), wide(res[:, 1, 0], 1)).then_inc(*dve_a.step("q3"))
                dve.tensor_copy(slots(zk, 0, 1, 1), wide(res[:, 1, 1], 1)).then_inc(*dve_a.step("k3"))
                dve.tensor_copy(zq[:, :, 14], resc[:, 1]).then_inc(*dve_a.step("c3"))

            def heads_out(psum, r, y, nj, d, steps, names, i):
                v = psum[0:TP, :].rearrange("p (n y) -> p n y", y=32)
                dve.reciprocal(r[:, :, 0:nj], v[:, :, d:d + (d + 1) * (nj - 1) + 1:d + 1]).then_inc(*steps.step(names[0]))
                dve.wait_ge(*steps.of(names[0], i))
                dve.tensor_tensor(y[:].rearrange("p n (g j d) -> p (n g) j d", g=4, d=d),
                                  v[:, :, 0:nj * (d + 1)].rearrange("p n (j d) -> p n j d", d=d + 1)[:, :, :, 0:d],
                                  r[:, :, 0:nj].unsqueeze(3).broadcast_to([TP, 16, nj, d]), ALU.mult)\
                   .then_inc(*steps.step(names[1]))

            def attended(i):
                dve.wait_ge(*pe_f.of("y0T", i))
                heads_out(ps_x, rec, yn, 8, HD0, dve_f, ("rec0", "yn0"), i)
                dve.wait_ge(*pe_f.of("proj0", i))
                dve.tensor_tensor(h1[:].rearrange("p n c -> p (n c)"), ps_x[0:TP, 0:256], h0[:].rearrange("p n c -> p (n c)"),
                                  ALU.add).then_inc(*dve_f.step("h1"))
                dve.wait_ge(*dve_f.of("h1", i))
                centre(h1, "c", i, dve_f)
                dve.tensor_tensor(hn1[:], cen[:], over(lnt[:, 4, :]), ALU.mult).then_inc(*dve_f.step("hn1"))

            def gates(i):
                dve.wait_ge(*pe_f.of("gate", i))
                dve.tensor_copy(lg[:].rearrange("p n e -> p (n e)"), ps_x[0:TP, 0:4 * E]).then_inc(*dve_f.step("lg"))
                dve.wait_ge(*dve_f.of("lg", i))
                for n in range(4):
                    apart(dve, turns_dve)
                    dve.max(gm[:, n, :], lg[:, n, :]).then_inc(*dve_f.step(f"gm{n}"))
                for n in range(4):
                    dve.wait_ge(*dve_f.of(f"gm{n}", i))
                    apart(dve, turns_dve)
                    dve.max_index(gi[:, n, :], gm[:, n, :], lg[:, n, :]).then_inc(*dve_f.step(f"gi{n}"))
                dve.wait_ge(*dve_f.of("gi3", i))
                dve.tensor_copy(gif[:], gi[:, :, 0:TOPK_E]).then_inc(*dve_f.step("gif"))
                dve.tensor_tensor(gs[:, 0, :], gm[:, :, 1], gm[:, :, 0], ALU.subtract).then_inc(*dve_f.step("gd"))
                dve.wait_ge(*act_f.of("gexp", i))
                dve.tensor_scalar(gs[:, 2, :], gs[:, 1, :], 1.0, None, ALU.add).then_inc(*dve_f.step("g1p"))
                dve.wait_ge(*dve_f.of("g1p", i))
                dve.reciprocal(gs[:, 3, :], gs[:, 2, :]).then_inc(*dve_f.step("p1"))
                dve.wait_ge(*dve_f.of("p1", i))
                dve.tensor_tensor(gs[:, 4, :], gs[:, 1, :], gs[:, 3, :], ALU.mult).then_inc(*dve_f.step("p2"))
                for n in range(2):
                    dve.tensor_tensor(ge[:, n], expert_id[:], over(gif[:, :, n], E), ALU.is_equal).then_inc(*dve_f.step(f"e{n + 1}"))
                for n in range(2):
                    dve.wait_ge(*dve_f.of(f"e{n + 1}", i))
                    dve.tensor_tensor(ge[:, 2 + n], ge[:, n], over(gs[:, 3 + n, :], E), ALU.mult).then_inc(*dve_f.step(f"e{n + 1}p"))
                dve.wait_ge(*dve_f.of("e2p", i))
                dve.tensor_tensor(gg[:, 0], ge[:, 2], ge[:, 3], ALU.add).then_inc(*dve_f.step("G"))
                dve.wait_ge(*dve_f.of("G", i))
                dve.tensor_copy(g3[:, :, 0, :], gg[:, 0]).then_inc(*dve_f.step("G1"))
                dve.wait_ge(*dve_f.of("G1", i))
                dve.tensor_tensor(gg[:, 1], gg[:, 0], g3[:, :, 0, :], ALU.subtract).then_inc(*dve_f.step("Gr"))
                dve.wait_ge(*dve_f.of("Gr", i))
                dve.tensor_copy(g3[:, :, 1, :], gg[:, 1]).then_inc(*dve_f.step("G2"))
                dve.wait_ge(*dve_f.of("G2", i))
                dve.tensor_tensor(gg[:, 2], gg[:, 1], g3[:, :, 1, :], ALU.subtract).then_inc(*dve_f.step("Gr2"))
                dve.wait_ge(*dve_f.of("Gr2", i))
                dve.tensor_copy(g3[:, :, 2, :], gg[:, 2]).then_inc(*dve_f.step("G3"))

            def mixed(i):
                dve.wait_ge(*pe_f.of("moeT", i))
                v = ps_x[0:TP, :].rearrange("p (n a c) -> p n a c", n=4, a=2)
                dve.tensor_tensor(my[:], hn1[:], v[:, :, 0, :], ALU.add).then_inc(*dve_f.step("ma"))
                dve.wait_ge(*dve_f.of("ma", i))
                dve.tensor_tensor(my[:], my[:], v[:, :, 1, :], ALU.add).then_inc(*dve_f.step("mb"))
                dve.wait_ge(*dve_f.of("mb", i))
                centre(my[:], "d", i, dve_f)
                dve.tensor_tensor(mn[:], cen[:], over(lnt[:, 4, :]), ALU.mult).then_inc(*dve_f.step("dn"))
                dve.wait_ge(*dve_f.of("dn", i))
                gb = [ln_gb[:, n, :].unsqueeze(1).broadcast_to([TP, 4, D]) for n in range(2)]
                dve.tensor_tensor(mn[:], mn[:], gb[0], ALU.mult).then_inc(*dve_f.step("dg"))
                dve.wait_ge(*dve_f.of("dg", i))
                dve.tensor_tensor(mn[:], mn[:], gb[1], ALU.add).then_inc(*dve_f.step("db"))
                dve.wait_ge(*dve_f.of("db", i))
                before(dve, pool_k, "h2k", i)
                dve.tensor_tensor(h2[:], mn[:], h1[:], ALU.add).then_inc(*dve_f.step("h2"))
                dve.wait_ge(*dve_f.of("h2", i))
                centre(h2, "f", i, dve_f)
                dve.tensor_tensor(hn2[:], cen[:], over(lnt[:, 4, :]), ALU.mult).then_inc(*dve_f.step("hn2"))

            def norm_heads(i):
                dve.wait_ge(*act_f.of("qk1c", i))
                groups = lambda t: t.rearrange("p k n (h d) -> p (k n h) d", d=HD1)
                dve.tensor_reduce(n1[:, 0, :], groups(qk1[:]), AX_X, ALU.add).then_inc(*dve_f.step("g_sum"))
                dve.wait_ge(*dve_f.of("g_sum", i))
                dve.tensor_scalar(n1[:, 1, :], n1[:, 0, :], 1.0 / HD1, None, ALU.mult).then_inc(*dve_f.step("g_mean"))
                dve.wait_ge(*dve_f.of("g_mean", i))
                dve.tensor_tensor(groups(c1), groups(qk1[:]), over(n1[:, 1, :], HD1), ALU.subtract).then_inc(*dve_f.step("g_cen"))
                dve.wait_ge(*pool_f.of("g_sq", i))
                dve.tensor_reduce(n1[:, 2, :], groups(sq1), AX_X, ALU.add).then_inc(*dve_f.step("g_ssq"))
                dve.wait_ge(*dve_f.of("g_ssq", i))
                dve.tensor_scalar(n1[:, 3, :], n1[:, 2, :], 1.0 / HD1, 1e-5, ALU.mult, ALU.add).then_inc(*dve_f.step("g_var"))
                dve.wait_ge(*dve_f.of("g_var", i))
                rsqrt(n1[:, 3, :], n1[:, 4, :], n1[:, 5, :], "g", i, dve_f)

            def first_max(i, k):
                dve.wait_ge(*act_s.of(f"sc{k}b", i))
                for t in range(3):
                    apart(dve, turns_dve)
                    dve.max(m8[:, k, t, :], w_s[:, k, t, :]).then_inc(*dve_s.step(f"m{k}t{t}"))
                dve.wait_ge(*dve_s.of(f"m{k}t2", i))
                dve.tensor_scalar(nmax[:, k, :], m8[:, k, :, 0], -1.0, None, ALU.mult).then_inc(*dve_s.step(f"m{k}n"))

            def topk(i, k):
                if i is None:
                    return
                dve.wait_ge(*act_s.of(f"e{k}", i))
                for r in range(ROUNDS):
                    if r:
                        for t in range(3):
                            dve.wait_ge(*dve_t.of(f"k{k}r{r - 1}r{t}", i))
                            apart(dve, turns_dve)
                            dve.max(m8[:, k, t, :], w_s[:, k, t, :]).then_inc(*dve_t.step(f"k{k}r{r}m{t}"))
                    for t in range(3):
                        if r:
                            dve.wait_ge(*dve_t.of(f"k{k}r{r}m{t}", i))
                        apart(dve, turns_dve)
                        dve.match_replace(w_s[:, k, t, :], m8[:, k, t, :], w_s[:, k, t, :], NEG)\
                           .then_inc(*dve_t.step(f"k{k}r{r}r{t}"))
                for t in range(3):
                    dve.wait_ge(*dve_t.of(f"k{k}r{ROUNDS - 1}r{t}", i))
                    dve.scalar_tensor_tensor(e_s[:, k, t, :], w_s[:, k, t, :], NEG_TEST, e_s[:, k, t, :], ALU.is_lt, ALU.mult)\
                       .then_inc(*dve_t.step(f"k{k}r{ROUNDS}p{t}"))

            def back_attended(i):
                dve.wait_ge(*pe_b.of("y1T", i))
                heads_out(ps_u, rec1, yn1, 2, HD1, dve_b, ("rec1", "yn1"), i)

            def back_norm(i):
                dve.wait_ge(*pe_b.of("proj1", i))
                dve.wait_ge(*pool_k.of("h2k", i))
                dve.tensor_tensor(h3[:].rearrange("p n c -> p (n c)"), ps_u[0:TP, 0:256], h2k[:].rearrange("p n c -> p (n c)"),
                                  ALU.add).then_inc(*dve_b.step("h3"))
                dve.wait_ge(*dve_b.of("h3", i))
                centre(h3, "r", i, dve_b)
                dve.tensor_tensor(hn3[:], cen[:], over(lnt[:, 4, :]), ALU.mult).then_inc(*dve_b.step("hn3"))
                dve.wait_ge(*dve_b.of("hn3", i))
                if not (isinstance(i, int) and i == 0):
                    dve.wait_ge(h_stored, 16 * i)
                dve.tensor_tensor(hsum[:], h3[:], hn3[:], ALU.add).then_inc(*dve_b.step("hsum"))

            def body(i, prev, done, after):
                if done is not None:
                    back_attended(done)
                topk(prev, 0)
                if done is not None:
                    back_norm(done)
                topk(prev, 1)
                topk(prev, 2)
                topk(prev, 3)
                attended(i)
                gates(i)
                topk(prev, 4)
                if after is not None:
                    norm_tok(after)
                topk(prev, 5)
                if after is not None:
                    roots0(after)
                mixed(i)
                norm_heads(i)
                topk(prev, 6)
                if after is not None:
                    parts0(after)
                topk(prev, 7)
                for k in range(CHUNKS):
                    first_max(i, k)

            norm_tok(0)
            roots0(0)
            parts0(0)
            body(0, None, None, 1)
            body(1, 0, None, 2)
            with dve.Fori(2, PAIRS - 1) as i:
                body(i, i - 1, i - 2, i + 1)
            body(PAIRS - 1, PAIRS - 2, PAIRS - 3, None)
            back_attended(PAIRS - 2)
            back_norm(PAIRS - 2)
            for k in range(CHUNKS):
                topk(PAIRS - 1, k)
            back_attended(PAIRS - 1)
            back_norm(PAIRS - 1)

            count = [0]

            def tail(ins):
                count[0] += 1
                ins.then_inc(tail_dve, 1)
                dve.wait_ge(tail_dve, count[0])

            dve.wait_ge(sel_loaded, 16)
            tail(dve.tensor_copy(tail_x, tail_w))
            for _ in range(CAP // 8):
                tail(dve.max(tail_8, tail_x))
                tail(dve.match_replace(tail_x, tail_8, tail_x, NEG))
            tail(dve.max(tail_8, tail_x))
            edge = tail_8[:, CAP % 8 - 1:CAP % 8]
            tail(dve.tensor_scalar(tail_gt, tail_x, edge, None, ALU.is_gt))
            tail(dve.tensor_scalar(tail_eq, tail_x, edge, None, ALU.is_equal))
            tail(dve.tensor_reduce(tail_n[:, 0:1], tail_gt, AX_X, ALU.add))
            tail(dve.tensor_scalar(tail_n[:, 1:2], tail_n[:, 0:1], -1.0, float(CAP % 8), ALU.mult, ALU.add))
            tail(dve.tensor_copy(tail_c[:, 0, :], tail_eq))
            shift, a = 1, 0
            while shift < T:
                tail(dve.tensor_copy(tail_c[:, 1 - a, 0:shift], tail_c[:, a, 0:shift]))
                tail(dve.tensor_tensor(tail_c[:, 1 - a, shift:T], tail_c[:, a, shift:T], tail_c[:, a, 0:T - shift], ALU.add))
                shift, a = 2 * shift, 1 - a
            tail(dve.scalar_tensor_tensor(tail_eq, tail_c[:, a, :], tail_n[:, 1:2], tail_eq, ALU.is_le, ALU.mult))
            tail(dve.tensor_tensor(tail_gt, tail_gt, tail_eq, ALU.add))
            tail(dve.scalar_tensor_tensor(tail_gt, tail_x, NEG_TEST, tail_gt, ALU.is_lt, ALU.add))
            tail(dve.tensor_tensor(tail_s, tail_gt, tail_w, ALU.mult))
            assert count[0] == TAIL_SELECTED, count[0]
            dve.wait_ge(tail_pe, 1)
            tail(dve.tensor_copy(wt.rearrange("p t b -> p (t b)"), ps_x[0:TP, 0:2 * B]))
            assert count[0] == TAIL_FIRST
            for n in range(PIECES):
                dve.wait_ge(piece_loaded[n % 2], 32 * (n // 2) + 32)
                for m in range(4):
                    w = wt[:, m // 2, :].rearrange("p (i u) -> p i u", u=2)[:, TAIL * n:TAIL * n + TAIL, m % 2]
                    y = fin_y[n % 2][:, :, m, :]
                    tail(dve.tensor_tensor(y, y, over(w), ALU.mult))
                    tail(dve.tensor_tensor(y, y, fin_h[n % 2][:, :, m, :], ALU.add))


POOL_CONSTANTS = 6
DVE_CONSTANTS = 36
TAIL_SELECTED = 1 + 2 * (CAP // 8) + 1 + 5 + 2 * 8 + 4
TAIL_FIRST = TAIL_SELECTED + 1

NAMES = ["x", "L0_tok_W_in", "L0_tok_b_in", "L0_tok_W_out", "L0_tok_b_out", "L0_tok_core_diag", "L0_tok_conv_filter",
         "L0_attn_w_qkv", "L0_attn_w_proj", "L0_attn_qn_w", "L0_attn_kn_w", "L0_ffn_gate_w", "L0_ffn_gate_b", "L0_ffn_w1",
         "L0_ffn_b1", "L0_ffn_w2", "L0_ffn_b2", "L0_ffn_gamma", "L0_ffn_beta", "L1_attn_qkv_w", "L1_attn_qkv_b",
         "L1_attn_q_gamma", "L1_attn_q_beta", "L1_attn_k_gamma", "L1_attn_k_beta", "L1_attn_proj_w", "L1_attn_proj_b",
         "L1_ffn_wr", "L1_ffn_br", "L1_ffn_w1", "L1_ffn_b1", "L1_ffn_w2", "L1_ffn_b2"]


def kernel(**inputs):
    import numpy as np
    import concourse.bacc as bacc
    from concourse.bass_utils import run_bass_kernel_spmd

    nc = bacc.Bacc("TRN2", target_bir_lowering=False, num_devices=1)
    arrays, dram = {}, {}
    for name in NAMES:
        a = np.ascontiguousarray(inputs[name])
        arrays["in_" + name] = a
        dram[name] = nc.dram_tensor("in_" + name, a.shape, mybir.dt.from_np(a.dtype), kind="ExternalInput").ap()
    out = nc.dram_tensor("out", (2 * PAIRS, T, D), F32, kind="ExternalOutput").ap()
    route = nc.dram_tensor("route", (PAIRS, 2 * T), F32, kind="Internal").ap()
    h3, ffy = (nc.dram_tensor(n, (PAIRS, TP, 4 * D), F32, kind="Internal").ap() for n in ("h3_rows", "ff_rows"))
    audio_tower(nc, dram, out, route, h3, ffy)
    return run_bass_kernel_spmd(nc, [arrays], core_ids=[0]).results[0]["out"]
```

```python
from contextlib import ExitStack

import concourse.bass as bass
from concourse import mybir

F32 = mybir.dt.float32
BF16 = mybir.dt.bfloat16
I32 = mybir.dt.int32
U32 = mybir.dt.uint32
ALU = mybir.AluOpType
ACT = mybir.ActivationFunctionType
AX_X = mybir.AxisListType.X

P = 128
PAIRS = 32
T_IN, D = 375, 64
XT = T_IN // 3
TAPS, PAD = 15, 7
T = 188
TP = T // 2
S1 = T - P
UNIT = T + S1
H0, HD0 = 32, 2
H1, HD1 = 8, 8
TERMS = 6
ROWS0 = TERMS * HD0 + 3
E, TOPK_E, F_E = 16, 2, 128
KEEP = int(T * 0.3)
ROUNDS = KEEP // 8
CAP = T // 2 - 1
NEG = -3.0e38
NEG_TEST = -1.0e38
RSQRT_MAGIC = 1597463007.0
SHIFT_ROOM = 80.0
EXP_AT = 3
CHUNKS = 8


class Steps:

    def __init__(self, sem, names):
        self.sem, self.names, self.next = sem, names, 0
        self.index = {n: k for k, n in enumerate(names)}
        assert len(self.index) == len(names)

    def step(self, name):
        assert self.names[self.next % len(self.names)] == name, (name, self.names[self.next % len(self.names)])
        self.next += 1
        return self.sem, 1

    def of(self, name, i):
        return self.sem, i * len(self.names) + (self.index[name] + 1)


def newton(x):
    return [f"{x}_guess"] + [f"{x}_n{r}{c}" for r in range(3) for c in "abc"]


def ln_steps(x):
    return [f"{x}_sum", f"{x}_cen", f"{x}_sq", f"{x}_ssq", f"{x}_var"] + newton(x)


PE_FIRST = ["xT", "tok0", "tok1", "tok2", "tok3", "conv", "hn0T", "qk0", "v0"] + [f"zT{f}" for f in range(8)]
ACT_FIRST = ["x0", "x1", "x2", "x2s", "x3", "x4", "h0", "hn0Tc", "qk0c", "qk0s", "v0c"]
ACT_FIRST += ["q1", "k1", "c1", "q2", "k2", "c2", "q3", "k3", "c3"]
ACT_FIRST += [f"zTc{f}" for f in range(8)]
DVE_FIRST = ln_steps("a") + ["hn0"] + ["b_guess", "qr", "qw", "qkp", "self", "negc"]
POOL_FIRST = ["ss", "sx"] + [f"rn{r}{c}" for r in range(3) for c in "abcd"] + ["rq1", "rk1", "rc1", "rq2", "rk2", "rc2"]
PE_FRONT = ([x for n in range(18) for x in ([f"sc{n}"] if n < 16 else []) + ([f"pv{n - 2}"] if n >= 2 else [])]
            + ["y0T", "yn0T", "proj0"]
            + ["hn1T", "gate", "gT"]
            + [x for e in range(E + 2) for x in ([f"z{e}"] if e < E else []) + ([f"o{e - 2}"] if e >= 2 else [])]
            + ["moeT", "hn2T", "qk1"] + [f"kqT{f}" for f in range(5)])
ACT_FRONT = ([f"ex{n}" for n in range(16)] + ["y0c", "yn0Tc"]
             + ["hn1Tc", "gexp", "gTc"] + [x for e in range(E) for x in (f"relu{e}", f"gc{e}")]
             + ["moec", "hn2Tc"] + [f"kqTc{f}" for f in range(5)])
DVE_FRONT = (["rec0", "yn0", "h1"] + ln_steps("c") + ["hn1"]
             + ["lg"] + [f"gm{t}" for t in range(4)] + [f"gi{t}" for t in range(4)]
             + ["gif", "gd", "g1p", "p1", "p2", "e1", "e2", "e1p", "e2p", "G", "G1", "Gr", "G2", "Gr2", "G3"]
             + ["ma", "mb"] + ln_steps("d") + ["dn", "dg", "h2"] + ln_steps("f") + ["hn2"]
             + ["qk1a", "qk1b", "g_sum", "g_cen", "g_ssq", "g_var"] + newton("g") + ["g_norm", "g_gam", "gk0", "gk1"])
POOL_FRONT = [f"sel{n}" for n in range(16)] + ["h1b"] + [f"hp{e}" for e in range(E)] + ["g_sq", "gq0", "gq1"]
PE_SCORE = [f"s{k}" for k in range(CHUNKS)] + ["v1"]
ACT_SCORE = ([x for k in range(CHUNKS) for x in [f"sc{k}a", f"sc{k}b"] + (["e0"] if k == EXP_AT else [])]
             + ["e1", "v1c"] + [f"e{k}" for k in range(2, CHUNKS)])
DVE_SCORE = [f"m{k}{x}" for k in range(CHUNKS) for x in ("t0", "t1", "t2", "n")]
DVE_TOPK = [x for k in range(CHUNKS)
            for x in [f"k{k}r{r}{c}{t}" for r in range(ROUNDS) for c in ("mr" if r else "r") for t in range(3)] + [f"kept{k}"]]
PE_BACK = ([f"{x}{k}" for k in range(CHUNKS) for x in ("pt0_", "pt1_", "pv")]
           + ["y1T", "yn1T", "proj1", "h3T", "route", "ffz0", "ffz1", "ffo", "ffT"])
ACT_BACK = ([f"{x}{k}" for k in range(CHUNKS) for x in ("pc0_", "pc1_")]
            + ["y1c", "yn1Tc", "h3Tc", "routec", "gelu0", "gelu1", "ffoc", "ffTc"])
DVE_BACK = ["rec1", "yn1", "h3"] + ln_steps("r") + ["hn3", "hsum"]
POOL_KEEP = ["h2k"]

FIRST_XT, FIRST_DENSE, FIRST_TOK3, FIRST_CONV, FIRST_HN0T, FIRST_QK0, FIRST_V0 = 0, (1, 2, 3), 4, 5, 10, 11, 13
FIRST_SQUARES = 12
PARTS_AT = (0, 2)
ROWS_AT = 4
BACK_Y1T, BACK_YN1T, BACK_PROJ1, BACK_H3T, BACK_ROUTE, BACK_FFZ1, BACK_FFO, BACK_FFT = 0, 4, 5, 11, 12, 13, 14, 15


def audio_tower(nc, dram, out, route_dram, h_dram, y_dram):
    with ExitStack() as ctx:
        def sb(name, shape, dt=F32):
            return ctx.enter_context(nc.sbuf_tensor(name, shape, dt))

        def ps(name, shape, dt=F32):
            return ctx.enter_context(nc.psum_tensor(name, shape, dt))

        def sem(name):
            return ctx.enter_context(nc.semaphore(name))

        ident = sb("ident", [P, P])
        ident_b = sb("ident_b", [P, P], BF16)
        ones = sb("ones", [1, P])
        tok_w = sb("tok_w", [P, 4, P])
        tok_b = sb("tok_b", [P, 3])
        core = sb("core", [P, 1])
        core_abs = sb("core_abs", [P, 1])
        tok_brow = sb("tok_brow", [1, 2, D])
        taps = sb("taps", [XT, TAPS])
        toeplitz = sb("toeplitz", [XT, 3, T])
        w_qkv0 = sb("w_qkv0", [P, 3, 2, D])
        w_qkv1 = sb("w_qkv1", [P, 3, 2, D])
        w_proj = sb("w_proj", [P, 2, 2, D])
        rms_raw = sb("rms_raw", [TP, 2, 2])
        rms_w = sb("rms_w", [TP, 2, P])
        wprod = sb("wprod", [TP, 2])
        room = sb("room", [TP, 1])
        gate_w = sb("gate_w", [D, E])
        gate_b = sb("gate_b", [TP, E])
        w1e = sb("w1e", [D, E, F_E])
        w2e = sb("w2e", [F_E, E, D])
        b1e = sb("b1e", [F_E, E])
        b2raw = sb("b2raw", [3 * E, D])
        b2res = sb("b2res", [3 * E, 2, D])
        b2e = sb("b2e", [3 * E, 3, D], BF16)
        pick = sb("pick", [3 * E, E, P], BF16)
        expert_id = sb("expert_id", [TP, 4, E])
        ln_gb = sb("ln_gb", [TP, 2, D])
        brow1 = sb("brow1", [1, 3, 2, D])
        bqk1 = sb("bqk1", [TP, 2, D])
        gb_raw = sb("gb_raw", [TP, 4, HD1])
        gam1 = sb("gam1", [TP, 2, P])
        bet1 = sb("bet1", [TP, 2, P])
        projb1 = sb("projb1", [1, 2, D])
        wr = sb("wr", [D, 1])
        br = sb("br", [1, 1])
        fw1 = sb("fw1", [D, 2, P])
        fb1 = sb("fb1", [P, 2])
        fw2 = sb("fw2", [P, 2, D])
        fb2 = sb("fb2", [P, 1])

        x_in = sb("x_in", [XT, 3, 2, D])
        gh = sb("gh", [P, 2, 2 * T])
        x0, x1 = gh[:, 0, 0:T_IN], gh[:, 1, 0:T_IN]
        x2 = sb("x2", [P, T_IN])
        x2s, x3 = x0, x1
        x4 = sb("x4", [XT, 3, P])
        h0 = sb("h0", [TP, 4, D])
        h1 = sb("h1", [TP, 4, D])
        h2 = sb("h2", [TP, 4, D])
        h2k = sb("h2k", [TP, 4, D])
        h3 = sb("h3", [TP, 4, D])
        hn3 = sb("hn3", [TP, 4, D])
        hsum = sb("hsum", [TP, 4, D])
        cen = sb("cen", [TP, 4, D])
        sq = sb("sq", [TP, 4, D])
        lnt = sb("lnt", [TP, 6, 4])
        hn0 = sb("hn0", [TP, 4, D])
        hn1 = sb("hn1", [TP, 4, D])
        hn2 = sb("hn2", [TP, 4, D])
        hn0T = sb("hn0T", [P, T])
        hn1T = sb("hn1T", [D, 2 * T])
        hn2T = sb("hn2T", [P, T])
        qk0 = sb("qk0", [TP, 2, 2, P])
        qk0s = sb("qk0s", [TP, 2, 2, P])
        rx = sb("rx", [TP, 256])
        rr = sb("rr", [TP, 256])
        rt = sb("rt", [TP, 256])
        selfp = rt
        selfs = sb("selfs", [TP, P])
        negc = sb("negc", [TP, P])
        hrg = sb("hrg", [P, 2, 2, 2 * T])
        hr, hg = hrg[:, 0], hrg[:, 1]
        resc = sb("resc", [TP, 2, P])
        zq = sb("zq", [TP, P, 32], BF16)
        zk = sb("zk", [TP, P, 32], BF16)
        qT0 = sb("qT0", [P, 2, 8, T], BF16)
        kT0 = sb("kT0", [P, 2, 8, T], BF16)
        e0 = sb("e0", [P, 2, 4, UNIT])
        res = e0[0:TP].rearrange("p a b c -> p (a b c)")[:, 0:1024].rearrange("p (r s c) -> p r s c", r=2, s=2)
        vp0 = [sb(f"vp0{m}", [P, 2, 1048]) for m in range(2)]
        y0 = sb("y0", [P, 2 * T])
        rec = sb("rec", [TP, 16, 8])
        yn = sb("yn", [TP, 4, D])
        ynT = sb("ynT", [P, T])
        lg = sb("lg", [TP, 4, E])
        gm = sb("gm", [TP, 4, 8])
        gi = sb("gi", [TP, 4, 8], U32)
        gif = sb("gif", [TP, 4, 2])
        gs = sb("gs", [TP, 5, 4])
        ge = sb("ge", [TP, 4, 4, E])
        gg = sb("gg", [TP, 3, 4, E])
        g3 = sb("g3", [TP, 4, 3, E], BF16)
        gT = sb("gT", [3 * E, 2 * T], BF16)
        hp = sb("hp", [P, 2, 2 * T])
        moe = y0
        my = mn = yn

        qk1 = sb("qk1", [TP, 2, 4, D])
        c1, sq1 = (hrg[0:TP].rearrange("p a b c -> p (a b c)")[:, 512 * n:512 * n + 512]
                   .rearrange("p (k n c) -> p k n c", k=2, n=4) for n in range(2))
        n1 = sb("n1", [TP, 6, 64])
        zq1 = sb("zq1", [TP, 4, 2, D])
        zk1 = sb("zk1", [TP, 4, 8 * D + 64])
        qT1 = sb("qT1", [P, 2, T])
        kT1 = sb("kT1", [P, 2, 4, T])
        w_s = sb("w_s", [P, CHUNKS, 3, T])
        e_s = sb("e_s", [P, CHUNKS, 3, T])
        m8 = sb("m8", [P, CHUNKS, 3, 8])
        nmax = sb("nmax", [P, CHUNKS, 3])
        vp1 = [sb(f"vp1{m}", [P, 2, 274]) for m in range(2)]
        pt = [sb("pt0", [P, T + D + P]), sb("pt1", [S1, T + D + P])]
        y1 = y0
        rec1 = sb("rec1", [TP, 16, 2])
        yn1 = yn
        yn1T = sb("yn1T", [P, T])
        h3T = sb("h3T", [D, 2 * T])
        rw = sb("rw", [1, 2 * T])
        ffo = sb("ffo", [P, T])
        ffy = sb("ffy", [TP, 4, D])

        def part(tile, at, rows, shape):
            n = 1
            for k in shape:
                n *= k
            flat = tile[0:rows].rearrange("p k a t -> p (k a t)")[:, at:at + n]
            if len(shape) == 1:
                return flat
            names = "abcd"[:len(shape)]
            return flat.rearrange(f"p ({' '.join(names)}) -> p {' '.join(names)}", **dict(zip(names[1:], shape[1:])))

        tap_mask = part(w_s, 0, XT, [2, 3, T])
        nat0 = part(w_s, 6 * T, 96, [2, 2, D])
        nat1 = part(w_s, 6 * T + 256, 96, [2, 2, D])
        natp = part(w_s, 6 * T + 512, D, [2, 2, D])

        B = 2 * PAIRS
        tail_w, tail_x, tail_gt, tail_eq, tail_s = (part(w_s, n * T, B, [T]) for n in range(5))
        tail_c = part(w_s, 5 * T, B, [2, T])
        tail_8 = part(w_s, 7 * T, B, [8])
        tail_n = part(w_s, 7 * T + 8, B, [2])
        wt = part(w_s, 8 * T, TP, [2, B])
        TAIL = min(PAIRS, 8)
        PIECES = PAIRS // TAIL
        fin_y = [part(e_s, 2048 * n, TP, [TAIL, 4, D]) for n in range(2)]
        fin_h = [part(w_s, 12 * T, TP, [TAIL, 4, D]),
                 zq[:].rearrange("p h r -> p (h r)").bitcast(F32)[:, 0:TAIL * 256].rearrange("p (i n c) -> p i n c", i=TAIL, n=4)]

        ps_s = [ps(f"ps_s{n}", [P, 2, 512]) for n in range(2)]
        ps_x = ps("ps_x", [P, 512])
        ps_y = ps("ps_y", [P, 512])
        ps_u = ps("ps_u", [P, 512])
        ps_v = ps("ps_v", [P, 512])

        def bank(n):
            return ps_s[n // 2][:, n % 2, :]

        loaded = sem("weights_loaded")
        zeroed = sem("weight_tiles_zeroed")
        const_pool = sem("pool_constants")
        const_dve = sem("vector_constants")
        const_pe = sem("weights_transposed")
        const_act = sem("weights_copied")
        tap_done = sem("tap_added")
        tap_made = sem("tap_mask_made")
        x_loaded = sem("x_loaded")
        routed = sem("router_rows_stored")
        h_stored = sem("h_stored")
        y_stored = sem("y_stored")
        piece_loaded = [sem("even_last_pieces_loaded"), sem("odd_last_pieces_loaded")]
        sel_loaded = sem("router_rows_loaded")
        tail_dve = sem("tail_vector")
        tail_pe = sem("tail_transposed")
        stored = sem("output_stored")
        pe_a = Steps(sem("pe_first"), PE_FIRST)
        act_a = Steps(sem("act_first"), ACT_FIRST)
        dve_a = Steps(sem("vector_first"), DVE_FIRST)
        pool_a = Steps(sem("pool_first"), POOL_FIRST)
        pe_f = Steps(sem("pe_front"), PE_FRONT)
        act_f = Steps(sem("act_front"), ACT_FRONT)
        dve_f = Steps(sem("vector_front"), DVE_FRONT)
        pool_f = Steps(sem("pool_front"), POOL_FRONT)
        pe_s = Steps(sem("pe_scores"), PE_SCORE)
        act_s = Steps(sem("act_scores"), ACT_SCORE)
        dve_s = Steps(sem("vector_first_max"), DVE_SCORE)
        dve_t = Steps(sem("vector_topk"), DVE_TOPK)
        pe_b = Steps(sem("pe_back"), PE_BACK)
        act_b = Steps(sem("act_back"), ACT_BACK)
        dve_b = Steps(sem("vector_back"), DVE_BACK)
        pool_k = Steps(sem("pool_kept_h2"), POOL_KEEP)

        def before(eng, steps, name, i):
            if isinstance(i, int) and i == 0:
                return
            eng.wait_ge(*steps.of(name, i - 1))

        turns_pe, turns_dve, turns_pool = sem("pe_turns"), sem("vector_turns"), sem("pool_turns")

        def apart(eng, turns):
            eng.sem_inc(turns, 1)

        def v_view(t, u, step, parts, d0, d1):
            nj = {131: 8, 137: 2}[step]
            return (t[0:parts, u, 0:nj * step].rearrange("p (j x) -> p j x", x=step)[:, :, 0:P]
                    .rearrange("p j (g y) -> p j g y", y=32)[:, :, :, d0:d1])

        block = ctx.enter_context(nc.Block())

        weight_loads = []

        @block.sync
        def _(sp):
            sp.wait_ge(zeroed, 1)

            def load(dst, src):
                sp.dma_start(dst, src).then_inc(loaded, 16)
                weight_loads.append(1)

            with nc.allow_non_contiguous_dma("weights, once"):
                for u in range(2):
                    half = slice(D * u, D * u + D)
                    load(tok_w[half, 0:2, half], dram["L0_tok_W_in"].rearrange("n c m -> c n m"))
                    load(tok_w[half, 2, half], dram["L0_tok_W_out"][1])
                    load(tok_w[half, 3, half], dram["L0_tok_W_out"][0])
                    load(tok_b[half, 0:2], dram["L0_tok_b_in"].rearrange("n c -> c n"))
                    load(tok_b[half, 2:3], dram["L0_tok_b_out"][1:2].rearrange("n c -> c n"))
                    load(core[half, :], dram["L0_tok_core_diag"].rearrange("(c a) -> c a", a=1))
                    load(tok_brow[:, u, :], dram["L0_tok_b_out"][0:1])
                    load(nat0[:, :, u, :], dram["L0_attn_w_qkv"].rearrange("(t r) c -> r t c", r=96))
                    load(nat1[:, :, u, :], dram["L1_attn_qkv_w"].rearrange("(t r) c -> r t c", r=96))
                    for a in range(2):
                        for b in range(2):
                            for gq in range(2):
                                load(natp[:, 0, u, :].rearrange("r (c jp gh d) -> r c gh jp d", c=4, gh=2, d=2)[:, 2 * b + a, gq],
                                     dram["L0_attn_w_proj"].rearrange("r (jp a gh b d) -> r a gh b jp d", a=2, gh=2, b=2, d=2)[:, a, gq, b])
                    for g in range(4):
                        load(natp[:, 1, u, :].rearrange("r (g j d) -> r g j d", g=4, j=2)[:, g],
                             dram["L1_attn_proj_w"].rearrange("r (j g d) -> r g j d", g=4, j=2)[:, g])
                    load(brow1[:, :, u, :], dram["L1_attn_qkv_b"].rearrange("(a k c) -> a k c", a=1, k=3))
                    load(projb1[:, u, :], dram["L1_attn_proj_b"].rearrange("(a c) -> a c", a=1))
                    load(fb2[half, :], dram["L1_ffn_b2"].rearrange("(c a) -> c a", a=1))
                load(bqk1[:].rearrange("p k c -> p (k c)"), dram["L1_attn_qkv_b"][0:2 * D].partition_broadcast(TP))
                load(gate_w[:], dram["L0_ffn_gate_w"])
                load(gate_b[:], dram["L0_ffn_gate_b"].partition_broadcast(TP))
                load(w1e[:], dram["L0_ffn_w1"].rearrange("e c f -> c e f"))
                load(wr[:], dram["L1_ffn_wr"])
                load(br[:], dram["L1_ffn_br"].rearrange("(a c) -> a c", a=1))
                load(fw1[:], dram["L1_ffn_w1"].rearrange("c (h f) -> c h f", h=2))
                for s in range(3):
                    load(b2raw[E * s:E * s + E, :], dram["L0_ffn_b2"])
                load(w2e[:], dram["L0_ffn_w2"].rearrange("e f c -> f e c"))
                load(b1e[:], dram["L0_ffn_b1"].rearrange("e f -> f e"))
                load(fw2[:], dram["L1_ffn_w2"].rearrange("(h f) c -> f h c", h=2))
                load(fb1[:], dram["L1_ffn_b1"].rearrange("(h f) -> f h", h=2))
                load(taps[:], dram["L0_tok_conv_filter"].partition_broadcast(XT))
                load(rms_raw[:, 0, :], dram["L0_attn_qn_w"].partition_broadcast(TP))
                load(rms_raw[:, 1, :], dram["L0_attn_kn_w"].partition_broadcast(TP))
                load(ln_gb[:, 0, :], dram["L0_ffn_gamma"].partition_broadcast(TP))
                load(ln_gb[:, 1, :], dram["L0_ffn_beta"].partition_broadcast(TP))
                for n, name in enumerate(("q_gamma", "k_gamma", "q_beta", "k_beta")):
                    load(gb_raw[:, n, :], dram["L1_attn_" + name].partition_broadcast(TP))

            x_pairs = dram["x"].rearrange("(i u) (j p) c -> i u p j c", u=2, p=XT)

            def load_x(i):
                before(sp, pe_a, "xT", i)
                for u in range(2):
                    sp.dma_start(x_in[:, :, u, :], x_pairs[bass.ds(i, 1), u].rearrange("a p j c -> p (a j) c"))\
                      .then_inc(x_loaded, 16)

            def store_route(i):
                sp.wait_ge(*act_b.of("routec", i))
                sp.dma_start(route_dram[bass.ds(i, 1)], rw[:]).then_inc(routed, 16)
                sp.wait_ge(*dve_b.of("hsum", i))
                sp.dma_start(h_dram[bass.ds(i, 1)].rearrange("a p c -> p (a c)"), hsum[:].rearrange("p n c -> p (n c)"))\
                  .then_inc(h_stored, 16)
                sp.wait_ge(*act_b.of("ffTc", i))
                sp.dma_start(y_dram[bass.ds(i, 1)].rearrange("a p c -> p (a c)"), ffy[:].rearrange("p n c -> p (n c)"))\
                  .then_inc(y_stored, 16)

            for i in range(3):
                load_x(i)
            with sp.Fori(3, PAIRS) as i:
                load_x(i)
                store_route(i - 3)
            for i in range(PAIRS - 3, PAIRS):
                store_route(i)
            sp.wait_ge(routed, 16 * PAIRS)
            sp.wait_ge(h_stored, 16 * PAIRS)
            sp.wait_ge(y_stored, 16 * PAIRS)
            sp.wait_ge(*dve_t.of(f"kept{CHUNKS - 1}", PAIRS - 1))
            sp.wait_ge(*pe_b.of(f"pt1_{CHUNKS - 1}", PAIRS - 1))
            sp.dma_start(tail_w, route_dram.rearrange("i (u t) -> (i u) t", u=2)).then_inc(sel_loaded, 16)

            def load_piece(n):
                if n >= 2:
                    sp.wait_ge(stored, 64 * (n - 1))
                    sp.wait_ge(tail_dve, TAIL_FIRST + 8 * (n - 1))
                rows = slice(TAIL * n, TAIL * n + TAIL)
                sp.dma_start(fin_y[n % 2], y_dram[rows].rearrange("i p (n c) -> p i n c", n=4)).then_inc(piece_loaded[n % 2], 16)
                sp.dma_start(fin_h[n % 2], h_dram[rows].rearrange("i p (n c) -> p i n c", n=4)).then_inc(piece_loaded[n % 2], 16)

            out_v = out.rearrange("(i u) (t p) c -> t u p i c", u=2, p=TP)
            load_piece(0)
            if PIECES > 1:
                load_piece(1)
            for n in range(PIECES):
                sp.wait_ge(tail_dve, TAIL_FIRST + 8 * n + 8)
                for m in range(4):
                    sp.dma_start(out_v[m // 2, m % 2, :, TAIL * n:TAIL * n + TAIL, :], fin_y[n % 2][:, :, m, :]).then_inc(stored, 16)
                if n + 2 < PIECES:
                    load_piece(n + 2)
            sp.wait_ge(stored, 64 * PIECES)

        n_loads = 16 * len(weight_loads)

        @block.tensor
        def _(pe):
            pe.wait_ge(loaded, n_loads)
            pe.wait_ge(const_pool, 1)
            for n, nat in enumerate((nat0, nat1)):
                for t in range(2):
                    pe.transpose(ps_x[:, 192 * n + 96 * t:192 * n + 96 * t + 96],
                                 nat[:, t].rearrange("r u c -> r (u c)"), ident[0:96, 0:96])
            for n in range(2):
                last = pe.transpose(ps_x[:, 384 + D * n:384 + D * n + D],
                                    natp[:, n].rearrange("r u c -> r (u c)"), ident[0:D, 0:D])
            last.then_inc(const_pe, 1)
            pe.wait_ge(const_pool, POOL_CONSTANTS)
            pe.wait_ge(const_dve, DVE_CONSTANTS)
            pe.wait_ge(const_act, 1)

            def first_xT(i):
                pe.wait_ge(x_loaded, 32 * i + 32)
                for j in range(3):
                    last = pe.transpose(ps_x[:, XT * j:XT * j + XT], x_in[:, j].rearrange("p u c -> p (u c)"),
                                        ident[0:XT, 0:XT])
                last.then_inc(*pe_a.step("xT"))

            def first_dense(i, n):
                name, rhs = (("x0", x0), ("x1", x1), ("x2s", x2s))[n]
                pe.wait_ge(*act_a.of(name, i))
                pe.matmul(ps_x[:, 0:T_IN], tok_w[:, n, :], rhs, start=True, stop=True).then_inc(*pe_a.step(f"tok{n}"))

            def first_tok3(i):
                pe.wait_ge(*act_a.of("x3", i))
                for j in range(3):
                    o = ps_x[0:XT, P * j:P * j + P]
                    pe.matmul(o, x3[:, XT * j:XT * j + XT], tok_w[:, 3, :], start=True, stop=False)
                    last = pe.matmul(o, ones[:, 0:XT], tok_brow[:].rearrange("a u c -> a (u c)"), start=False, stop=True)
                last.then_inc(*pe_a.step("tok3"))

            def first_conv(i):
                pe.wait_ge(*act_a.of("x4", i))
                for t in range(2):
                    for j in range(2):
                        last = pe.matmul(ps_x[0:TP, P * t:P * t + P], toeplitz[:, t + j, TP * t:TP * t + TP],
                                         x4[:, t + j, :], start=(j == 0), stop=(j == 1))
                last.then_inc(*pe_a.step("conv"))

            def first_hn0T(i):
                pe.wait_ge(*dve_a.of("hn0", i))
                to_features(hn0, ps_u).then_inc(*pe_a.step("hn0T"))

            def first_qk0(i):
                pe.wait_ge(*act_a.of("hn0Tc", i))
                for t in range(2):
                    last = pe.matmul(ps_u[0:TP, 256 * t:256 * t + 256], hn0T[:, TP * t:TP * t + TP],
                                     w_qkv0[:, 0:2].rearrange("p k u c -> p (k u c)"), start=True, stop=True)
                last.then_inc(*pe_a.step("qk0"))

            def first_v0(i):
                pe.wait_ge(*act_a.of("qk0s", i))
                w_v = w_qkv0[:, 2].rearrange("p u c -> p (u c)")
                pe.matmul(ps_u[:, 0:P], hn0T[:, 0:P], w_v, start=True, stop=True)
                pe.matmul(ps_u[0:S1, P:2 * P], hn0T[:, P:T], w_v, start=True, stop=True)\
                  .then_inc(*pe_a.step("v0"))

            def first(i, e):
                if i is None:
                    return
                if e == FIRST_XT:
                    first_xT(i)
                elif e in FIRST_DENSE:
                    first_dense(i, FIRST_DENSE.index(e))
                elif e == FIRST_TOK3:
                    first_tok3(i)
                elif e == FIRST_CONV:
                    first_conv(i)
                elif e == FIRST_HN0T:
                    first_hn0T(i)
                elif e == FIRST_QK0:
                    first_qk0(i)
                elif e == FIRST_V0:
                    first_v0(i)

            def rows0(i, f):
                side, u, half = f // 4, f // 2 % 2, f % 2
                if f == 0:
                    pe.wait_ge(*act_a.of("c3", i))
                if f >= 2:
                    pe.wait_ge(*act_a.of(f"zTc{f - 2}", i))
                o = (ps_x, ps_y)[f % 2][:].bitcast(BF16)
                z = (zq, zk)[side][:].rearrange("p (n j y) r -> p n j (y r)", n=4, y=4)
                for j in range(4):
                    for t in range(2):
                        c = T * j + TP * t
                        last = pe.transpose(o[:, c:c + TP], z[:, 2 * t + u, 4 * half + j, :], ident_b[0:TP, 0:TP])
                last.then_inc(*pe_a.step(f"zT{f}"))

            def attention0(i, done):
                pe.wait_ge(*act_a.of("zTc7", i))
                before(pe, act_s, f"sc{CHUNKS - 1}b", i)

                def scores(n):
                    u, m = n // 8, n % 8
                    if n >= 2:
                        pe.wait_ge(*act_f.of(f"ex{n - 2}", i))
                    for b in range(2):
                        o = ps_s[n % 2][:, b, :]
                        g = 2 * (m % 2) + b
                        rows = slice(32 * g, 32 * g + ROWS0)
                        for a in range(2):
                            j = 2 * (m // 2) + a
                            pe.matmul(o[:, UNIT * a:UNIT * a + T], kT0[rows, u, j, 0:P], qT0[rows, u, j, :],
                                      start=True, stop=True)
                            last = pe.matmul(o[0:S1, UNIT * a + T:UNIT * a + UNIT], kT0[rows, u, j, P:T],
                                             qT0[rows, u, j, P:T], start=True, stop=True)
                    last.then_inc(*pe_f.step(f"sc{n}"))

                def values(n):
                    u, m = n // 8, n % 8
                    pe.wait_ge(*pool_f.of(f"sel{n}", i))
                    for c in range(4):
                        w = slice(32 * (4 * m + c), 32 * (4 * m + c) + 32)
                        pe.matmul(ps_y[32 * c:32 * c + 32, T * u:T * u + T], vp0[0][:, u, w], e0[:, n % 2, c, 0:T],
                                  start=(m == 0), stop=False, skip_group_check=True)
                    for c in range(4):
                        w = slice(32 * (4 * m + c), 32 * (4 * m + c) + 32)
                        last = pe.matmul(ps_y[32 * c:32 * c + 32, T * u + P:T * u + T], vp0[1][0:S1, u, w],
                                         e0[0:S1, n % 2, c, T:UNIT], start=False, stop=(m == 7), skip_group_check=True)
                    last.then_inc(*pe_f.step(f"pv{n}"))

                for n in range(18):
                    if n < 16:
                        scores(n)
                    if n >= 2:
                        values(n - 2)
                    if done is not None:
                        back(done, n)

            def middle(i, prev):
                before(pe, act_s, "v1c", i)
                pe.wait_ge(*act_f.of("y0c", i))
                to_tokens(y0, ps_x).then_inc(*pe_f.step("y0T"))
                pe.wait_ge(*dve_f.of("yn0", i))
                to_features(yn, ps_x).then_inc(*pe_f.step("yn0T"))
                pe.wait_ge(*act_f.of("yn0Tc", i))
                for t in range(2):
                    last = pe.matmul(ps_x[0:TP, P * t:P * t + P], ynT[:, TP * t:TP * t + TP],
                                     w_proj[:, 0].rearrange("p u c -> p (u c)"), start=True, stop=True)
                last.then_inc(*pe_f.step("proj0"))
                values1(prev, 0)
                values1(prev, 1)
                pe.wait_ge(*dve_f.of("hn1", i))
                apart(pe, turns_pe)
                to_features64(hn1, ps_x).then_inc(*pe_f.step("hn1T"))
                pe.wait_ge(*act_f.of("hn1Tc", i))
                for n in range(4):
                    t, u = n // 2, n % 2
                    o = ps_x[0:TP, E * n:E * n + E]
                    last = pe.matmul(o, hn1T[:, T * u + TP * t:T * u + TP * t + TP], gate_w[:], start=True, stop=True)
                last.then_inc(*pe_f.step("gate"))
                values1(prev, 2)
                pe.wait_ge(*dve_f.of("G3", i))
                apart(pe, turns_pe)
                o = ps_x[:].bitcast(BF16)
                for n in range(4):
                    t, u = n // 2, n % 2
                    last = pe.transpose(o[0:3 * E, T * u + TP * t:T * u + TP * t + TP],
                                        g3[:, n].rearrange("p s e -> p (s e)"), ident_b[0:TP, 0:TP])
                last.then_inc(*pe_f.step("gT"))
                pe.wait_ge(*act_f.of("gTc", i))

            def experts(i, after):
                def up(e):
                    if e >= 2:
                        pe.wait_ge(*act_f.of(f"gc{e - 2}", i))
                    pe.matmul(bank(e % 2)[:, 0:2 * T], w1e[:, e, :], hn1T[:], start=True, stop=True)
                    pe.matmul(bank(2 + e % 2)[:, 0:2 * T], pick[:, e, :], gT[:], start=True, stop=True)\
                      .then_inc(*pe_f.step(f"z{e}"))

                def down(e):
                    if e == 0:
                        for s in range(3):
                            pe.matmul(ps_y[0:D, 0:2 * T], b2e[:, s, :], gT[:], start=(s == 0), stop=False,
                                      skip_group_check=True)
                    pe.wait_ge(*pool_f.of(f"hp{e}", i))
                    r = D * (e % 2)
                    pe.matmul(ps_y[r:r + D, 0:2 * T], w2e[:, e, :], hp[:, e % 2, :], start=(e == 1), stop=(e >= E - 2),
                              skip_group_check=True).then_inc(*pe_f.step(f"o{e}"))

                for e in range(E + 2):
                    if e < E:
                        up(e)
                    if e >= 2:
                        down(e - 2)
                    first(after, e)

            def rest(i, prev, after):
                if after is not None:
                    pe.wait_ge(*act_a.of("h0", after))
                pe.wait_ge(*act_f.of("moec", i))
                to_tokens(moe, ps_x).then_inc(*pe_f.step("moeT"))
                if after is not None:
                    pe.wait_ge(*act_a.of("v0c", after))
                values1(prev, 3)
                values1(prev, 4)
                pe.wait_ge(*dve_f.of("hn2", i))
                to_features(hn2, ps_x).then_inc(*pe_f.step("hn2T"))
                pe.wait_ge(*act_f.of("hn2Tc", i))
                for t in range(2):
                    o = ps_x[0:TP, 256 * t:256 * t + 256]
                    last = pe.matmul(o, hn2T[:, TP * t:TP * t + TP], w_qkv1[:, 0:2].rearrange("p k u c -> p (k u c)"),
                                     start=True, stop=True)
                last.then_inc(*pe_f.step("qk1"))
                values1(prev, 5)
                pe.wait_ge(*act_f.of(f"gc{E - 1}", i))
                pe.wait_ge(*dve_f.of("gk1", i))
                for f in range(5):
                    if f == 4:
                        pe.wait_ge(*pool_f.of("gq1", i))
                        pe.wait_ge(*act_f.of("kqTc0", i))
                    for a in range(2):
                        for t in range(2):
                            if f < 4:
                                u, p = f // 2, 2 * (f % 2) + a
                                src = zk1[:, 2 * t + u, P * p:P * p + P]
                            else:
                                u = a
                                src = zq1[:, 2 * t + u].rearrange("p n c -> p (n c)")
                            c = T * a + TP * t
                            last = pe.transpose(bank(f % 4)[:, c:c + TP], src, ident[0:TP, 0:TP])
                    last.then_inc(*pe_f.step(f"kqT{f}"))
                pe.wait_ge(*act_f.of("kqTc4", i))

            def to_features(src, dst):
                for t in range(2):
                    last = pe.transpose(dst[:, TP * t:TP * t + TP], src[:, 2 * t:2 * t + 2].rearrange("p u c -> p (u c)"),
                                        ident[0:TP, 0:TP])
                return last

            def to_features64(src, dst):
                for n in range(4):
                    t, u = n // 2, n % 2
                    last = pe.transpose(dst[0:D, T * u + TP * t:T * u + TP * t + TP], src[:, n, :], ident[0:TP, 0:TP])
                return last

            def to_tokens(src, dst):
                for n in range(4):
                    t, u = n // 2, n % 2
                    last = pe.transpose(dst[0:TP, P * n:P * n + P], src[:, T * u + TP * t:T * u + TP * t + TP], ident[:])
                return last

            def scores1(i, k):
                u, p = k // 4, k % 4
                if k >= 2:
                    pe.wait_ge(*act_s.of(f"sc{k - 2}b", i))
                o = ps_s[k % 2]
                for a in range(2):
                    half = slice(D * a, D * a + D)
                    pe.matmul(o[:, a, 0:T], qT1[half, u, 0:P], kT1[half, u, p, :], start=True, stop=True)
                for a in range(2):
                    half = slice(D * a, D * a + D)
                    last = pe.matmul(o[half, a, T:2 * T], qT1[half, u, T - D:T], kT1[half, u, p, :], start=True, stop=True)
                last.then_inc(*pe_s.step(f"s{k}"))

            def values1(i, k):
                if i is None:
                    return
                u, p = k // 4, k % 4
                pe.wait_ge(*dve_t.of(f"kept{k}", i))
                if k:
                    pe.wait_ge(*act_b.of(f"pc1_{k - 1}", i))
                else:
                    before(pe, act_b, "ffTc", i)
                for m, (m0, m1) in enumerate(((0, P), (P, T))):
                    if m:
                        pe.wait_ge(*act_b.of(f"pc0_{k}", i))
                        apart(pe, turns_pe)
                    pe.transpose(ps_u[0:m1 - m0, T - D:T + D], e_s[:, k, 2, m0:m1], ident[:])
                    pe.transpose(ps_u[0:m1 - m0, 0:P], e_s[:, k, 0, m0:m1], ident[:])
                    last = pe.transpose(ps_u[0:m1 - m0, T + D:T + D + P], e_s[:, k, 1, m0:m1], ident[:])
                    last.then_inc(*pe_b.step(f"pt{m}_{k}"))
                pe.wait_ge(*act_b.of(f"pc1_{k}", i))
                for a in range(2):
                    h = 2 * p + a
                    g, j = h % 4, h // 4
                    pieces = ((T + D, 0, P), (T + D - S1, P, T)) if a else ((0, 0, T),)
                    for m, rows in enumerate((P, S1)):
                        for at, n0, n1 in pieces:
                            last = pe.matmul(ps_v[32 * g:32 * g + 32, T * u + n0:T * u + n1], vp1[m][0:rows, u, 32 * h:32 * h + 32],
                                             pt[m][0:rows, at:at + n1 - n0], start=(j == 0 and m == 0 and n0 == 0),
                                             stop=(j == 1 and m == 1), skip_group_check=True)
                last.then_inc(*pe_b.step(f"pv{k}"))

            def v1(i):
                pe.wait_ge(*dve_f.of("qk1b", i))
                w_v, b_v = (w[:, 2].rearrange("p u c -> p (u c)") for w in (w_qkv1, brow1))
                for o, c, n in ((ps_x[:, 0:P], slice(0, P), P), (ps_x[0:S1, P:2 * P], slice(P, T), S1)):
                    pe.matmul(o, hn2T[:, c], w_v, start=True, stop=False)
                    last = pe.matmul(o, ones[:, 0:n], b_v, start=False, stop=True)
                last.then_inc(*pe_s.step("v1"))

            def back_y1T(i):
                pe.wait_ge(*act_b.of("y1c", i))
                to_tokens(y1, ps_u).then_inc(*pe_b.step("y1T"))

            def back_yn1T(i):
                pe.wait_ge(*dve_b.of("yn1", i))
                to_features(yn1, ps_u).then_inc(*pe_b.step("yn1T"))

            def back_proj1(i):
                pe.wait_ge(*act_b.of("yn1Tc", i))
                for t in range(2):
                    o = ps_u[0:TP, P * t:P * t + P]
                    pe.matmul(o, yn1T[:, TP * t:TP * t + TP], w_proj[:, 1].rearrange("p u c -> p (u c)"), start=True, stop=False)
                    last = pe.matmul(o, ones[:, 0:TP], projb1[:].rearrange("a u c -> a (u c)"), start=False, stop=True)
                last.then_inc(*pe_b.step("proj1"))

            def back_h3T(i):
                pe.wait_ge(*dve_b.of("hn3", i))
                apart(pe, turns_pe)
                to_features64(hn3, ps_u).then_inc(*pe_b.step("h3T"))

            def back_route(i):
                pe.wait_ge(*act_b.of("h3Tc", i))
                apart(pe, turns_pe)
                pe.matmul(ps_u[0:1, 0:2 * T], wr[:], h3T[:], start=True, stop=True).then_inc(*pe_b.step("route"))

            def back_ffz(i, h):
                if h:
                    pe.wait_ge(*act_b.of("routec", i))
                pe.matmul((ps_v, ps_u)[h][:, 0:2 * T], fw1[:, h, :], h3T[:], start=True, stop=True)\
                  .then_inc(*pe_b.step(f"ffz{h}"))

            def back_ffo(i):
                pe.wait_ge(*act_b.of("gelu1", i))
                for u in range(2):
                    for h in range(2):
                        last = pe.matmul(ps_v[D * u:D * u + D, 0:T], fw2[:, h, :], gh[:, h, T * u:T * u + T],
                                         start=(h == 0), stop=(h == 1))
                last.then_inc(*pe_b.step("ffo"))

            def back_ffT(i):
                pe.wait_ge(*act_b.of("ffoc", i))
                for t in range(2):
                    last = pe.transpose(ps_u[0:TP, P * t:P * t + P], ffo[:, TP * t:TP * t + TP], ident[:])
                last.then_inc(*pe_b.step("ffT"))

            def back(i, n):
                if n == BACK_Y1T:
                    back_y1T(i)
                elif n == BACK_YN1T:
                    back_yn1T(i)
                elif n == BACK_PROJ1:
                    back_proj1(i)
                elif n == BACK_H3T:
                    back_h3T(i)
                elif n == BACK_ROUTE:
                    back_route(i)
                    back_ffz(i, 0)
                elif n == BACK_FFZ1:
                    back_ffz(i, 1)
                elif n == BACK_FFO:
                    back_ffo(i)
                elif n == BACK_FFT:
                    back_ffT(i)

            def body(i, prev, done, after):
                attention0(i, done)
                middle(i, prev)
                experts(i, after)
                rest(i, prev, after)
                for k in range(CHUNKS):
                    if k == 2:
                        values1(prev, 6)
                    if k == 6:
                        values1(prev, 7)
                    scores1(i, k)
                    if after is not None and k >= ROWS_AT:
                        rows0(after, 2 * (k - ROWS_AT))
                        rows0(after, 2 * (k - ROWS_AT) + 1)
                if after is not None:
                    pe.wait_ge(*act_a.of("zTc6", after))
                v1(i)

            for e in range(E):
                first(0, e)
            for f in range(8):
                rows0(0, f)
            body(0, None, None, 1)
            body(1, 0, None, 2)
            body(2, 1, 0, 3)
            with pe.Fori(3, PAIRS - 1) as i:
                body(i, i - 1, i - 2, i + 1)
            body(PAIRS - 1, PAIRS - 2, PAIRS - 3, None)
            for n in range(18):
                back(PAIRS - 2, n)
            for k in range(CHUNKS):
                values1(PAIRS - 1, k)
            for n in range(18):
                back(PAIRS - 1, n)
            pe.wait_ge(tail_dve, TAIL_SELECTED)
            for t in range(2):
                last = pe.transpose(ps_x[0:TP, B * t:B * t + B], tail_s[:, TP * t:TP * t + TP], ident[0:B, 0:B])
            last.then_inc(tail_pe, 1)

        @block.scalar
        def _(act):
            act.wait_ge(const_pe, 1)
            for n, w in enumerate((w_qkv0, w_qkv1)):
                for u in range(2):
                    half = slice(D * u, D * u + D)
                    kinds = 2 + n
                    act.copy(w[half, 0:kinds, u, :], ps_x[half, 192 * n:192 * n + D * kinds].rearrange("p (k c) -> p k c", k=kinds))
            for u in range(2):
                half = slice(D * u, D * u + D)
                for a in range(2):
                    for gq in range(2):
                        act.copy(w_qkv0[half, 2, u, :].rearrange("p (jp gh b a d) -> p a gh jp b d", gh=2, b=2, a=2, d=2)[:, a, gq],
                                 ps_x[half, 128:192].rearrange("p (jp a gh b d) -> p a gh jp b d", a=2, gh=2, b=2, d=2)[:, a, gq])
            for u in range(2):
                half = slice(D * u, D * u + D)
                last = act.copy(w_proj[half, :, u, :], ps_x[half, 384:512].rearrange("p (k c) -> p k c", k=2))
            last.then_inc(const_act, 1)
            act.wait_ge(const_pool, POOL_CONSTANTS)
            act.wait_ge(const_dve, DVE_CONSTANTS)
            act.wait_ge(loaded, n_loads)

            def v_copy(tiles, psum, u, step, j, d):
                for m, rows in enumerate((P, S1)):
                    src = psum[0:rows, P * m + D * u:P * m + D * u + D].rearrange("p (j g d) -> p j g d", j=j, g=4)
                    last = act.copy(v_view(tiles[m], u, step, rows, 0, d), src)
                return last

            def first_dense(i, n):
                if n == 0:
                    act.wait_ge(*pe_a.of("xT", i))
                    act.copy(x0, ps_x[:, 0:T_IN]).then_inc(*act_a.step("x0"))
                elif n == 1:
                    act.wait_ge(*pe_a.of("tok0", i))
                    act.activation(x1, ps_x[:, 0:T_IN], ACT.Tanh, bias=tok_b[:, 0:1]).then_inc(*act_a.step("x1"))
                elif n == 2:
                    act.wait_ge(*pe_a.of("tok1", i))
                    act.activation(x2[:], ps_x[:, 0:T_IN], ACT.Tanh, bias=tok_b[:, 1:2]).then_inc(*act_a.step("x2"))
                    act.wait_ge(*act_a.of("x2", i))
                    act.activation(x2s, x2[:], ACT.Square).then_inc(*act_a.step("x2s"))
                else:
                    act.wait_ge(*pe_a.of("tok2", i))
                    act.activation(x3, ps_x[:, 0:T_IN], ACT.Tanh, bias=tok_b[:, 2:3]).then_inc(*act_a.step("x3"))

            def first_x4(i):
                act.wait_ge(*pe_a.of("tok3", i))
                act.activation(x4[:].rearrange("p j c -> p (j c)"), ps_x[0:XT, 0:3 * P], ACT.Tanh).then_inc(*act_a.step("x4"))

            def first_h0(i):
                act.wait_ge(*pe_a.of("conv", i))
                before(act, dve_f, "h1", i)
                act.copy(h0[:].rearrange("p n c -> p (n c)"), ps_x[0:TP, 0:256]).then_inc(*act_a.step("h0"))

            def first_hn0T(i):
                act.wait_ge(*pe_a.of("hn0T", i))
                act.copy(hn0T[:], ps_u[:, 0:T]).then_inc(*act_a.step("hn0Tc"))

            def first_qk0(i):
                act.wait_ge(*pe_a.of("qk0", i))
                src = ps_u[0:TP, :].rearrange("p (t k c) -> p k t c", t=2, k=2)
                act.copy(qk0[:], src).then_inc(*act_a.step("qk0c"))
                act.activation(qk0s[:], src, ACT.Square).then_inc(*act_a.step("qk0s"))

            def first_v0(i):
                act.wait_ge(*pe_a.of("v0", i))
                for u in range(2):
                    last = v_copy(vp0, ps_u, u, 131, 8, HD0)
                last.then_inc(*act_a.step("v0c"))

            def first(i, e):
                if i is None:
                    return
                if e == FIRST_XT:
                    first_dense(i, 0)
                elif e in FIRST_DENSE:
                    first_dense(i, 1 + FIRST_DENSE.index(e))
                elif e == FIRST_TOK3:
                    first_x4(i)
                elif e == FIRST_CONV:
                    first_h0(i)
                elif e == FIRST_HN0T:
                    first_hn0T(i)
                elif e == FIRST_QK0:
                    first_qk0(i)
                elif e == FIRST_V0:
                    first_v0(i)

            def slots(z, a, b, s):
                return z[:, :, 0:12].rearrange("p h (s d) -> p h s d", d=2)[:, :, a:b:s, :]

            def wide(x, n):
                return x.rearrange("p (h d) -> p h d", d=2).unsqueeze(2).broadcast_to([TP, P, n, 2])

            def rows0(i, f):
                side, u, half = f // 4, f // 2 % 2, f % 2
                act.wait_ge(*pe_a.of(f"zT{f}", i))
                dst = (qT0, kT0)[side][:, u, 4 * half:4 * half + 4, :].rearrange("p j t -> p (j t)")
                act.copy(dst, (ps_x, ps_y)[f % 2][:].bitcast(BF16)[:, 0:4 * T]).then_inc(*act_a.step(f"zTc{f}"))

            def parts0(i, r):
                if i is None:
                    return
                if r == 0:
                    qn, kn = (qk0[:, s].rearrange("p t c -> p (t c)") for s in range(2))
                    act.wait_ge(*dve_a.of("negc", i))
                    before(act, pe_a, "zT7", i)
                    act.copy(slots(zq, 0, 3, 1), wide(qn, 3)).then_inc(*act_a.step("q1"))
                    act.copy(slots(zk, 2, 5, 1), wide(kn, 3)).then_inc(*act_a.step("k1"))
                    act.copy(zq[:, :, 12], negc[:]).then_inc(*act_a.step("c1"))
                elif r == 1:
                    act.wait_ge(*pool_a.of("rc1", i))
                    act.copy(slots(zq, 3, 6, 2), wide(res[:, 0, 0], 2)).then_inc(*act_a.step("q2"))
                    act.copy(slots(zk, 1, 6, 4), wide(res[:, 0, 1], 2)).then_inc(*act_a.step("k2"))
                    act.copy(zq[:, :, 13], resc[:, 0]).then_inc(*act_a.step("c2"))
                else:
                    act.wait_ge(*pool_a.of("rc2", i))
                    act.copy(slots(zq, 4, 5, 1), wide(res[:, 1, 0], 1)).then_inc(*act_a.step("q3"))
                    act.copy(slots(zk, 0, 1, 1), wide(res[:, 1, 1], 1)).then_inc(*act_a.step("k3"))
                    act.copy(zq[:, :, 14], resc[:, 1]).then_inc(*act_a.step("c3"))

            def attention0(i, prev, done):
                for n in range(18):
                    if n < 16:
                        act.wait_ge(*pe_f.of(f"sc{n}", i))
                        if n >= 2:
                            act.wait_ge(*pe_f.of(f"pv{n - 2}", i))
                        src = ps_s[n % 2][:, :, 0:2 * UNIT].rearrange("p b (a c) -> p b a c", a=2)
                        dst = e0[:, n % 2].rearrange("p (b a) c -> p b a c", b=2)
                        act.activation(dst[:, :, :, 0:T], src[:, :, :, 0:T], ACT.Exp)
                        act.activation(dst[0:S1, :, :, T:UNIT], src[0:S1, :, :, T:UNIT], ACT.Exp).then_inc(*act_f.step(f"ex{n}"))
                    if prev is not None and n + 2 < CHUNKS:
                        exps1(prev, n + 2)
                    if done is not None:
                        back(done, n)

            def middle(i, prev):
                act.wait_ge(*pe_f.of("pv15", i))
                act.copy(y0[:], ps_y[:, 0:2 * T]).then_inc(*act_f.step("y0c"))
                act.wait_ge(*pe_f.of("yn0T", i))
                act.copy(ynT[:], ps_x[:, 0:T]).then_inc(*act_f.step("yn0Tc"))
                values1(prev, 0)
                values1(prev, 1)
                act.wait_ge(*pe_f.of("hn1T", i))
                act.copy(hn1T[:], ps_x[0:D, 0:2 * T]).then_inc(*act_f.step("hn1Tc"))
                values1(prev, 2)
                act.wait_ge(*dve_f.of("gd", i))
                act.activation(gs[:, 1, :], gs[:, 0, :], ACT.Exp).then_inc(*act_f.step("gexp"))
                act.wait_ge(*pe_f.of("gT", i))
                act.copy(gT[:], ps_x[:].bitcast(BF16)[0:3 * E, 0:2 * T]).then_inc(*act_f.step("gTc"))

            def experts(i, after):
                for e in range(E):
                    act.wait_ge(*pe_f.of(f"z{e}", i))
                    if e >= 2:
                        act.wait_ge(*pool_f.of(f"hp{e - 2}", i))
                    act.activation(hr[:, e % 2, :], bank(e % 2)[:, 0:2 * T], ACT.Relu, bias=b1e[:, e:e + 1])\
                       .then_inc(*act_f.step(f"relu{e}"))
                    act.copy(hg[:, e % 2, :], bank(2 + e % 2)[:, 0:2 * T]).then_inc(*act_f.step(f"gc{e}"))
                    first(after, e)

            def rest(i, prev, after):
                act.wait_ge(*pe_f.of(f"o{E - 1}", i))
                act.copy(moe[:], ps_y[:, 0:2 * T]).then_inc(*act_f.step("moec"))
                values1(prev, 3)
                values1(prev, 4)
                act.wait_ge(*pe_f.of("hn2T", i))
                act.copy(hn2T[:], ps_x[:, 0:T]).then_inc(*act_f.step("hn2Tc"))
                parts0(after, 0)
                values1(prev, 5)
                for f in range(5):
                    act.wait_ge(*pe_f.of(f"kqT{f}", i))
                    dst = kT1[:, f // 2, 2 * (f % 2):2 * (f % 2) + 2, :] if f < 4 else qT1[:]
                    act.copy(dst.rearrange("p a t -> p (a t)"), bank(f % 4)[:, 0:2 * T]).then_inc(*act_f.step(f"kqTc{f}"))

            def scores1(i, k):
                before(act, dve_t, f"kept{k}", i)
                act.wait_ge(*pe_s.of(f"s{k}", i))
                act.copy(w_s[:, k, 0:2, :], ps_s[k % 2][:, :, 0:T]).then_inc(*act_s.step(f"sc{k}a"))
                for a in range(2):
                    half = slice(D * a, D * a + D)
                    last = act.copy(w_s[half, k, 2, :], ps_s[k % 2][half, a, T:2 * T])
                last.then_inc(*act_s.step(f"sc{k}b"))

            def exps1(i, k):
                act.wait_ge(*dve_s.of(f"m{k}n", i))
                before(act, pe_b, f"pt1_{k}", i)
                for t in range(3):
                    last = act.activation(e_s[:, k, t, :], w_s[:, k, t, :], ACT.Exp, bias=nmax[:, k, t:t + 1])
                last.then_inc(*act_s.step(f"e{k}"))

            def values1(i, k):
                if i is None:
                    return
                for m, rows in enumerate((P, S1)):
                    act.wait_ge(*pe_b.of(f"pt{m}_{k}", i))
                    act.copy(pt[m][:], ps_u[0:rows, 0:T + D + P]).then_inc(*act_b.step(f"pc{m}_{k}"))

            def v1(i):
                act.wait_ge(*pe_s.of("v1", i))
                before(act, pe_b, f"pv{CHUNKS - 1}", i)
                for u in range(2):
                    last = v_copy(vp1, ps_x, u, 137, 2, HD1)
                last.then_inc(*act_s.step("v1c"))

            def back_y1(i):
                act.wait_ge(*pe_b.of(f"pv{CHUNKS - 1}", i))
                act.copy(y1[:], ps_v[:, 0:2 * T]).then_inc(*act_b.step("y1c"))

            def back_yn1T(i):
                act.wait_ge(*pe_b.of("yn1T", i))
                act.copy(yn1T[:], ps_u[:, 0:T]).then_inc(*act_b.step("yn1Tc"))

            def back_h3T(i):
                act.wait_ge(*pe_b.of("h3T", i))
                act.copy(h3T[:], ps_u[0:D, 0:2 * T]).then_inc(*act_b.step("h3Tc"))

            def back_route(i):
                act.wait_ge(*pe_b.of("route", i))
                if not (isinstance(i, int) and i == 0):
                    act.wait_ge(routed, 16 * i)
                act.activation(rw[:], ps_u[0:1, 0:2 * T], ACT.Identity, bias=br[:, 0:1]).then_inc(*act_b.step("routec"))

            def back_gelu(i):
                for h in range(2):
                    act.wait_ge(*pe_b.of(f"ffz{h}", i))
                    act.activation(gh[:, h, :], (ps_v, ps_u)[h][:, 0:2 * T], ACT.Gelu_apprx_tanh, bias=fb1[:, h:h + 1])\
                       .then_inc(*act_b.step(f"gelu{h}"))

            def back_ffo(i):
                act.wait_ge(*pe_b.of("ffo", i))
                act.activation(ffo[:], ps_v[:, 0:T], ACT.Identity, bias=fb2[:, 0:1]).then_inc(*act_b.step("ffoc"))

            def back_ffT(i):
                act.wait_ge(*pe_b.of("ffT", i))
                if not (isinstance(i, int) and i == 0):
                    act.wait_ge(y_stored, 16 * i)
                act.copy(ffy[:].rearrange("p n c -> p (n c)"), ps_u[0:TP, 0:256]).then_inc(*act_b.step("ffTc"))

            def back(i, n):
                if n == BACK_Y1T:
                    back_y1(i)
                elif n == BACK_YN1T:
                    back_yn1T(i)
                elif n == BACK_H3T:
                    back_h3T(i)
                elif n == BACK_ROUTE:
                    back_route(i)
                elif n == BACK_FFZ1:
                    back_gelu(i)
                elif n == BACK_FFO:
                    back_ffo(i)
                elif n == BACK_FFT:
                    back_ffT(i)

            def body(i, prev, done, after):
                attention0(i, prev, done)
                middle(i, prev)
                experts(i, after)
                rest(i, prev, after)
                for k in range(CHUNKS):
                    if k == 2:
                        values1(prev, 6)
                    if k == 6:
                        values1(prev, 7)
                    scores1(i, k)
                    if k == EXP_AT:
                        exps1(i, 0)
                    if k in PARTS_AT:
                        parts0(after, 1 + PARTS_AT.index(k))
                    if after is not None and k >= ROWS_AT:
                        rows0(after, 2 * (k - ROWS_AT))
                        rows0(after, 2 * (k - ROWS_AT) + 1)
                exps1(i, 1)
                v1(i)

            for e in range(E):
                first(0, e)
            for r in range(3):
                parts0(0, r)
            for f in range(8):
                rows0(0, f)
            body(0, None, None, 1)
            body(1, 0, None, 2)
            body(2, 1, 0, 3)
            with act.Fori(3, PAIRS - 1) as i:
                body(i, i - 1, i - 2, i + 1)
            body(PAIRS - 1, PAIRS - 2, PAIRS - 3, None)
            for k in range(2, CHUNKS):
                exps1(PAIRS - 1, k)
            for n in range(18):
                back(PAIRS - 2, n)
            for k in range(CHUNKS):
                values1(PAIRS - 1, k)
            for n in range(18):
                back(PAIRS - 1, n)

        @block.gpsimd
        def _(pool):
            for w in (tok_w, w_qkv0, w_qkv1):
                pool.memset(w[:], 0.0)
            pool.memset(w_proj[:], 0.0).then_inc(zeroed, 1)
            pool.memset(ident[:], 0.0)
            pool.memset(ident_b[:], 0.0)
            pool.memset(pick[:], 0.0).then_inc(zeroed, 1)
            pool.wait_ge(zeroed, 2)
            pool.affine_select(ident[:], ident[:], [[-1, P]], ALU.not_equal, 1.0, base=0, channel_multiplier=1)
            pool.affine_select(ident_b[:], ident_b[:], [[-1, P]], ALU.not_equal, 1.0, base=0, channel_multiplier=1)\
                .then_inc(const_pool, 1)
            for s in range(3):
                pool.wait_ge(const_pool, 1 + s)
                pool.affine_select(pick[:], pick[:], [[-1, E], [0, P]], ALU.not_equal, 1.0,
                                   base=-E * s, channel_multiplier=1).then_inc(const_pool, 1)
            pool.iota(expert_id[:], [[0, 4], [1, E]], base=0, channel_multiplier=0,
                      allow_small_or_imprecise_dtypes=True).then_inc(const_pool, 1)
            for k in range(TAPS):
                if k >= 2:
                    pool.wait_ge(tap_done, k)
                pool.memset(tap_mask[:, k % 2], 0.0).then_inc(tap_made, 1)
                pool.wait_ge(tap_made, 2 * k + 1)
                pool.affine_select(tap_mask[:, k % 2], tap_mask[:, k % 2], [[XT, 3], [-2, T]], ALU.not_equal, 1.0,
                                   base=PAD - k, channel_multiplier=1).then_inc(tap_made, 1)
            pool.wait_ge(const_dve, DVE_CONSTANTS)

            def squares(i):
                pool.wait_ge(*act_a.of("qk0s", i))
                sq2 = qk0s[:].rearrange("p k t (h d) -> p (k t h) d", d=2)
                pool.tensor_tensor(rx[:], sq2[:, :, 0], sq2[:, :, 1], ALU.add).then_inc(*pool_a.step("ss"))
                pool.wait_ge(*pool_a.of("ss", i))
                apart(pool, turns_pool)
                pool.tensor_scalar(rx[:], rx[:], 1.0 / HD0, 1e-6, ALU.mult, ALU.add).then_inc(*pool_a.step("sx"))

            def roots0(i):
                y = rr[:]
                pool.wait_ge(*dve_a.of("b_guess", i))
                for r in range(3):
                    pool.tensor_tensor(rt[:], y, y, ALU.mult).then_inc(*pool_a.step(f"rn{r}a"))
                    pool.wait_ge(*pool_a.of(f"rn{r}a", i))
                    pool.tensor_tensor(rt[:], rt[:], rx[:], ALU.mult).then_inc(*pool_a.step(f"rn{r}b"))
                    pool.wait_ge(*pool_a.of(f"rn{r}b", i))
                    apart(pool, turns_pool)
                    pool.tensor_scalar(rt[:], rt[:], -0.5, 1.5, ALU.mult, ALU.add).then_inc(*pool_a.step(f"rn{r}c"))
                    pool.wait_ge(*pool_a.of(f"rn{r}c", i))
                    pool.tensor_tensor(y, y, rt[:], ALU.mult).then_inc(*pool_a.step(f"rn{r}d"))
                    if r < 2:
                        pool.wait_ge(*pool_a.of(f"rn{r}d", i))

            q4 = [qk0[:, s].rearrange("p t (h d) -> p (t h) d", d=2) for s in range(2)]
            r4 = [[res[:, r, s].rearrange("p (h d) -> p h d", d=2) for s in range(2)] for r in range(2)]
            slot = lambda z, n: z[:, :, 2 * n:2 * n + 2]

            def first_parts(i):
                pool.wait_ge(*act_a.of("c1", i))
                pool.tensor_tensor(r4[0][0], q4[0], slot(zq, 0), ALU.subtract).then_inc(*pool_a.step("rq1"))
                pool.tensor_tensor(r4[0][1], q4[1], slot(zk, 2), ALU.subtract).then_inc(*pool_a.step("rk1"))
                pool.tensor_tensor(resc[:, 0], negc[:], zq[:, :, 12], ALU.subtract).then_inc(*pool_a.step("rc1"))

            def second_parts(i):
                pool.wait_ge(*act_a.of("c2", i))
                pool.tensor_tensor(r4[1][0], r4[0][0], slot(zq, 3), ALU.subtract).then_inc(*pool_a.step("rq2"))
                pool.tensor_tensor(r4[1][1], r4[0][1], slot(zk, 1), ALU.subtract).then_inc(*pool_a.step("rk2"))
                pool.tensor_tensor(resc[:, 1], resc[:, 0], zq[:, :, 13], ALU.subtract).then_inc(*pool_a.step("rc2"))

            def experts(i, after):
                pool.wait_ge(*dve_f.of("c_cen", i))
                pool.tensor_tensor(h1[:], h1[:], ln_gb[:, 1, :].unsqueeze(1).broadcast_to([TP, 4, D]), ALU.add)\
                    .then_inc(*pool_f.step("h1b"))
                for e in range(E):
                    pool.wait_ge(*act_f.of(f"gc{e}", i))
                    if e >= 2:
                        pool.wait_ge(*pe_f.of(f"o{e - 2}", i))
                    pool.tensor_tensor(hp[:, e % 2, :], hr[:, e % 2, :], hg[:, e % 2, :], ALU.mult).then_inc(*pool_f.step(f"hp{e}"))
                    if e == FIRST_SQUARES and after is not None:
                        squares(after)

            def norm_heads(i):
                flat = lambda t: t.rearrange("p k n c -> p (k n c)")
                pool.wait_ge(*dve_f.of("g_cen", i))
                pool.tensor_tensor(flat(sq1), flat(c1), flat(c1), ALU.mult).then_inc(*pool_f.step("g_sq"))
                pool.wait_ge(*dve_f.of("g_gam", i))
                for n in range(2):
                    dst = zq1[:, :, n, :].rearrange("p (t u) c -> p t u c", t=2)
                    pool.tensor_tensor(dst, c1[:, 0].rearrange("p (t u) c -> p t u c", t=2),
                                       bet1[:, 0].rearrange("p (u c) -> p u c", u=2).unsqueeze(1).broadcast_to([TP, 2, 2, D]),
                                       ALU.add).then_inc(*pool_f.step(f"gq{n}"))

            def keep(i):
                if not (isinstance(i, int) and i == 0):
                    pool.wait_ge(*dve_b.of("h3", i - 1))
                pool.wait_ge(*dve_f.of("h2", i))
                apart(pool, turns_pool)
                pool.tensor_copy(h2k[:], h2[:]).then_inc(*pool_k.step("h2k"))

            def causal(i, units):
                for n in units:
                    pool.wait_ge(*act_f.of(f"ex{n}", i))
                    apart(pool, turns_pool)
                    pool.affine_select(e0[:, n % 2, :, 0:P], e0[:, n % 2, :, 0:P], [[0, 4], [1, P]], ALU.is_ge, 0.0,
                                       base=0, channel_multiplier=-1)
                    late = e0[0:S1, n % 2, :, T:UNIT]
                    pool.affine_select(late, late, [[0, 4], [1, S1]], ALU.is_ge, 0.0, base=0, channel_multiplier=-1)\
                        .then_inc(*pool_f.step(f"sel{n}"))

            def body(i, prev, after):
                causal(i, range(16))
                if prev is not None:
                    keep(prev)
                experts(i, after)
                if after is not None:
                    roots0(after)
                norm_heads(i)
                if after is not None:
                    first_parts(after)
                    second_parts(after)

            squares(0)
            roots0(0)
            first_parts(0)
            second_parts(0)
            body(0, None, 1)
            body(1, 0, 2)
            body(2, 1, 3)
            with pool.Fori(3, PAIRS - 1) as i:
                body(i, i - 1, i + 1)
            body(PAIRS - 1, PAIRS - 2, None)
            keep(PAIRS - 1)

        @block.vector
        def _(dve):
            chain = [0]

            def const(ins):
                chain[0] += 1
                ins.then_inc(const_dve, 1)

            const(dve.memset(ones[:], 1.0))
            for m in range(2):
                const(dve.memset(vp0[m][:], 0.0))
                const(dve.memset(vp1[m][:], 0.0))
            for z in (zq, zk, zk1):
                const(dve.memset(z[:], 0.0))
            const(dve.memset(toeplitz[:], 0.0))
            dve.wait_ge(const_dve, chain[0])
            for m in range(2):
                for u in range(2):
                    const(dve.memset(v_view(vp0[m], u, 131, P, HD0, HD0 + 1), 1.0))
                    const(dve.memset(v_view(vp1[m], u, 137, P, HD1, HD1 + 1), 1.0))
            const(dve.memset(zk[:, :, 12:15], 1.0))
            dve.wait_ge(loaded, n_loads)
            const(dve.tensor_scalar(core_abs[:], core[:], -1.0, None, ALU.mult))
            dve.wait_ge(const_dve, chain[0])
            const(dve.tensor_tensor(core_abs[:], core_abs[:], core[:], ALU.max))
            dve.wait_ge(const_dve, chain[0])
            const(dve.tensor_scalar(tok_w[:, 2, :], tok_w[:, 2, :], core_abs[:, 0:1], None, ALU.mult))
            for s in range(2):
                const(dve.tensor_scalar(rms_w[:, s, :].rearrange("p (h d) -> p h d", d=2),
                                        rms_raw[:, s, :].unsqueeze(1).broadcast_to([TP, D, 2]),
                                        HD0 ** -0.5 if s == 0 else 1.0, None, ALU.mult))
            dve.wait_ge(const_dve, chain[0])
            const(dve.tensor_tensor(wprod[:], rms_w[:, 0, 0:2], rms_w[:, 1, 0:2], ALU.mult))
            dve.wait_ge(const_dve, chain[0])
            const(dve.tensor_reduce(room[:], wprod[:], AX_X, ALU.max, apply_absolute_value=True))
            dve.wait_ge(const_dve, chain[0])
            const(dve.tensor_scalar(room[:], room[:], float(HD0), -SHIFT_ROOM, ALU.mult, ALU.add))
            for s in range(2):
                for dst, n in ((gam1, s), (bet1, 2 + s)):
                    const(dve.tensor_scalar(dst[:, s, :].rearrange("p (h d) -> p h d", d=HD1),
                                            gb_raw[:, n, :].unsqueeze(1).broadcast_to([TP, 16, HD1]),
                                            HD1 ** -0.5 if s == 0 else 1.0, None, ALU.mult))
            const(dve.tensor_copy(b2e[:, 0, :], b2raw[:]))
            dve.wait_ge(const_dve, chain[0])
            const(dve.tensor_tensor(b2res[:, 0, :], b2raw[:], b2e[:, 0, :], ALU.subtract))
            dve.wait_ge(const_dve, chain[0])
            const(dve.tensor_copy(b2e[:, 1, :], b2res[:, 0, :]))
            dve.wait_ge(const_dve, chain[0])
            const(dve.tensor_tensor(b2res[:, 1, :], b2res[:, 0, :], b2e[:, 1, :], ALU.subtract))
            dve.wait_ge(const_dve, chain[0])
            const(dve.tensor_copy(b2e[:, 2, :], b2res[:, 1, :]))
            for k in range(TAPS):
                dve.wait_ge(tap_made, 2 * k + 2)
                if k:
                    dve.wait_ge(tap_done, k)
                dve.scalar_tensor_tensor(toeplitz[:], tap_mask[:, k % 2], taps[:, k:k + 1], toeplitz[:], ALU.mult, ALU.add)\
                   .then_inc(tap_done, 1)
            dve.wait_ge(tap_done, TAPS)
            const(dve.memset(gs[:, 4, :], 0.0))
            assert chain[0] == DVE_CONSTANTS, chain[0]
            dve.wait_ge(const_pool, POOL_CONSTANTS)

            def rsqrt(x, y, t, tag, i, steps):
                dve.tensor_scalar(y.bitcast(I32), x.bitcast(I32), -0.5, RSQRT_MAGIC, ALU.mult, ALU.add)\
                   .then_inc(*steps.step(f"{tag}_guess"))
                dve.wait_ge(*steps.of(f"{tag}_guess", i))
                for r in range(3):
                    dve.scalar_tensor_tensor(t, y, -0.5, y, ALU.mult, ALU.mult).then_inc(*steps.step(f"{tag}_n{r}a"))
                    dve.wait_ge(*steps.of(f"{tag}_n{r}a", i))
                    dve.tensor_tensor(t, t, x, ALU.mult).then_inc(*steps.step(f"{tag}_n{r}b"))
                    dve.wait_ge(*steps.of(f"{tag}_n{r}b", i))
                    dve.scalar_tensor_tensor(y, t, 1.5, y, ALU.add, ALU.mult).then_inc(*steps.step(f"{tag}_n{r}c"))
                    dve.wait_ge(*steps.of(f"{tag}_n{r}c", i))

            def centre(src, tag, i, steps):
                dve.tensor_reduce(lnt[:, 0, :], src[:], AX_X, ALU.add).then_inc(*steps.step(f"{tag}_sum"))
                dve.wait_ge(*steps.of(f"{tag}_sum", i))
                dve.scalar_tensor_tensor(cen[:], over(lnt[:, 0, :]), -1.0 / D, src[:], ALU.mult, ALU.add)\
                   .then_inc(*steps.step(f"{tag}_cen"))
                dve.wait_ge(*steps.of(f"{tag}_cen", i))
                dve.tensor_tensor(sq[:], cen[:], cen[:], ALU.mult).then_inc(*steps.step(f"{tag}_sq"))
                dve.wait_ge(*steps.of(f"{tag}_sq", i))
                dve.tensor_reduce(lnt[:, 2, :], sq[:], AX_X, ALU.add).then_inc(*steps.step(f"{tag}_ssq"))
                dve.wait_ge(*steps.of(f"{tag}_ssq", i))
                dve.tensor_scalar(lnt[:, 3, :], lnt[:, 2, :], 1.0 / D, 1e-5, ALU.mult, ALU.add).then_inc(*steps.step(f"{tag}_var"))
                dve.wait_ge(*steps.of(f"{tag}_var", i))
                rsqrt(lnt[:, 3, :], lnt[:, 4, :], lnt[:, 5, :], tag, i, steps)

            def over(x, n=D):
                return x.unsqueeze(2).broadcast_to([TP, x.shape[1], n])

            def norm_tok(i):
                dve.wait_ge(*act_a.of("h0", i))
                centre(h0, "a", i, dve_a)
                dve.tensor_tensor(hn0[:], cen[:], over(lnt[:, 4, :]), ALU.mult).then_inc(*dve_a.step("hn0"))

            def roots0(i):
                dve.wait_ge(*pool_a.of("sx", i))
                dve.tensor_scalar(rr[:].bitcast(I32), rx[:].bitcast(I32), -0.5, RSQRT_MAGIC, ALU.mult, ALU.add)\
                   .then_inc(*dve_a.step("b_guess"))

            def scaled0(i):
                dve.wait_ge(*pool_a.of("rn2d", i))
                y = rr[:]
                q2 = qk0[:].rearrange("p k t (h d) -> p (k t h) d", d=2)
                dve.tensor_tensor(q2, q2, y.unsqueeze(2).broadcast_to([TP, 256, 2]), ALU.mult).then_inc(*dve_a.step("qr"))
                dve.wait_ge(*dve_a.of("qr", i))
                dve.tensor_tensor(qk0[:], qk0[:], rms_w[:].unsqueeze(2).broadcast_to([TP, 2, 2, P]), ALU.mult)\
                    .then_inc(*dve_a.step("qw"))
                dve.wait_ge(*dve_a.of("qw", i))
                qn, kn = (qk0[:, s].rearrange("p t c -> p (t c)") for s in range(2))
                dve.tensor_tensor(selfp[:], qn, kn, ALU.mult).then_inc(*dve_a.step("qkp"))
                dve.wait_ge(*dve_a.of("qkp", i))
                sp2 = selfp[:].rearrange("p (h d) -> p h d", d=2)
                dve.tensor_tensor(selfs[:], sp2[:, :, 0], sp2[:, :, 1], ALU.add).then_inc(*dve_a.step("self"))
                dve.wait_ge(*dve_a.of("self", i))
                dve.tensor_scalar(negc[:], selfs[:], room[:, 0:1], -1.0, ALU.max, ALU.mult).then_inc(*dve_a.step("negc"))

            def heads_out(psum, r, y, nj, d, steps, names, i):
                v = psum[0:TP, :].rearrange("p (n y) -> p n y", y=32)
                dve.reciprocal(r[:, :, 0:nj], v[:, :, d:d + (d + 1) * (nj - 1) + 1:d + 1]).then_inc(*steps.step(names[0]))
                dve.wait_ge(*steps.of(names[0], i))
                dve.tensor_tensor(y[:].rearrange("p n (g j d) -> p (n g) j d", g=4, d=d),
                                  v[:, :, 0:nj * (d + 1)].rearrange("p n (j d) -> p n j d", d=d + 1)[:, :, :, 0:d],
                                  r[:, :, 0:nj].unsqueeze(3).broadcast_to([TP, 16, nj, d]), ALU.mult)\
                   .then_inc(*steps.step(names[1]))

            def attended(i, prev):
                dve.wait_ge(*pe_f.of("y0T", i))
                heads_out(ps_x, rec, yn, 8, HD0, dve_f, ("rec0", "yn0"), i)
                topk(prev, 4, 0, 1)
                dve.wait_ge(*pe_f.of("proj0", i))
                dve.tensor_tensor(h1[:].rearrange("p n c -> p (n c)"), ps_x[0:TP, 0:256], h0[:].rearrange("p n c -> p (n c)"),
                                  ALU.add).then_inc(*dve_f.step("h1"))
                dve.wait_ge(*dve_f.of("h1", i))
                centre(h1, "c", i, dve_f)
                dve.tensor_tensor(hn1[:], cen[:], over(lnt[:, 4, :]), ALU.mult).then_inc(*dve_f.step("hn1"))

            def gates(i):
                dve.wait_ge(*pe_f.of("gate", i))
                dve.tensor_tensor(lg[:], ps_x[0:TP, 0:4 * E].rearrange("p (n e) -> p n e", e=E),
                                  gate_b[:].unsqueeze(1).broadcast_to([TP, 4, E]), ALU.add).then_inc(*dve_f.step("lg"))
                dve.wait_ge(*dve_f.of("lg", i))
                for n in range(4):
                    apart(dve, turns_dve)
                    dve.max(gm[:, n, :], lg[:, n, :]).then_inc(*dve_f.step(f"gm{n}"))
                for n in range(4):
                    dve.wait_ge(*dve_f.of(f"gm{n}", i))
                    apart(dve, turns_dve)
                    dve.max_index(gi[:, n, :], gm[:, n, :], lg[:, n, :]).then_inc(*dve_f.step(f"gi{n}"))
                dve.wait_ge(*dve_f.of("gi3", i))
                dve.tensor_copy(gif[:], gi[:, :, 0:TOPK_E]).then_inc(*dve_f.step("gif"))
                dve.tensor_tensor(gs[:, 0, :], gm[:, :, 1], gm[:, :, 0], ALU.subtract).then_inc(*dve_f.step("gd"))
                dve.wait_ge(*act_f.of("gexp", i))
                dve.tensor_scalar(gs[:, 2, :], gs[:, 1, :], 1.0, None, ALU.add).then_inc(*dve_f.step("g1p"))
                dve.wait_ge(*dve_f.of("g1p", i))
                dve.reciprocal(gs[:, 3, :], gs[:, 2, :]).then_inc(*dve_f.step("p1"))
                dve.wait_ge(*dve_f.of("p1", i))
                dve.tensor_tensor(gs[:, 4, :], gs[:, 1, :], gs[:, 3, :], ALU.mult).then_inc(*dve_f.step("p2"))
                for n in range(2):
                    dve.tensor_tensor(ge[:, n], expert_id[:], over(gif[:, :, n], E), ALU.is_equal).then_inc(*dve_f.step(f"e{n + 1}"))
                for n in range(2):
                    dve.wait_ge(*dve_f.of(f"e{n + 1}", i))
                    dve.tensor_tensor(ge[:, 2 + n], ge[:, n], over(gs[:, 3 + n, :], E), ALU.mult).then_inc(*dve_f.step(f"e{n + 1}p"))
                dve.wait_ge(*dve_f.of("e2p", i))
                dve.tensor_tensor(gg[:, 0], ge[:, 2], ge[:, 3], ALU.add).then_inc(*dve_f.step("G"))
                dve.wait_ge(*dve_f.of("G", i))
                dve.tensor_copy(g3[:, :, 0, :], gg[:, 0]).then_inc(*dve_f.step("G1"))
                dve.wait_ge(*dve_f.of("G1", i))
                dve.tensor_tensor(gg[:, 1], gg[:, 0], g3[:, :, 0, :], ALU.subtract).then_inc(*dve_f.step("Gr"))
                dve.wait_ge(*dve_f.of("Gr", i))
                dve.tensor_copy(g3[:, :, 1, :], gg[:, 1]).then_inc(*dve_f.step("G2"))
                dve.wait_ge(*dve_f.of("G2", i))
                dve.tensor_tensor(gg[:, 2], gg[:, 1], g3[:, :, 1, :], ALU.subtract).then_inc(*dve_f.step("Gr2"))
                dve.wait_ge(*dve_f.of("Gr2", i))
                dve.tensor_copy(g3[:, :, 2, :], gg[:, 2]).then_inc(*dve_f.step("G3"))

            def mixed(i):
                dve.wait_ge(*pe_f.of("moeT", i))
                v = ps_x[0:TP, :].rearrange("p (n a c) -> p n a c", n=4, a=2)
                dve.tensor_tensor(my[:], hn1[:], v[:, :, 0, :], ALU.add).then_inc(*dve_f.step("ma"))
                dve.wait_ge(*dve_f.of("ma", i))
                dve.tensor_tensor(my[:], my[:], v[:, :, 1, :], ALU.add).then_inc(*dve_f.step("mb"))
                dve.wait_ge(*dve_f.of("mb", i))
                centre(my[:], "d", i, dve_f)
                dve.tensor_tensor(mn[:], cen[:], over(lnt[:, 4, :]), ALU.mult).then_inc(*dve_f.step("dn"))
                dve.wait_ge(*dve_f.of("dn", i))
                gamma = ln_gb[:, 0, :].unsqueeze(1).broadcast_to([TP, 4, D])
                dve.tensor_tensor(mn[:], mn[:], gamma, ALU.mult).then_inc(*dve_f.step("dg"))
                dve.wait_ge(*dve_f.of("dg", i))
                dve.wait_ge(*pool_f.of("h1b", i))
                before(dve, pool_k, "h2k", i)
                dve.tensor_tensor(h2[:], mn[:], h1[:], ALU.add).then_inc(*dve_f.step("h2"))
                dve.wait_ge(*dve_f.of("h2", i))
                centre(h2, "f", i, dve_f)
                dve.tensor_tensor(hn2[:], cen[:], over(lnt[:, 4, :]), ALU.mult).then_inc(*dve_f.step("hn2"))

            def norm_heads(i, prev):
                dve.wait_ge(*pe_f.of("qk1", i))
                for t in range(2):
                    dve.tensor_tensor(qk1[:, :, 2 * t:2 * t + 2, :],
                                      ps_x[0:TP, 256 * t:256 * t + 256].rearrange("p (k u c) -> p k u c", k=2, u=2),
                                      bqk1[:].unsqueeze(2).broadcast_to([TP, 2, 2, D]), ALU.add).then_inc(*dve_f.step(("qk1a", "qk1b")[t]))
                dve.wait_ge(*dve_f.of("qk1b", i))
                groups = lambda t: t.rearrange("p k n (h d) -> p (k n h) d", d=HD1)
                dve.tensor_reduce(n1[:, 0, :], groups(qk1[:]), AX_X, ALU.add).then_inc(*dve_f.step("g_sum"))
                dve.wait_ge(*dve_f.of("g_sum", i))
                dve.scalar_tensor_tensor(groups(c1), over(n1[:, 0, :], HD1), -1.0 / HD1, groups(qk1[:]), ALU.mult, ALU.add)\
                   .then_inc(*dve_f.step("g_cen"))
                topk(prev, 6, 2, 3)
                dve.wait_ge(*pool_f.of("g_sq", i))
                dve.tensor_reduce(n1[:, 2, :], groups(sq1), AX_X, ALU.add).then_inc(*dve_f.step("g_ssq"))
                dve.wait_ge(*dve_f.of("g_ssq", i))
                dve.tensor_scalar(n1[:, 3, :], n1[:, 2, :], 1.0 / HD1, 1e-5, ALU.mult, ALU.add).then_inc(*dve_f.step("g_var"))
                dve.wait_ge(*dve_f.of("g_var", i))
                rsqrt(n1[:, 3, :], n1[:, 4, :], n1[:, 5, :], "g", i, dve_f)
                dve.tensor_tensor(groups(c1), groups(c1), over(n1[:, 4, :], HD1), ALU.mult).then_inc(*dve_f.step("g_norm"))
                dve.wait_ge(*dve_f.of("g_norm", i))
                c4 = c1.rearrange("p k (t u) c -> p k t (u c)", t=2)
                dve.tensor_tensor(c4, c4, gam1[:].unsqueeze(2).broadcast_to([TP, 2, 2, P]), ALU.mult).then_inc(*dve_f.step("g_gam"))
                dve.wait_ge(*dve_f.of("g_gam", i))
                for t in range(2):
                    dst = zk1[:, 2 * t:2 * t + 2, :].rearrange("p u (h x) -> p u h x", x=72)[:, :, :, 0:HD1]
                    dve.tensor_tensor(dst, c1[:, 1, 2 * t:2 * t + 2].rearrange("p u (h d) -> p u h d", d=HD1),
                                      bet1[:, 1].rearrange("p (u h d) -> p u h d", u=2, d=HD1), ALU.add)\
                       .then_inc(*dve_f.step(f"gk{t}"))

            def first_max(i, k):
                dve.wait_ge(*act_s.of(f"sc{k}b", i))
                for t in range(3):
                    apart(dve, turns_dve)
                    dve.max(m8[:, k, t, :], w_s[:, k, t, :]).then_inc(*dve_s.step(f"m{k}t{t}"))
                dve.wait_ge(*dve_s.of(f"m{k}t2", i))
                dve.tensor_scalar(nmax[:, k, :], m8[:, k, :, 0], -1.0, None, ALU.mult).then_inc(*dve_s.step(f"m{k}n"))

            def topk(i, k, first=0, last=ROUNDS):
                if i is None:
                    return
                if first == 0:
                    dve.wait_ge(*act_s.of(f"e{k}", i))
                for r in range(first, last):
                    if r:
                        for t in range(3):
                            dve.wait_ge(*dve_t.of(f"k{k}r{r - 1}r{t}", i))
                            apart(dve, turns_dve)
                            dve.max(m8[:, k, t, :], w_s[:, k, t, :]).then_inc(*dve_t.step(f"k{k}r{r}m{t}"))
                    for t in range(3):
                        if r:
                            dve.wait_ge(*dve_t.of(f"k{k}r{r}m{t}", i))
                        apart(dve, turns_dve)
                        dve.match_replace(w_s[:, k, t, :], m8[:, k, t, :], w_s[:, k, t, :], NEG)\
                           .then_inc(*dve_t.step(f"k{k}r{r}r{t}"))
                if last < ROUNDS:
                    return
                dve.wait_ge(*dve_t.of(f"k{k}r{ROUNDS - 1}r2", i))
                dve.scalar_tensor_tensor(e_s[:, k], w_s[:, k], NEG_TEST, e_s[:, k], ALU.is_lt, ALU.mult)\
                   .then_inc(*dve_t.step(f"kept{k}"))

            def back_attended(i):
                dve.wait_ge(*pe_b.of("y1T", i))
                heads_out(ps_u, rec1, yn1, 2, HD1, dve_b, ("rec1", "yn1"), i)

            def back_norm(i):
                dve.wait_ge(*pe_b.of("proj1", i))
                dve.wait_ge(*pool_k.of("h2k", i))
                dve.tensor_tensor(h3[:].rearrange("p n c -> p (n c)"), ps_u[0:TP, 0:256], h2k[:].rearrange("p n c -> p (n c)"),
                                  ALU.add).then_inc(*dve_b.step("h3"))
                dve.wait_ge(*dve_b.of("h3", i))
                centre(h3, "r", i, dve_b)
                dve.tensor_tensor(hn3[:], cen[:], over(lnt[:, 4, :]), ALU.mult).then_inc(*dve_b.step("hn3"))
                dve.wait_ge(*dve_b.of("hn3", i))
                if not (isinstance(i, int) and i == 0):
                    dve.wait_ge(h_stored, 16 * i)
                dve.tensor_tensor(hsum[:], h3[:], hn3[:], ALU.add).then_inc(*dve_b.step("hsum"))

            def body(i, prev, done, after):
                topk(prev, 1, 0, 4)
                if done is not None:
                    back_attended(done)
                topk(prev, 1, 4)
                topk(prev, 2, 0, 4)
                if done is not None:
                    back_norm(done)
                topk(prev, 2, 4)
                topk(prev, 3)
                attended(i, prev)
                topk(prev, 4, 1, 3)
                gates(i)
                topk(prev, 4, 3)
                topk(prev, 5, 0, 3)
                if after is not None:
                    norm_tok(after)
                topk(prev, 5, 3)
                topk(prev, 6, 0, 2)
                if after is not None:
                    roots0(after)
                mixed(i)
                if after is not None:
                    scaled0(after)
                norm_heads(i, prev)
                topk(prev, 6, 3)
                first_max(i, 0)
                first_max(i, 1)
                topk(prev, 7)
                for k in range(2, 6):
                    first_max(i, k)
                topk(i, 0, 0, 3)
                first_max(i, 6)
                topk(i, 0, 3, 5)
                first_max(i, 7)
                topk(i, 0, 5)

            norm_tok(0)
            roots0(0)
            scaled0(0)
            body(0, None, None, 1)
            body(1, 0, None, 2)
            body(2, 1, 0, 3)
            with dve.Fori(3, PAIRS - 1) as i:
                body(i, i - 1, i - 2, i + 1)
            body(PAIRS - 1, PAIRS - 2, PAIRS - 3, None)
            back_attended(PAIRS - 2)
            back_norm(PAIRS - 2)
            for k in range(1, CHUNKS):
                topk(PAIRS - 1, k)
            back_attended(PAIRS - 1)
            back_norm(PAIRS - 1)

            count = [0]

            def tail(ins):
                count[0] += 1
                ins.then_inc(tail_dve, 1)
                dve.wait_ge(tail_dve, count[0])

            dve.wait_ge(sel_loaded, 16)
            tail(dve.tensor_copy(tail_x, tail_w))
            for _ in range(CAP // 8):
                tail(dve.max(tail_8, tail_x))
                tail(dve.match_replace(tail_x, tail_8, tail_x, NEG))
            tail(dve.max(tail_8, tail_x))
            edge = tail_8[:, CAP % 8 - 1:CAP % 8]
            tail(dve.tensor_scalar(tail_gt, tail_x, edge, None, ALU.is_gt))
            tail(dve.tensor_scalar(tail_eq, tail_x, edge, None, ALU.is_equal))
            tail(dve.tensor_reduce(tail_n[:, 0:1], tail_gt, AX_X, ALU.add))
            tail(dve.tensor_scalar(tail_n[:, 1:2], tail_n[:, 0:1], -1.0, float(CAP % 8), ALU.mult, ALU.add))
            tail(dve.tensor_copy(tail_c[:, 0, :], tail_eq))
            shift, a = 1, 0
            while shift < T:
                tail(dve.tensor_copy(tail_c[:, 1 - a, 0:shift], tail_c[:, a, 0:shift]))
                tail(dve.tensor_tensor(tail_c[:, 1 - a, shift:T], tail_c[:, a, shift:T], tail_c[:, a, 0:T - shift], ALU.add))
                shift, a = 2 * shift, 1 - a
            tail(dve.scalar_tensor_tensor(tail_eq, tail_c[:, a, :], tail_n[:, 1:2], tail_eq, ALU.is_le, ALU.mult))
            tail(dve.tensor_tensor(tail_gt, tail_gt, tail_eq, ALU.add))
            tail(dve.scalar_tensor_tensor(tail_gt, tail_x, NEG_TEST, tail_gt, ALU.is_lt, ALU.add))
            tail(dve.tensor_tensor(tail_s, tail_gt, tail_w, ALU.mult))
            assert count[0] == TAIL_SELECTED, count[0]
            dve.wait_ge(tail_pe, 1)
            tail(dve.tensor_copy(wt.rearrange("p t b -> p (t b)"), ps_x[0:TP, 0:2 * B]))
            assert count[0] == TAIL_FIRST
            for n in range(PIECES):
                dve.wait_ge(piece_loaded[n % 2], 32 * (n // 2) + 32)
                for m in range(4):
                    w = wt[:, m // 2, :].rearrange("p (i u) -> p i u", u=2)[:, TAIL * n:TAIL * n + TAIL, m % 2]
                    y = fin_y[n % 2][:, :, m, :]
                    tail(dve.tensor_tensor(y, y, over(w), ALU.mult))
                    tail(dve.tensor_tensor(y, y, fin_h[n % 2][:, :, m, :], ALU.add))


POOL_CONSTANTS = 5
DVE_CONSTANTS = 36
TAIL_SELECTED = 1 + 2 * (CAP // 8) + 1 + 5 + 2 * 8 + 4
TAIL_FIRST = TAIL_SELECTED + 1

NAMES = ["x", "L0_tok_W_in", "L0_tok_b_in", "L0_tok_W_out", "L0_tok_b_out", "L0_tok_core_diag", "L0_tok_conv_filter",
         "L0_attn_w_qkv", "L0_attn_w_proj", "L0_attn_qn_w", "L0_attn_kn_w", "L0_ffn_gate_w", "L0_ffn_gate_b", "L0_ffn_w1",
         "L0_ffn_b1", "L0_ffn_w2", "L0_ffn_b2", "L0_ffn_gamma", "L0_ffn_beta", "L1_attn_qkv_w", "L1_attn_qkv_b",
         "L1_attn_q_gamma", "L1_attn_q_beta", "L1_attn_k_gamma", "L1_attn_k_beta", "L1_attn_proj_w", "L1_attn_proj_b",
         "L1_ffn_wr", "L1_ffn_br", "L1_ffn_w1", "L1_ffn_b1", "L1_ffn_w2", "L1_ffn_b2"]


def kernel(**inputs):
    import numpy as np
    import concourse.bacc as bacc
    from concourse.bass_utils import run_bass_kernel_spmd

    nc = bacc.Bacc("TRN2", target_bir_lowering=False, num_devices=1)
    arrays, dram = {}, {}
    for name in NAMES:
        a = np.ascontiguousarray(inputs[name])
        arrays["in_" + name] = a
        dram[name] = nc.dram_tensor("in_" + name, a.shape, mybir.dt.from_np(a.dtype), kind="ExternalInput").ap()
    out = nc.dram_tensor("out", (2 * PAIRS, T, D), F32, kind="ExternalOutput").ap()
    route = nc.dram_tensor("route", (PAIRS, 2 * T), F32, kind="Internal").ap()
    h3, ffy = (nc.dram_tensor(n, (PAIRS, TP, 4 * D), F32, kind="Internal").ap() for n in ("h3_rows", "ff_rows"))
    audio_tower(nc, dram, out, route, h3, ffy)
    return run_bass_kernel_spmd(nc, [arrays], core_ids=[0]).results[0]["out"]
```
